# Optimizing a Trainium2 kernel written in Bass

```python
import numpy as np
import jax
import jax.numpy as jnp

def _softmax(x, axis=-1):
    return jax.nn.softmax(x, axis=axis)

def _gelu(x):
    return jax.nn.gelu(x, approximate=True)

def _silu(x):
    return jax.nn.silu(x)

def _sigmoid(x):
    return jax.nn.sigmoid(x)

def _layernorm(x, axis=-1, eps=1e-05):
    m = jnp.mean(x, axis=axis, keepdims=True)
    v = jnp.var(x, axis=axis, keepdims=True)
    return (x - m) / jnp.sqrt(v + eps)

def _scatter_add(tgt, idx, src, axis=0):
    return tgt.at[idx].add(src)

def _segment_sum(src, seg, n):
    return jax.ops.segment_sum(src, seg, n)
kernel_name = 'mk_vit_tower_d2_tok_img768_r4_9b0f2a'

def setup_inputs(seed: int=0):
    np.random.seed(seed)
    _w = jnp.asarray

    def _rec_inputs():
        import jax
        import jax.numpy as jnp
        _rk = jax.random.key(seed)
        x = -0.00016672 + 0.999947 * jax.random.normal(jax.random.fold_in(_rk, 1), (32, 112, 112, 3), jnp.float32)
        return x
    x = _rec_inputs()

    def _L0_tok_setup():
        import jax, jax.numpy as jnp
        import numpy as np
        PATCH = 16
        key = jax.random.key(seed)
        k1, k2 = jax.random.split(key)
        B, H, Wd, C = (64, 96, 96, 3)
        patch_vec = PATCH * PATCH * C
        proj_dim = 192
        images = jax.random.normal(k1, (B, H, Wd, C), dtype=jnp.float32)
        W = jax.random.normal(k2, (patch_vec, proj_dim), dtype=jnp.float32) * (1.0 / np.sqrt(patch_vec))
        b = jnp.zeros((proj_dim,), dtype=jnp.float32)
        return {'images': images, 'W': W, 'b': b}
    _L0_tok_all = _L0_tok_setup()
    _L0_tok_in = {k: v for k, v in _L0_tok_all.items() if k in ('W', 'b')}
    del _L0_tok_all

    def _L0_attn_setup():
        import jax, jax.numpy as jnp
        import numpy as np
        EMBED_DIM = 192
        MAX_LEN = 256
        ALPHA = 0.99
        BATCH = 16

        def _retention_mask(sl, alpha, dtype):
            i = jnp.arange(sl)[:, None]
            j = jnp.arange(sl)[None, :]
            causal = i >= j
            exponent = jnp.where(causal, (i - j).astype(dtype), 0.0)
            decay = jnp.asarray(alpha, dtype) ** exponent
            return jnp.where(causal, decay, jnp.zeros((), dtype))
        key = jax.random.key(seed)
        k1, k2, k3 = jax.random.split(key, 3)
        x = jax.random.normal(k1, (BATCH, MAX_LEN, EMBED_DIM), dtype=jnp.float32)
        scale = 1.0 / np.sqrt(EMBED_DIM)
        W_qkv = jax.random.uniform(k2, (EMBED_DIM, 3 * EMBED_DIM), dtype=jnp.float32, minval=-scale, maxval=scale)
        b_qkv = jax.random.uniform(k3, (3 * EMBED_DIM,), dtype=jnp.float32, minval=-scale, maxval=scale)
        return {'x': x, 'W_qkv': W_qkv, 'b_qkv': b_qkv}
    _L0_attn_all = _L0_attn_setup()
    _L0_attn_in = {k: v for k, v in _L0_attn_all.items() if k in ('W_qkv', 'b_qkv')}
    del _L0_attn_all

    def _L0_ffn_setup():
        import jax, jax.numpy as jnp
        import numpy as np
        DIM = 192
        H = 12
        HD = 64
        SHARED = 2
        ROUTED = 2
        E_ROUTED = H - SHARED
        LN_EPS = 1e-05

        def _layernorm(x, w, b):
            m = x.mean(-1, keepdims=True)
            v = ((x - m) ** 2).mean(-1, keepdims=True)
            return (x - m) * jax.lax.rsqrt(v + LN_EPS) * w + b
        key = jax.random.key(seed)
        ks = jax.random.split(key, 12)
        B, N = (4, 512)
        s = 0.02
        return {'x': jax.random.normal(ks[0], (B, N, DIM), jnp.float32), 'qkv_w': jax.random.normal(ks[1], (DIM, 3 * H * HD), jnp.float32) * s, 'qkv_b': jnp.zeros((3 * H * HD,), jnp.float32), 'q_norm_w': jnp.ones((HD,), jnp.float32), 'q_norm_b': jnp.zeros((HD,), jnp.float32), 'k_norm_w': jnp.ones((HD,), jnp.float32), 'k_norm_b': jnp.zeros((HD,), jnp.float32), 'wg_w': jax.random.normal(ks[2], (DIM, E_ROUTED), jnp.float32) * s, 'wg0_w': jax.random.normal(ks[3], (DIM, 2), jnp.float32) * s, 'wg1_w': jax.random.normal(ks[4], (DIM, SHARED), jnp.float32) * s, 'proj_w': jax.random.normal(ks[5], (H * HD, DIM), jnp.float32) * s, 'proj_b': jnp.zeros((DIM,), jnp.float32)}
    _L0_ffn_all = _L0_ffn_setup()
    _L0_ffn_in = {k: v for k, v in _L0_ffn_all.items() if k in ('qkv_w', 'qkv_b', 'q_norm_w', 'q_norm_b', 'k_norm_w', 'k_norm_b', 'wg_w', 'wg0_w', 'wg1_w', 'proj_w', 'proj_b')}
    del _L0_ffn_all

    def _L1_attn_setup():
        import jax, jax.numpy as jnp
        import numpy as np
        B, N, DIM, H = (8, 256, 192, 12)
        DH = DIM // H
        LATENT = 32
        EPS = 1e-05

        def _heads(t):
            b, n, _ = t.shape
            return t.reshape(b, n, H, DH).transpose(0, 2, 1, 3).reshape(b * H, n, DH)

        def _merge(t, b):
            _, n, dh = t.shape
            return t.reshape(b, H, n, dh).transpose(0, 2, 1, 3).reshape(b, n, H * dh)

        def _ln(v, g, bta):
            mu = v.mean(-1, keepdims=True)
            var = ((v - mu) ** 2).mean(-1, keepdims=True)
            return (v - mu) * jax.lax.rsqrt(var + EPS) * g + bta

        def _rope(t):
            n, dh = (t.shape[-2], t.shape[-1])
            inv = 1.0 / 10000.0 ** (jnp.arange(0, dh, 2, dtype=jnp.float32) / dh)
            f = jnp.arange(n, dtype=jnp.float32)[:, None] * inv[None, :]
            f = jnp.concatenate([f, f], -1)[None]
            x1, x2 = jnp.split(t, 2, -1)
            rot = jnp.concatenate([-x2, x1], -1)
            return t * jnp.cos(f) + rot * jnp.sin(f)
        key = jax.random.key(seed)
        ks = jax.random.split(key, 6)
        s = 0.02
        return {'x': jax.random.normal(ks[0], (B, N, DIM), jnp.float32), 'Wq': jax.random.normal(ks[1], (DIM, DIM), jnp.float32) * s, 'Wkv': jax.random.normal(ks[2], (DIM, DIM), jnp.float32) * s, 'Wo_ctx': jax.random.normal(ks[3], (DIM, DIM), jnp.float32) * s, 'bo_ctx': jnp.zeros((DIM,), jnp.float32), 'Wo_lat': jax.random.normal(ks[4], (DIM, DIM), jnp.float32) * s, 'bo_lat': jnp.zeros((DIM,), jnp.float32), 'ln_g': jnp.ones((DH,), jnp.float32), 'ln_b': jnp.zeros((DH,), jnp.float32)}
    _L1_attn_all = _L1_attn_setup()
    _L1_attn_in = {k: v for k, v in _L1_attn_all.items() if k in ('Wq', 'Wkv', 'Wo_ctx', 'bo_ctx', 'Wo_lat', 'bo_lat', 'ln_g', 'ln_b')}
    del _L1_attn_all

    def _L1_ffn_setup():
        import jax, jax.numpy as jnp
        import numpy as np
        D_MODEL = 192
        N_EXPERTS = 16
        TOP_K = 2
        D_FF = 4 * D_MODEL
        B, L = (4, 512)
        key = jax.random.key(seed)
        ks = jax.random.split(key, 6)
        s_in = 1.0 / np.sqrt(D_MODEL)
        s_ff = 1.0 / np.sqrt(D_FF)
        x = jax.random.normal(ks[0], (B, L, D_MODEL), dtype=jnp.float32)
        Wr = jax.random.uniform(ks[1], (N_EXPERTS, D_MODEL), jnp.float32, -s_in, s_in)
        W1 = jax.random.uniform(ks[2], (N_EXPERTS, D_MODEL, D_FF), jnp.float32, -s_in, s_in)
        b1 = jax.random.uniform(ks[3], (N_EXPERTS, D_FF), jnp.float32, -s_in, s_in)
        W2 = jax.random.uniform(ks[4], (N_EXPERTS, D_FF, D_MODEL), jnp.float32, -s_ff, s_ff)
        b2 = jax.random.uniform(ks[5], (N_EXPERTS, D_MODEL), jnp.float32, -s_ff, s_ff)
        return {'x': x, 'Wr': Wr, 'W1': W1, 'b1': b1, 'W2': W2, 'b2': b2}
    _L1_ffn_all = _L1_ffn_setup()
    _L1_ffn_in = {k: v for k, v in _L1_ffn_all.items() if k in ('Wr', 'W1', 'b1', 'W2', 'b2')}
    del _L1_ffn_all
    return {'x': x, 'L0_tok_W': _L0_tok_in['W'], 'L0_tok_b': _L0_tok_in['b'], 'L0_attn_W_qkv': _L0_attn_in['W_qkv'], 'L0_attn_b_qkv': _L0_attn_in['b_qkv'], 'L0_ffn_qkv_w': _L0_ffn_in['qkv_w'], 'L0_ffn_qkv_b': _L0_ffn_in['qkv_b'], 'L0_ffn_q_norm_w': _L0_ffn_in['q_norm_w'], 'L0_ffn_q_norm_b': _L0_ffn_in['q_norm_b'], 'L0_ffn_k_norm_w': _L0_ffn_in['k_norm_w'], 'L0_ffn_k_norm_b': _L0_ffn_in['k_norm_b'], 'L0_ffn_wg_w': _L0_ffn_in['wg_w'], 'L0_ffn_wg0_w': _L0_ffn_in['wg0_w'], 'L0_ffn_wg1_w': _L0_ffn_in['wg1_w'], 'L0_ffn_proj_w': _L0_ffn_in['proj_w'], 'L0_ffn_proj_b': _L0_ffn_in['proj_b'], 'L1_attn_Wq': _L1_attn_in['Wq'], 'L1_attn_Wkv': _L1_attn_in['Wkv'], 'L1_attn_Wo_ctx': _L1_attn_in['Wo_ctx'], 'L1_attn_bo_ctx': _L1_attn_in['bo_ctx'], 'L1_attn_Wo_lat': _L1_attn_in['Wo_lat'], 'L1_attn_bo_lat': _L1_attn_in['bo_lat'], 'L1_attn_ln_g': _L1_attn_in['ln_g'], 'L1_attn_ln_b': _L1_attn_in['ln_b'], 'L1_ffn_Wr': _L1_ffn_in['Wr'], 'L1_ffn_W1': _L1_ffn_in['W1'], 'L1_ffn_b1': _L1_ffn_in['b1'], 'L1_ffn_W2': _L1_ffn_in['W2'], 'L1_ffn_b2': _L1_ffn_in['b2']}

def reference(x, L0_tok_W, L0_tok_b, L0_attn_W_qkv, L0_attn_b_qkv, L0_ffn_qkv_w, L0_ffn_qkv_b, L0_ffn_q_norm_w, L0_ffn_q_norm_b, L0_ffn_k_norm_w, L0_ffn_k_norm_b, L0_ffn_wg_w, L0_ffn_wg0_w, L0_ffn_wg1_w, L0_ffn_proj_w, L0_ffn_proj_b, L1_attn_Wq, L1_attn_Wkv, L1_attn_Wo_ctx, L1_attn_bo_ctx, L1_attn_Wo_lat, L1_attn_bo_lat, L1_attn_ln_g, L1_attn_ln_b, L1_ffn_Wr, L1_ffn_W1, L1_ffn_b1, L1_ffn_W2, L1_ffn_b2):
    import jax
    import jax.numpy as jnp

    def _L0_tok_ref(images, W, b):
        import jax, jax.numpy as jnp
        import numpy as np
        PATCH = 16
        B, H, Wd, C = images.shape
        p = PATCH
        nh, nw = (H // p, Wd // p)
        x = images.reshape(B, nh, p, nw, p, C)
        x = x.transpose(0, 1, 3, 2, 4, 5)
        patches = x.reshape(B, nh * nw, p * p * C)
        return jnp.einsum('bnd,de->bne', patches, W) + b

    def _L0_attn_ref(x, W_qkv, b_qkv):
        import jax, jax.numpy as jnp
        import numpy as np
        EMBED_DIM = 192
        MAX_LEN = 256
        ALPHA = 0.99
        BATCH = 16

        def _retention_mask(sl, alpha, dtype):
            i = jnp.arange(sl)[:, None]
            j = jnp.arange(sl)[None, :]
            causal = i >= j
            exponent = jnp.where(causal, (i - j).astype(dtype), 0.0)
            decay = jnp.asarray(alpha, dtype) ** exponent
            return jnp.where(causal, decay, jnp.zeros((), dtype))
        bs, sl, d = x.shape
        qkv = x @ W_qkv + b_qkv
        q, k, v = jnp.split(qkv, 3, axis=-1)
        M = _retention_mask(sl, ALPHA, x.dtype)
        scores = jnp.einsum('bsd,btd->bst', q, k) / jnp.sqrt(jnp.asarray(d, x.dtype))
        out = jnp.einsum('bst,btd->bsd', scores * M[None, :, :], v)
        return out

    def _L0_ffn_ref(x, qkv_w, qkv_b, q_norm_w, q_norm_b, k_norm_w, k_norm_b, wg_w, wg0_w, wg1_w, proj_w, proj_b):
        import jax, jax.numpy as jnp
        import numpy as np
        DIM = 192
        H = 12
        HD = 64
        SHARED = 2
        ROUTED = 2
        E_ROUTED = H - SHARED
        LN_EPS = 1e-05

        def _layernorm(x, w, b):
            m = x.mean(-1, keepdims=True)
            v = ((x - m) ** 2).mean(-1, keepdims=True)
            return (x - m) * jax.lax.rsqrt(v + LN_EPS) * w + b
        B, N, C = x.shape
        scale = HD ** (-0.5)
        gates = jax.nn.softmax(x @ wg_w, axis=-1)
        _, idx = jax.lax.top_k(gates, ROUTED)
        mask = jax.nn.one_hot(idx, E_ROUTED, dtype=gates.dtype).sum(-2)
        rg = gates * mask
        denom = jnp.clip(rg.sum(-1, keepdims=True), jnp.finfo(rg.dtype).eps, None)
        routed_gates = rg / denom * ROUTED
        qkv = (x @ qkv_w + qkv_b).reshape(B, N, 3, H, HD)
        qkv = jnp.transpose(qkv, (2, 0, 3, 1, 4))
        q, k, v = (qkv[0], qkv[1], qkv[2])
        q = _layernorm(q, q_norm_w, q_norm_b)
        k = _layernorm(k, k_norm_w, k_norm_b)
        attn = jax.nn.softmax(jnp.einsum('bhqd,bhkd->bhqk', q * scale, k), axis=-1)
        o = jnp.einsum('bhqk,bhkd->bhqd', attn, v)
        o = jnp.transpose(o, (0, 2, 1, 3))
        shared_gates = jax.nn.softmax(x @ wg1_w, axis=-1) * SHARED
        w0 = jax.nn.softmax(x @ wg0_w, axis=-1) * 2.0
        shared_gates = w0[..., 0:1] * shared_gates
        routed_gates = w0[..., 1:2] * routed_gates
        masked_gates = jnp.concatenate([shared_gates, routed_gates], axis=-1)
        o = (masked_gates[..., None] * o).reshape(B, N, H * HD)
        return o @ proj_w + proj_b

    def _L1_attn_ref(x, Wq, Wkv, Wo_ctx, bo_ctx, Wo_lat, bo_lat, ln_g, ln_b):
        import jax, jax.numpy as jnp
        import numpy as np
        B, N, DIM, H = (8, 256, 192, 12)
        DH = DIM // H
        LATENT = 32
        EPS = 1e-05

        def _heads(t):
            b, n, _ = t.shape
            return t.reshape(b, n, H, DH).transpose(0, 2, 1, 3).reshape(b * H, n, DH)

        def _merge(t, b):
            _, n, dh = t.shape
            return t.reshape(b, H, n, dh).transpose(0, 2, 1, 3).reshape(b, n, H * dh)

        def _ln(v, g, bta):
            mu = v.mean(-1, keepdims=True)
            var = ((v - mu) ** 2).mean(-1, keepdims=True)
            return (v - mu) * jax.lax.rsqrt(var + EPS) * g + bta

        def _rope(t):
            n, dh = (t.shape[-2], t.shape[-1])
            inv = 1.0 / 10000.0 ** (jnp.arange(0, dh, 2, dtype=jnp.float32) / dh)
            f = jnp.arange(n, dtype=jnp.float32)[:, None] * inv[None, :]
            f = jnp.concatenate([f, f], -1)[None]
            x1, x2 = jnp.split(t, 2, -1)
            rot = jnp.concatenate([-x2, x1], -1)
            return t * jnp.cos(f) + rot * jnp.sin(f)
        b, n, _ = x.shape
        ctx = n - LATENT
        q = _heads(x @ Wq)
        kv = _heads(x @ Wkv)
        q = _rope(q)
        kv = _rope(kv)
        q = q * DH ** (-0.5)
        q_lat, q_ctx = (q[:, ctx:], q[:, :ctx])
        kv_ctx = kv[:, :ctx]
        lkv = _ln(kv, ln_g, ln_b)
        lkv_ctx = _ln(kv_ctx, ln_g, ln_b)
        attn_lat = jax.nn.softmax(jnp.einsum('bid,bkd->bik', q_lat, kv), axis=-1)
        attn_ctx = jax.nn.softmax(jnp.einsum('bid,bkd->bik', q_ctx, kv_ctx), axis=-1)
        out_lat = _merge(jnp.einsum('bik,bkd->bid', attn_lat, lkv), b) @ Wo_lat + bo_lat
        out_ctx = _merge(jnp.einsum('bik,bkd->bid', attn_ctx, lkv_ctx), b) @ Wo_ctx + bo_ctx
        return jnp.concatenate([out_ctx, out_lat], axis=1)

    def _L1_ffn_ref(x, Wr, W1, b1, W2, b2):
        import jax, jax.numpy as jnp
        import numpy as np
        D_MODEL = 192
        N_EXPERTS = 16
        TOP_K = 2
        D_FF = 4 * D_MODEL
        B, L = (4, 512)
        logits = jnp.einsum('bld,ed->ble', x, Wr)
        probs = jax.nn.softmax(logits, axis=-1)
        top_p, top_idx = jax.lax.top_k(probs, TOP_K)
        gating = jnp.sum(jax.nn.one_hot(top_idx, N_EXPERTS, dtype=probs.dtype) * top_p[..., None], axis=-2)
        gate_e = jnp.moveaxis(gating, -1, 0)

        def step(y, params):
            W1e, b1e, W2e, b2e, ge = params
            h = jax.nn.gelu(jnp.einsum('bld,df->blf', x, W1e) + b1e, approximate=False)
            out = jnp.einsum('blf,fd->bld', h, W2e) + b2e
            return (y + ge[..., None] * out, None)
        y0 = jnp.zeros_like(x)
        y, _ = jax.lax.scan(step, y0, (W1, b1, W2, b2, gate_e))
        return x + y
    h = _L0_tok_ref(x, L0_tok_W, L0_tok_b)
    h = h + _L0_attn_ref(_layernorm(h, axis=-1), L0_attn_W_qkv, L0_attn_b_qkv)
    h = h + _L0_ffn_ref(_layernorm(h, axis=-1), L0_ffn_qkv_w, L0_ffn_qkv_b, L0_ffn_q_norm_w, L0_ffn_q_norm_b, L0_ffn_k_norm_w, L0_ffn_k_norm_b, L0_ffn_wg_w, L0_ffn_wg0_w, L0_ffn_wg1_w, L0_ffn_proj_w, L0_ffn_proj_b)
    h = h + _L1_attn_ref(_layernorm(h, axis=-1), L1_attn_Wq, L1_attn_Wkv, L1_attn_Wo_ctx, L1_attn_bo_ctx, L1_attn_Wo_lat, L1_attn_bo_lat, L1_attn_ln_g, L1_attn_ln_b)
    h = h + _L1_ffn_ref(_layernorm(h, axis=-1), L1_ffn_Wr, L1_ffn_W1, L1_ffn_b1, L1_ffn_W2, L1_ffn_b2)
    return h

_drawn_inputs = setup_inputs


def setup_inputs(seed=0):
    import zlib

    import numpy as np

    out = dict(_drawn_inputs(seed))
    spreads = {'L0_tok_b': (0.0, 0.1),
     'L0_ffn_qkv_b': (0.0, 0.334),
     'L0_ffn_q_norm_w': (1.0, 0.6),
     'L0_ffn_q_norm_b': (0.0, 0.8),
     'L0_ffn_k_norm_w': (1.0, 0.6),
     'L0_ffn_k_norm_b': (0.0, 0.8),
     'L0_ffn_proj_b': (0.0, 0.1),
     'L1_attn_bo_ctx': (0.0, 0.1),
     'L1_attn_bo_lat': (0.0, 0.1),
     'L1_attn_ln_g': (1.0, 0.6),
     'L1_attn_ln_b': (0.0, 0.465)}
    factors = {'L0_ffn_qkv_w': 3.209,
     'L0_ffn_wg_w': 2.971,
     'L0_ffn_wg0_w': 8.0,
     'L0_ffn_wg1_w': 8.0,
     'L1_attn_Wq': 8.0,
     'L1_ffn_Wr': 3.498,
     'L1_ffn_W1': 3.408,
     'L1_ffn_b1': 8.0,
     'L1_ffn_W2': 3.193,
     'L1_ffn_b2': 8.0}
    for name, (base, spread) in spreads.items():
        noise = np.random.default_rng([zlib.crc32(name.encode()), seed]).standard_normal(out[name].shape)
        drawn = base * np.exp(spread * noise) if base else spread * noise
        out[name] = jnp.asarray(drawn.astype(out[name].dtype))
    for name, factor in factors.items():
        out[name] = (out[name] * factor).astype(out[name].dtype)
    return out
```

```python
from contextlib import ExitStack

import numpy as np

import concourse.bass as bass
from concourse import mybir

BATCH, PATCH, GRID = 32, 16, 7
N_TOK = GRID * GRID
D = 192
DH2 = D // 2
PD = PATCH * PATCH * 3
PC = PD // 128
P = 2 * N_TOK
TILES = BATCH // 2
PAIRS = TILES // 2
H0, HD0 = 12, 64
RH, SH = 10, 2
H1, HD1, PAD1 = 12, 16, 32
LATENT = 32
CTX = N_TOK - LATENT
E, FF, FC = 16, 768, 6
EPS = 1e-5
HALF6 = 6 * P
BANK = 512
BIG = -1e30

ET = 128
ETILES = (2 * BATCH * N_TOK - E) // ET + E
ETILES += ETILES % 2
MAXT = -(-BATCH * N_TOK // ET)


def constants():
    f = np.float32
    r = np.arange(P)
    n, img = r % N_TOK, r // N_TOK
    diff = (n[:, None] - n[None, :]).astype(f)
    ok = (img[:, None] == img[None, :]) & (diff >= 0)
    decay = np.where(ok, f(0.99) ** np.where(ok, diff, 0).astype(f), f(0)).astype(f)
    retT = np.ascontiguousarray((decay / np.sqrt(f(D))).T.astype(f))
    inv = (1.0 / 10000.0 ** (np.arange(0, HD1, 2, dtype=f) / f(HD1))).astype(f)
    ang = n.astype(f)[:, None] * inv[None, :]
    ang = np.concatenate([ang, ang], -1)
    cos, sin = np.cos(ang).astype(f), np.sin(ang).astype(f)
    sin[:, :HD1 // 2] *= -1
    q = f(HD1 ** -0.5)
    rope = np.stack([np.concatenate([np.tile(cos * q, (1, H1)), np.tile(cos, (1, H1))], 1),
                     np.concatenate([np.tile(sin * q, (1, H1)), np.tile(sin, (1, H1))], 1)], 1)
    imgq = np.stack([img == 0, img == 1]).astype(f)
    imgk = np.stack([img == 1, img == 0]).astype(f) * f(BIG)
    ctx = n < CTX
    grpq = np.stack([(img == i) & (ctx == c) for i in (0, 1) for c in (True, False)]).astype(f)
    grpk = np.stack([(img != i) | (c & ~ctx) for i in (0, 1) for c in (True, False)]).astype(f) * f(BIG)
    m0, m1 = np.zeros((128, 4 * P), f), np.zeros((128, 4 * P), f)
    for r0 in range(0, 128, HD0):
        m0[r0:r0 + 2] = np.concatenate([imgq] + [imgk] * 3, 1)
    for r0 in range(0, 128, PAD1):
        m1[r0:r0 + 4] = np.concatenate([grpq] + [grpk] * 3, 1)
    small = np.zeros((P, 16 + 2 + ETILES + MAXT), f)
    small[:, :16] = np.arange(16)
    small[:, 16] = ctx
    small[:, 17] = ~ctx
    small[:, 18:18 + ETILES] = np.arange(ETILES)
    small[:, 18 + ETILES:] = np.arange(MAXT) * ET
    return {"ident": np.eye(128, dtype=f), "retT": retT, "rope": rope.reshape(P, -1).astype(f),
            "mask0": m0.astype(f), "mask1": m1.astype(f), "small": small,
            "before": (r[:, None] < r[None, :]).astype(f)}


def vit_tower(nc, a, out):
    F32, I32, U32, BF16 = mybir.dt.float32, mybir.dt.int32, mybir.dt.uint32, mybir.dt.bfloat16
    ALU, ACT, AX = mybir.AluOpType, mybir.ActivationFunctionType, mybir.AxisListType
    ctx = ExitStack()
    with ctx:
        def sb(name, shape, dt=F32):
            return ctx.enter_context(nc.sbuf_tensor(name, shape, dt))

        def sem(name):
            return ctx.enter_context(nc.semaphore(name))

        rows_dram = nc.dram_tensor("expert_rows", [ETILES * ET, D], F32, kind="Internal").ap()
        res_dram = nc.dram_tensor("expert_results", [ETILES * ET, D], F32, kind="Internal").ap()

        ident = sb("ident", [128, 128])
        retT = sb("retT", [P, P])
        rope = sb("rope", [P, 4 * D])
        mask0f, mask0 = sb("mask0f", [128, 4 * P]), sb("mask0", [128, 4 * P], BF16)
        mask1f, mask1 = sb("mask1f", [128, 4 * P]), sb("mask1", [128, 4 * P], BF16)
        small = sb("small", [P, 18 + ETILES + MAXT])
        before = sb("before", [P, P])
        w_tok = sb("w_tok", [128, PC, D])
        b_tok = sb("b_tok", [P, D])
        w_ret = sb("w_ret", [DH2 + 1, 2, 3 * D])
        w_moh = sb("w_moh", [DH2 + 1, 2, 3 * H0 * HD0])
        w_gate = sb("w_gate", [DH2, 2, RH + 4])
        w_proj = sb("w_proj", [128, H0 // 2, D])
        b_proj = sb("b_proj", [P, D])
        qk_affine = sb("qk_affine", [128, 4])
        w_l1 = sb("w_l1", [DH2, 2, 2 * D])
        w_out = sb("w_out", [DH2 + 1, 2, 2 * D])
        ln_gb = sb("ln_gb", [P, 2, HD1])
        w_rt = sb("w_rt", [DH2, 2, E])
        ones = sb("ones", [P, P])
        neg_half = sb("neg_half", [P, 24])
        wmean = sb("wmean", [DH2 + 1, 2, 24])
        zeros = sb("zeros", [128, ETILES * ET * D // 128 // 8])

        x_in = sb("x_in", [128, 2, PC * P])
        h = sb("h", [P, 2, D])
        hb = sb("hb", [P, 2, D])
        xn = sb("xn", [P, 2, D])
        stats = sb("stats", [P, 2, 6])
        mv = sb("mv", [P, 2, 2])
        rstd = sb("rstd", [P, 2, 1])
        xnT = sb("xnT", [DH2 + 1, 2, 2 * P])
        qkT0 = sb("qkT0", [DH2, 2, 4 * P])
        v0 = sb("v0", [P, 2, D])
        pT0 = sb("pT0", [P, 2, P])
        sq = sb("sq", [P, 2, 1536])
        ss = sb("ss", [P, 2, 24])
        sr = sb("sr", [P, 2, 24])
        qn = sb("qn", [P, 2, 1536])
        qT = sb("qT", [128, 2, 6 * P])
        kT = sb("kT", [128, 2, 6 * P])
        v_aug = sb("v_aug", [P, 2, H0 * (HD0 + 1)])
        nmax = sb("nmax", [P, 2, H0])
        sc = sb("sc", [128, 2, H0 * P])
        pr = sb("pr", [128, 2, H0 * P])
        pT = sb("pT", [P, 2, H0 * P])
        fac = sb("fac", [P, 2, H0])
        o = sb("o", [P, 2, H0 * HD0])
        oT = qT
        ropa, ropb = sc[0:P, :, 0:2 * D], sc[0:P, :, 2 * D:4 * D]
        qk1 = sb("qk1", [P, 2, 2 * H1 * PAD1])
        lsum = sb("lsum", [P, 2, H1])
        lc = sb("lc", [P, 2, D])
        lsq = sb("lsq", [P, 2, D])
        lr = sb("lr", [P, 2, H1])
        v1_aug = sb("v1_aug", [P, 2, H1 * (HD1 + 1)])
        om = sb("om", [P, 2, D])
        omT = sb("omT", [DH2 + 1, 2, 2 * P])
        gl = sb("gl", [P, 2, RH + 4])
        gmx = sb("gmx", [P, 2, 8])
        gidx = sb("gidx", [P, 2, 8], U32)
        gidf = sb("gidf", [P, 2, 2])
        gm2 = sb("gm2", [P, 4])
        gsum = sb("gsum", [P, 2, 4])
        ge = sb("ge", [P, 2, RH + 4])
        gmask = sb("gmask", [P, 2, RH])
        gden = sb("gden", [P, 2, 2])
        gates = sb("gates", [P, 2, H0])
        rmx = sb("rmx", [P, 2, 8])
        ridx = sb("ridx", [P, 2, 8], U32)

        oh = sb("oh", [P, 2, TILES * E])
        both = sb("both", [P, TILES * E])
        cnt = sb("cnt", [P, TILES * E])
        cum = sb("cum", [P, 2, TILES * E])
        prod = sb("prod", [P, 2, TILES * E])
        tmax = sb("tmax", [P, TILES])
        cmp = sb("cmp", [P, E * max(MAXT, ETILES)])
        tcum = sb("tcum", [P, 3, E])
        slot_f = sb("slot_f", [P, 2, TILES])
        slot_u = sb("slot_u", [P, 2, TILES], U32)
        gate_k = sb("gate_k", [P, 2, TILES])
        eid_f = sb("eid_f", [1, ETILES])
        eid = sb("eid", [1, ETILES], I32)
        xe = sb("xe", [ET, 2, D])
        xeT = sb("xeT", [DH2 + 1, 2, 2 * ET])
        w1, w2 = w_moh, pr
        b2 = sb("b2", [ET, 2, D])
        hT = sc
        ye = sb("ye", [ET, 2, D])
        got = [sq[:, :, :].rearrange("p a b -> p (a b)"), qn[:, :, :].rearrange("p a b -> p (a b)")]

        xn_all = sb("xn_all", [P, TILES, D])
        base_all = sb("base_all", [P, TILES, D])
        lg_all = sb("lg_all", [P, TILES, E])
        id_all = sb("id_all", [P, TILES, 2])

        PS = [ctx.enter_context(nc.psum_tensor(f"slot{i}", [128, 2 * BANK], F32)) for i in range(4)]

        def slot(stage, hf):
            return PS[2 * (stage % 2) + hf]

        s_w, s_center = sem("constants_loaded"), sem("weight_centering")
        s_setup_p, s_setup_v = sem("pool_setup"), sem("vector_setup")
        s_zero, s_zeros = sem("expert_rows_zeroed"), sem("zeros_ready")
        s_x = [sem(f"patches_loaded{i}") for i in range(2)]
        names = ("psum_tok psum_xnT0 psum_qkv0 psum_s0 psum_o0 psum_xnT1 psum_v psum_q psum_k psum_qT psum_kT "
                 "psum_sa psum_sb psum_pTa psum_pTb psum_pv psum_oT psum_proj psum_xnT2 psum_qkv1 psum_qkT1 "
                 "psum_s1a psum_s1b psum_p1Ta psum_p1Tb psum_pv1 psum_omT psum_out psum_xnT3 psum_rt "
                 "h0 ag0 ag1 ag2 ag3 st0 va0 rs0 xn0 xnT0 qkT0 v0 pT0 "
                 "h1 st1 va1 rs1 xn1 xnT1 hb v sqq sqk gl gpick gsub gexp gstep gates "
                 "ssk vss srk qn kn qT kT nma suba ea nmb subb eb pTa pTb fac0 fac o oT h2 st2 va2 rs2 xn2 xnT2 "
                 "ropa rope qk1 lsum lmean lc lsq lss lvar lr lv1 lv2 v1 q1T k1T nm1a sub1a e1a nm1b sub1b e1b "
                 "p1Ta p1Tb rden om omT h3a h3 st3 va3 rs3 xn3 xn_kept base xnT3 rtop rlg ridx").split()
        S = {n: sem(n) for n in names}

        def wait_apart(eng, sm, value):
            eng.wait_ge(s_setup_v, 2)
            eng.wait_ge(sm, value)

        def v3(ap, k):
            return ap.rearrange("p (a b) -> p a b", a=k)

        def banks(ps, n, used):
            return ps[0:n, :].rearrange("p (b c) -> p b c", b=2)[:, :, 0:used]


        s_route, s_eid = sem("routing_step"), sem("expert_of_tile_ready")
        s_both, s_rank, s_rexp, s_rsub = sem("choices_ready"), sem("psum_ranks"), sem("router_exp"), sem("router_logits_less_max")
        s_slots = sem("slots_ready")
        s_scat = sem("rows_scattered")
        s_rows = [sem(f"expert_rows_loaded{i}") for i in range(2)]
        s_wts = [sem(f"expert_weights_loaded{i}") for i in range(2)]
        s_xeT, s_xe, s_up, s_hT = sem("psum_xeT"), sem("xeT_ready"), sem("psum_hidden"), sem("hidden_ready")
        s_dn, s_y = sem("psum_expert_out"), sem("expert_out_ready")
        s_res = [sem(f"results_stored{i}") for i in range(2)]
        s_got = [sem(f"results_gathered{i}") for i in range(4)]
        s_yfree, s_fin, s_out = sem("result_buffer_free"), sem("output_ready"), sem("output_stored")

        def moe_sync(sp):
            def load(j, hf, again):
                e = sp.value_load(eid[0:1, bass.ds(j, 1)] if again is not None else eid[0:1, j:j + 1], min_val=0, max_val=E - 1)
                if again is not None:
                    sp.wait_ge(s_y, again + 2)
                for dst, src in ((w1[0:DH2, hf, 0:2 * FF], a["w1"]), (w1[DH2:DH2 + 1, hf, 0:FF], a["b1"]),
                                 (w2[:, hf, 0:FC * D], a["w2"])):
                    sp.dma_start(dst, src[bass.ds(e, 1)].rearrange("o p c -> (o p) c")).then_inc(s_wts[hf], 16)
                sp.dma_start(b2[:, hf, :], a["b2"][bass.ds(e, 1)].rearrange("o p c -> (o p) c").broadcast_to([ET, D]))\
                    .then_inc(s_wts[hf], 16)
                if again is None:
                    sp.wait_ge(s_scat, 16 * 2 * TILES)
                sp.dma_start(xe[:, hf, :], rows_dram[bass.ds(j * ET, ET), :] if again is not None
                             else rows_dram[j * ET:(j + 1) * ET, :]).then_inc(s_rows[hf], 16)

            sp.wait_ge(s_eid, 1)
            for hf in range(2):
                load(hf, hf, None)
            with sp.Fori(1, ETILES // 2) as i:
                for hf in range(2):
                    load(2 * i + hf, hf, 2 * i + hf - 1)
            for c in range(4):
                sp.wait_ge(s_fin, c + 1)
                t0, t1 = c * TILES // 4, (c + 1) * TILES // 4
                sp.dma_start(out.rearrange("b n d -> (b n) d").rearrange("(t p) d -> p t d", p=P)[:, t0:t1, :],
                             base_all[:, t0:t1, :]).then_inc(s_out, 16)
            sp.wait_ge(s_out, 64)

        def moe_tensor(pe):
            pe.wait_ge(s_both, 1)
            pe.matmul(PS[0][0:P, 0:TILES * E], before[:, :], both[:, :], start=True, stop=True)
            pe.matmul(PS[0][0:P, BANK:BANK + TILES * E], ones[:, :], both[:, :], start=True, stop=True).then_inc(s_rank, 1)
            pe.wait_ge(s_slots, 1)
            with pe.Fori(0, ETILES // 2) as i:
                pair = [(0, 2 * i + 1), (1, 2 * i + 2)]
                for hf, t1 in pair:
                    pe.wait_ge(s_rows[hf], 16 * i + 16)
                    pe.wait_ge(s_y, t1)
                    for c in range(2):
                        mm = pe.transpose(PS[hf][0:DH2, ET * c:ET * c + ET], xe[:, hf, DH2 * c:DH2 * c + DH2], ident[:, :])
                    mm.then_inc(s_xeT, 1)
                for hf, t1 in pair:
                    pe.wait_ge(s_wts[hf], 64 * i + 64)
                    pe.wait_ge(s_xe, t1)
                    for f in range(FC):
                        for c in range(2):
                            k = DH2 + 1 - c
                            mm = pe.matmul(PS[2 + hf][:, ET * f:ET * f + ET],
                                           w1[0:k, hf, c * FF + 128 * f:c * FF + 128 * f + 128],
                                           xeT[0:k, hf, ET * c:ET * c + ET], start=c == 0, stop=c == 1)
                    mm.then_inc(s_up, 1)
                for hf, t1 in pair:
                    pe.wait_ge(s_hT, t1)
                    for f in range(FC):
                        mm = pe.matmul(PS[hf][:, 0:D], hT[:, hf, ET * f:ET * f + ET], w2[:, hf, f * D:f * D + D],
                                       start=f == 0, stop=f == FC - 1)
                    mm.then_inc(s_dn, 1)

        def moe_scalar(act):
            act.wait_ge(s_rsub, 1)
            act.activation(lg_all[:, :, :], lg_all[:, :, :], ACT.Exp).then_inc(s_rexp, 1)
            with act.Fori(0, ETILES // 2) as i:
                for hf, t1 in [(0, 2 * i + 1), (1, 2 * i + 2)]:
                    act.wait_ge(s_up, t1)
                    act.activation(hT[:, hf, 0:FF], PS[2 + hf][:, 0:FF], ACT.Gelu).then_inc(s_hT, 1)

        def moe_gpsimd(pool):
            pool.wait_ge(s_zero, 16 * 8)
            pool.wait_ge(s_slots, 2)
            pool.wait_ge(S["base"], TILES + 2)
            for t in range(TILES):
                for k in range(2):
                    pool.indirect_dma_start(out=rows_dram, out_offset=bass.IndirectOffsetOnAxis(ap=slot_u[:, k, t:t + 1], axis=0),
                                            in_=xn_all[:, t, :], in_offset=None).then_inc(s_scat, 16)
            pool.sem_inc(s_yfree, 2)
            with pool.Fori(0, ETILES // 2) as i:
                for hf, t1 in [(0, 2 * i + 1), (1, 2 * i + 2)]:
                    pool.wait_ge(s_y, t1 + 2)
                    pool.dma_start(res_dram[bass.ds((2 * i + hf) * ET, ET), :], ye[:, hf, :]).then_inc(s_res[hf], 16)
                    pool.wait_ge(s_res[hf], 16 * i + 16)
                    pool.sem_inc(s_yfree, 1)
            for t in range(TILES):
                for k in range(2):
                    pool.indirect_dma_start(out=got[k][:, t * D:(t + 1) * D], out_offset=None, in_=res_dram,
                                            in_offset=bass.IndirectOffsetOnAxis(ap=slot_u[:, k, t:t + 1], axis=0))\
                        .then_inc(s_got[4 * t // TILES], 16)

        def moe_vector(dve):
            steps = [0]

            def after(ins):
                steps[0] += 1
                ins.then_inc(s_route, 1)
                dve.wait_ge(s_route, steps[0])

            TE = TILES * E
            dve.wait_ge(S["rlg"], TILES + 2)
            L = lg_all[:, :, :]
            after(dve.tensor_reduce(tmax[:, :], L, AX.X, ALU.max))
            dve.tensor_tensor(L, L, tmax[:, :].unsqueeze(2).broadcast_to([P, TILES, E]), ALU.subtract).then_inc(s_rsub, 1)
            for k in range(2):
                m = dve.tensor_tensor(v3(oh[:, k, :], TILES), small[:, 0:E].unsqueeze(1).broadcast_to([P, TILES, E]),
                                      id_all[:, :, k:k + 1].broadcast_to([P, TILES, E]), ALU.is_equal)
            after(m)
            dve.tensor_tensor(both[:, :], oh[:, 0, :], oh[:, 1, :], ALU.add).then_inc(s_both, 1)
            dve.wait_ge(s_rank, 1)
            after(dve.tensor_copy(cnt[:, :], PS[0][0:P, BANK:BANK + TE]))
            src, dst = cnt[:, :], 0
            s = 1
            while s < TILES:
                d = cum[:, dst, :]
                dve.tensor_copy(d[:, 0:s * E], src[:, 0:s * E])
                after(dve.tensor_tensor(d[:, s * E:TE], src[:, s * E:TE], src[:, 0:TE - s * E], ALU.add))
                src, dst, s = d, 1 - dst, 2 * s
            total = src[:, TE - E:TE]
            c3 = v3(cmp[:, 0:E * MAXT], E)
            after(dve.tensor_tensor(c3, total.unsqueeze(2).broadcast_to([P, E, MAXT]),
                                    small[:, 18 + ETILES:].unsqueeze(1).broadcast_to([P, E, MAXT]), ALU.is_gt))
            after(dve.tensor_reduce(tcum[:, 0, :], c3, AX.X, ALU.add))
            tsrc, tdst, s = tcum[:, 0, :], 1, 1
            while s < E:
                d = tcum[:, tdst, :]
                dve.tensor_copy(d[:, 0:s], tsrc[:, 0:s])
                after(dve.tensor_tensor(d[:, s:E], tsrc[:, s:E], tsrc[:, 0:E - s], ALU.add))
                tsrc, tdst, s = d, 3 - tdst, 2 * s
            e3 = v3(cmp[0:1, 0:ETILES * E], ETILES)
            after(dve.tensor_tensor(e3, small[0:1, 18:18 + ETILES].unsqueeze(2).broadcast_to([1, ETILES, E]),
                                    tsrc[0:1, :].unsqueeze(1).broadcast_to([1, ETILES, E]), ALU.is_ge))
            after(dve.tensor_reduce(eid_f[:, :], e3, AX.X, ALU.add))
            dve.tensor_scalar(eid[:, :], eid_f[:, :], float(E - 1), None, ALU.min).then_inc(s_eid, 1)
            after(dve.tensor_tensor(tcum[:, 0, :], tsrc, tcum[:, 0, :], ALU.subtract))
            after(dve.tensor_scalar(tcum[:, 0, :], tcum[:, 0, :], float(ET), None, ALU.mult))
            after(dve.tensor_tensor(src, src, cnt[:, :], ALU.subtract))
            after(dve.tensor_tensor(src, PS[0][0:P, 0:TE], src, ALU.add))
            after(dve.tensor_tensor(v3(src, TILES), v3(src, TILES), tcum[:, 0:1, :].broadcast_to([P, TILES, E]), ALU.add))
            for k in range(2):
                m = dve.tensor_tensor(prod[:, k, :], oh[:, k, :], src, ALU.mult)
            m.then_inc(s_slots, 1)
            dve.wait_ge(s_slots, 1)
            dve.tensor_reduce(slot_f[:, 0, :], v3(prod[:, 0, :], TILES), AX.X, ALU.add)
            after(dve.tensor_reduce(slot_f[:, 1, :], v3(prod[:, 1, :], TILES), AX.X, ALU.add))
            dve.tensor_copy(slot_u[:, :, :], slot_f[:, :, :]).then_inc(s_slots, 1)
            dve.wait_ge(s_rexp, 1)
            after(dve.tensor_reduce(tmax[:, :], L, AX.X, ALU.add))
            after(dve.reciprocal(tmax[:, :], tmax[:, :]))
            for k in range(2):
                m = dve.tensor_tensor(prod[:, k, :], oh[:, k, :], L.rearrange("p a b -> p (a b)"), ALU.mult)
            after(m)
            for k in range(2):
                m = dve.tensor_reduce(gate_k[:, k, :], v3(prod[:, k, :], TILES), AX.X, ALU.add)
            after(m)
            for k in range(2):
                m = dve.tensor_tensor(gate_k[:, k, :], gate_k[:, k, :], tmax[:, :], ALU.mult)
            after(m)

            dve.sem_inc(s_y, 2)
            with dve.Fori(0, ETILES // 2) as i:
                pair = [(0, 2 * i + 1), (1, 2 * i + 2)]
                for hf, t1 in pair:
                    dve.wait_ge(s_xeT, t1)
                    dve.tensor_copy(xeT[0:DH2, hf, :], PS[hf][0:DH2, 0:2 * ET]).then_inc(s_xe, 1)
                for hf, t1 in pair:
                    dve.wait_ge(s_dn, t1)
                    dve.wait_ge(s_yfree, t1)
                    dve.tensor_tensor(ye[:, hf, :], PS[hf][:, 0:D], b2[:, hf, :], ALU.add).then_inc(s_y, 1)
            for c in range(4):
                dve.wait_ge(s_got[c], 16 * 2 * TILES // 4)
                ts = range(c * TILES // 4, (c + 1) * TILES // 4)
                for k in range(2):
                    for t in ts:
                        m = dve.scalar_tensor_tensor(base_all[:, t, :], got[k][:, t * D:(t + 1) * D], gate_k[:, k, t:t + 1],
                                                     base_all[:, t, :], ALU.mult, ALU.add)
                    if k == 0:
                        after(m)
                m.then_inc(s_fin, 1)

        block = ctx.enter_context(nc.Block())

        def head0_at(g, b, j):
            return 6 * g + 2 * j + b

        def head1_at(g, b, j):
            return 4 * j + 2 * g + b

        place0 = {head0_at(g, b, j): 6 * g + 3 * b + j for g in range(2) for b in range(2) for j in range(3)}
        place1 = {head1_at(g, b, j): 6 * g + 3 * b + j for g in range(2) for b in range(2) for j in range(3)}

        loads = [(ident[:, :], a["ident"]), (retT[:, :], a["retT"]), (rope[:, :], a["rope"]),
                 (mask0f[:, :], a["mask0"]), (mask1f[:, :], a["mask1"]), (small[:, :], a["small"]),
                 (before[:, :], a["before"]),
                 (w_tok[:, :, :], a["w_tok"]), (b_tok[:, :], a["b_tok"].partition_broadcast(P)),
                 (w_ret[0:DH2, :, :], a["w_ret"]), (w_ret[DH2:DH2 + 1, 0, :], a["b_ret"]),
                 (w_moh[0:DH2, :, :], a["w_moh"]), (w_moh[DH2:DH2 + 1, 0, :], a["b_moh"]),
                 (w_gate[:, :, 0:RH], a["w_gr"]), (w_gate[:, :, RH:RH + 2], a["w_g0"]),
                 (w_gate[:, :, RH + 2:RH + 4], a["w_g1"]),
                 (w_proj[:, :, :], a["w_proj"]), (b_proj[:, :], a["b_proj"].partition_broadcast(P)),
                 (w_l1[:, :, 0:D], a["w_q1"]), (w_l1[:, :, D:2 * D], a["w_kv1"]),
                 (w_out[0:DH2, :, 0:D], a["w_octx"]), (w_out[0:DH2, :, D:2 * D], a["w_olat"]),
                 (w_out[DH2:DH2 + 1, 0, 0:D], a["b_octx"]), (w_out[DH2:DH2 + 1, 0, D:2 * D], a["b_olat"]),
                 (ln_gb[:, 0, :], a["ln_g"].partition_broadcast(P)),
                 (ln_gb[:, 1, :], a["ln_b"].partition_broadcast(P)),
                 (w_rt[:, :, :], a["w_rt"])]
        for col, name in enumerate(("qw", "qb", "kw", "kb")):
            for k in range(2):
                loads.append((qk_affine[64 * k:64 * k + 64, col:col + 1], a[name]))

        @block.sync
        def _(sp):
            for hf in range(2):
                sp.dma_start(x_in[:, hf, :], a["x"][hf]).then_inc(s_x[hf], 16)
            for dst, src in loads:
                sp.dma_start(dst, src).then_inc(s_w, 16)
            with sp.Fori(1, PAIRS) as i:
                for hf in range(2):
                    sp.wait_ge(S["psum_tok"], 2 * i + hf - 1)
                    sp.dma_start(x_in[:, hf, :], a["x"][bass.ds(2 * i + hf, 1)].rearrange("o p c -> (o p) c")).then_inc(s_x[hf], 16)

            moe_sync(sp)

        @block.tensor
        def _(pe):
            pe.wait_ge(s_w, 16 * len(loads))
            pe.wait_ge(s_setup_p, 1)
            pe.wait_ge(s_setup_v, 2)

            def transposes(dst, src, n, w, rows=P):
                for c in range(n):
                    mm = pe.transpose(dst(c), src[:, w * c:w * (c + 1)], ident[0:rows, 0:rows])
                return mm

            def over_width(dst, lhsT, hf, rhs, rows0=DH2 + 1):
                for c in range(2):
                    k = rows0 if c == 0 else DH2
                    mm = pe.matmul(dst, lhsT[0:k, hf, c * P:(c + 1) * P], rhs(c, k), start=c == 0, stop=c == 1)
                return mm

            with pe.Fori(0, PAIRS) as i:
                pair = [(0, 2 * i + 1), (1, 2 * i + 2)]
                for hf, t1 in pair:
                    pe.wait_ge(s_x[hf], 16 * i + 16)
                    pe.wait_ge(S["xnT3"], t1 + 0)
                    ps = slot(0, hf)
                    for c in range(PC):
                        mm = pe.matmul(ps[0:P, 0:D], x_in[:, hf, c * P:(c + 1) * P], w_tok[:, c, :],
                                       start=c == 0, stop=c == PC - 1)
                    mm.then_inc(S["psum_tok"], 1)
                for hf, t1 in pair:
                    pe.wait_ge(S["rlg"], t1 + 0)
                    pe.wait_ge(S["xn0"], t1)
                    ps = slot(1, hf)
                    transposes(lambda c: ps[0:DH2, P * c:P * c + P], xn[:, hf, :], 2, DH2).then_inc(S["psum_xnT0"], 1)
                for hf, t1 in pair:
                    pe.wait_ge(S["h0"], t1)
                    pe.wait_ge(S["xnT0"], t1)
                    ps = slot(2, hf)
                    for m in range(4):
                        for c in range(2):
                            k = DH2 + 1 - c
                            pe.matmul(ps[0:DH2, P * m:P * m + P], w_ret[0:k, c, DH2 * m:DH2 * m + DH2],
                                      xnT[0:k, hf, c * P:(c + 1) * P], start=c == 0, stop=c == 1)
                    over_width(ps[0:P, BANK:BANK + D], xnT, hf, lambda c, k: w_ret[0:k, c, 2 * D:3 * D])\
                        .then_inc(S["psum_qkv0"], 1)
                for hf, t1 in pair:
                    pe.wait_ge(S["qkT0"], t1)
                    ps = slot(3, hf)
                    for c in range(2):
                        mm = pe.matmul(ps[0:P, 0:P], qkT0[:, hf, (2 + c) * P:(3 + c) * P],
                                       qkT0[:, hf, c * P:(c + 1) * P], start=c == 0, stop=c == 1)
                    mm.then_inc(S["psum_s0"], 1)
                for hf, t1 in pair:
                    pe.wait_ge(S["v0"], t1)
                    pe.wait_ge(S["pT0"], t1)
                    ps = slot(4, hf)
                    pe.matmul(ps[0:P, 0:D], pT0[:, hf, :], v0[:, hf, :], start=True, stop=True)\
                        .then_inc(S["psum_o0"], 1)
                for hf, t1 in pair:
                    pe.wait_ge(S["xn1"], t1)
                    ps = slot(5, hf)
                    transposes(lambda c: ps[0:DH2, P * c:P * c + P], xn[:, hf, :], 2, DH2).then_inc(S["psum_xnT1"], 1)
                for st, part, name in ((6, 2, "psum_v"), (7, 0, "psum_q"), (8, 1, "psum_k")):
                    for hf, t1 in pair:
                        if st == 6:
                            pe.wait_ge(S["h1"], t1)
                            pe.wait_ge(S["xnT1"], t1)
                        if st == 8:
                            pe.wait_ge(S["v"], t1)
                            pe.wait_ge(S["gl"], t1)
                        ps = slot(st, hf)
                        for b in range(2):
                            c0 = part * H0 * HD0 + b * 384
                            mm = over_width(ps[0:P, b * BANK:b * BANK + 384], xnT, hf,
                                            lambda c, k: w_moh[0:k, c, c0:c0 + 384])
                        if st == 6:
                            mm = over_width(ps[0:P, BANK + 384:BANK + 384 + RH + 4], xnT, hf,
                                            lambda c, k: w_gate[0:k, c, :], DH2)
                        mm.then_inc(S[name], 1)
                for st, n0, ready, name in ((9, 0, "qn", "psum_qT"), (10, 768, "kn", "psum_kT")):
                    for hf, t1 in pair:
                        pe.wait_ge(S[ready], t1)
                        ps = slot(st, hf)
                        transposes(lambda c: ps[:, (c // 3) * BANK + (c % 3) * P:(c // 3) * BANK + (c % 3) * P + P],
                                   qn[:, hf, n0:n0 + 768], 6, 128).then_inc(S[name], 1)

                def scores(ps, hf, g, rows, head_at, mask):
                    for b in range(2):
                        for j in range(3):
                            hd = head_at(g, b, j)
                            r0, col = rows * (hd % (128 // rows)), hd // (128 // rows) * P
                            pe.matmul(ps[0:P, b * BANK + j * P:b * BANK + j * P + P],
                                      qT[r0:r0 + rows, hf, col:col + P], kT[r0:r0 + rows, hf, col:col + P],
                                      start=j == 0, stop=False, skip_group_check=True)
                        mm = pe.matmul(ps[0:P, b * BANK:b * BANK + 3 * P], mask[r0:r0 + rows, 0:P],
                                       mask[r0:r0 + rows, P:4 * P], start=False, stop=True, skip_group_check=True)
                    return mm

                for st, g, name in ((11, 0, "psum_sa"), (12, 1, "psum_sb")):
                    for hf, t1 in pair:
                        if st == 11:
                            pe.wait_ge(S["qT"], t1)
                            pe.wait_ge(S["kT"], t1)
                        scores(slot(st, hf), hf, g, HD0, head0_at, mask0).then_inc(S[name], 1)
                for st, g, ready, free, name in ((13, 0, "ea", "suba", "psum_pTa"), (14, 1, "eb", "subb", "psum_pTb")):
                    for hf, t1 in pair:
                        pe.wait_ge(S[ready], t1)
                        ps = slot(st, hf)
                        transposes(lambda c: ps[0:P, (c // 3) * BANK + (c % 3) * P:(c // 3) * BANK + (c % 3) * P + P],
                                   pr[0:P, hf, g * HALF6:(g + 1) * HALF6], 6, P).then_inc(S[name], 1)
                for hf, t1 in pair:
                    pe.wait_ge(S["pTa"], t1)
                    pe.wait_ge(S["pTb"], t1)
                    ps = slot(15, hf)
                    for hd in range(H0):
                        c0 = (hd // 6) * BANK + (hd % 6) * (HD0 + 1)
                        mm = pe.matmul(ps[0:P, c0:c0 + HD0 + 1], pT[:, hf, place0[hd] * P:(place0[hd] + 1) * P],
                                       v_aug[:, hf, hd * (HD0 + 1):(hd + 1) * (HD0 + 1)], start=True, stop=True)
                    mm.then_inc(S["psum_pv"], 1)
                for hf, t1 in pair:
                    pe.wait_ge(S["o"], t1)
                    ps = slot(16, hf)
                    transposes(lambda c: ps[:, (c // 3) * BANK + (c % 3) * P:(c // 3) * BANK + (c % 3) * P + P],
                               o[:, hf, :], 6, 128).then_inc(S["psum_oT"], 1)
                for hf, t1 in pair:
                    pe.wait_ge(S["oT"], t1)
                    ps = slot(17, hf)
                    for c in range(6):
                        mm = pe.matmul(ps[0:P, 0:D], oT[:, hf, c * P:(c + 1) * P], w_proj[:, c, :],
                                       start=c == 0, stop=c == 5)
                    mm.then_inc(S["psum_proj"], 1)
                for hf, t1 in pair:
                    pe.wait_ge(S["xn2"], t1)
                    ps = slot(18, hf)
                    transposes(lambda c: ps[0:DH2, P * c:P * c + P], xn[:, hf, :], 2, DH2).then_inc(S["psum_xnT2"], 1)
                for hf, t1 in pair:
                    pe.wait_ge(S["xnT2"], t1)
                    over_width(slot(19, hf)[0:P, 0:2 * D], xnT, hf, lambda c, k: w_l1[0:k, c, :], DH2)\
                        .then_inc(S["psum_qkv1"], 1)
                for hf, t1 in pair:
                    pe.wait_ge(S["qk1"], t1)
                    ps = slot(20, hf)
                    transposes(lambda c: ps[:, (c // 3) * BANK + (c % 3) * P:(c // 3) * BANK + (c % 3) * P + P],
                               qk1[:, hf, :], 6, 128).then_inc(S["psum_qkT1"], 1)
                for st, g, name in ((21, 0, "psum_s1a"), (22, 1, "psum_s1b")):
                    for hf, t1 in pair:
                        if st == 21:
                            pe.wait_ge(S["q1T"], t1)
                        scores(slot(st, hf), hf, g, PAD1, head1_at, mask1).then_inc(S[name], 1)
                for st, g, ready, name in ((23, 0, "e1a", "psum_p1Ta"), (24, 1, "e1b", "psum_p1Tb")):
                    for hf, t1 in pair:
                        pe.wait_ge(S[ready], t1)
                        ps = slot(st, hf)
                        transposes(lambda c: ps[0:P, (c // 3) * BANK + (c % 3) * P:(c // 3) * BANK + (c % 3) * P + P],
                                   pr[0:P, hf, g * HALF6:(g + 1) * HALF6], 6, P).then_inc(S[name], 1)
                for hf, t1 in pair:
                    pe.wait_ge(S["v1"], t1)
                    pe.wait_ge(S["p1Ta"], t1)
                    pe.wait_ge(S["p1Tb"], t1)
                    ps = slot(25, hf)
                    for hd in range(H1):
                        w = HD1 + 1
                        mm = pe.matmul(ps[0:P, hd * w:(hd + 1) * w], pT[:, hf, place1[hd] * P:(place1[hd] + 1) * P],
                                       v1_aug[:, hf, hd * w:(hd + 1) * w], start=True, stop=True)
                    mm.then_inc(S["psum_pv1"], 1)
                for hf, t1 in pair:
                    pe.wait_ge(S["om"], t1)
                    ps = slot(26, hf)
                    transposes(lambda c: ps[0:DH2, P * c:P * c + P], om[:, hf, :], 2, DH2).then_inc(S["psum_omT"], 1)
                for hf, t1 in pair:
                    pe.wait_ge(S["omT"], t1)
                    over_width(slot(27, hf)[0:P, 0:2 * D], omT, hf, lambda c, k: w_out[0:k, c, :])\
                        .then_inc(S["psum_out"], 1)
                for hf, t1 in pair:
                    pe.wait_ge(S["xn3"], t1)
                    ps = slot(28, hf)
                    transposes(lambda c: ps[0:DH2, P * c:P * c + P], xn[:, hf, :], 2, DH2).then_inc(S["psum_xnT3"], 1)
                for hf, t1 in pair:
                    pe.wait_ge(S["xnT3"], t1 + 2)
                    over_width(slot(29, hf)[0:P, 0:E], xnT, hf, lambda c, k: w_rt[0:k, c, :], DH2)\
                        .then_inc(S["psum_rt"], 1)
            moe_tensor(pe)

        @block.scalar
        def _(act):
            act.wait_ge(s_w, 16 * len(loads))
            act.wait_ge(s_setup_v, 2)
            act.wait_ge(s_setup_p, 1)
            act.sem_inc(S["xnT3"], 2)

            def copy(dst, src, ready, t1, done):
                act.wait_ge(S[ready], t1)
                act.activation(dst, src, ACT.Copy).then_inc(S[done], 1)

            def expo(hf, g, ready, t1, done):
                act.wait_ge(S[ready], t1)
                act.activation(pr[0:P, hf, g * HALF6:(g + 1) * HALF6], sc[0:P, hf, g * HALF6:(g + 1) * HALF6],
                               ACT.Exp).then_inc(S[done], 1)

            with act.Fori(0, PAIRS) as i:
                pair = [(0, 2 * i + 1), (1, 2 * i + 2)]

                def xnT_copy(st, ready, done):
                    for hf, t1 in pair:
                        copy(xnT[0:DH2, hf, :], slot(st, hf)[0:DH2, 0:2 * P], ready, t1, done)

                xnT_copy(1, "psum_xnT0", "xnT0")
                for hf, t1 in pair:
                    copy(qkT0[:, hf, :], slot(2, hf)[0:DH2, 0:4 * P], "psum_qkv0", t1, "qkT0")
                xnT_copy(5, "psum_xnT1", "xnT1")
                for hf, t1 in pair:
                    copy(v_aug[:, hf, :].rearrange("p (b h d) -> p b h d", b=2, h=6)[:, :, :, 0:HD0],
                         banks(slot(6, hf), P, 384).rearrange("p b (h d) -> p b h d", h=6), "psum_v", t1, "v")
                for st, c0, ready, done in ((7, 0, "psum_q", "sqq"), (8, 768, "psum_k", "sqk")):
                    for hf, t1 in pair:
                        act.wait_ge(S[ready], t1)
                        act.activation(v3(sq[:, hf, c0:c0 + 768], 2), banks(slot(st, hf), P, 384),
                                       ACT.Square).then_inc(S[done], 1)
                act.wait_ge(S["gsub"], i + 1)
                act.activation(ge[:, :, :], gl[:, :, :], ACT.Exp).then_inc(S["gexp"], 1)
                for hf, t1 in pair:
                    act.wait_ge(S["psum_qT"], t1)
                    act.activation(v3(qT[:, hf, :], 2), banks(slot(9, hf), 128, 3 * P), ACT.Identity,
                                   bias=qk_affine[:, 1:2], scale=qk_affine[:, 0:1]).then_inc(S["qT"], 1)
                for g, ready, done in ((0, "suba", "ea"), (1, "subb", "eb")):
                    for hf, t1 in pair:
                        expo(hf, g, ready, t1, done)
                for st, g, ready, done in ((13, 0, "psum_pTa", "pTa"), (14, 1, "psum_pTb", "pTb")):
                    for hf, t1 in pair:
                        copy(v3(pT[:, hf, g * HALF6:(g + 1) * HALF6], 2), banks(slot(st, hf), P, 3 * P), ready, t1, done)
                for hf, t1 in pair:
                    copy(v3(oT[:, hf, :], 2), banks(slot(16, hf), 128, 3 * P), "psum_oT", t1, "oT")
                xnT_copy(18, "psum_xnT2", "xnT2")
                for hf, t1 in pair:
                    act.wait_ge(S["psum_qkT1"], t1)
                    act.activation(qT[:, hf, 0:3 * P], slot(20, hf)[:, 0:3 * P], ACT.Copy)
                    act.activation(kT[:, hf, 0:3 * P], slot(20, hf)[:, BANK:BANK + 3 * P], ACT.Copy).then_inc(S["q1T"], 1)
                for g, ready, done in ((0, "sub1a", "e1a"), (1, "sub1b", "e1b")):
                    for hf, t1 in pair:
                        expo(hf, g, ready, t1, done)
                for st, g, ready, done in ((23, 0, "psum_p1Ta", "p1Ta"), (24, 1, "psum_p1Tb", "p1Tb")):
                    for hf, t1 in pair:
                        copy(v3(pT[:, hf, g * HALF6:(g + 1) * HALF6], 2), banks(slot(st, hf), P, 3 * P), ready, t1, done)
                for hf, t1 in pair:
                    copy(omT[0:DH2, hf, :], slot(26, hf)[0:DH2, 0:2 * P], "psum_omT", t1, "omT")
                xnT_copy(28, "psum_xnT3", "xnT3")
            moe_scalar(act)

        @block.gpsimd
        def _(pool):
            pool.memset(zeros[:, :], 0.0).then_inc(s_zeros, 1)
            pool.memset(ones[:, :], 1.0)
            pool.memset(neg_half[:, :], -0.5)
            pool.memset(v_aug[:, :, :], 1.0)
            pool.memset(v1_aug[:, :, :], 1.0)
            pool.memset(qk1[:, :, :], 0.0).then_inc(s_setup_p, 1)
            pool.wait_ge(s_zeros, 1)
            flat = rows_dram.rearrange("(a p b) d -> a p (b d)", a=8, p=128)
            for k in range(8):
                pool.dma_start(flat[k], zeros[:, :]).then_inc(s_zero, 16)
            pool.wait_ge(s_w, 16 * len(loads))
            pool.wait_ge(s_setup_p, 1)

            def power(dst, src, n, ready, t1, done):
                pool.wait_ge(S[ready], t1)
                pool.tensor_tensor(dst, src, neg_half[:, 0:n], ALU.pow).then_inc(S[done], 1)

            pool.sem_inc(S["base"], 2)
            with pool.Fori(0, PAIRS) as i:
                pair = [(0, 2 * i + 1), (1, 2 * i + 2)]
                for hf, t1 in pair:
                    power(rstd[:, hf, :], mv[:, hf, 1:2], 1, "va0", t1, "rs0")
                for hf, t1 in pair:
                    power(rstd[:, hf, :], mv[:, hf, 1:2], 1, "va1", t1, "rs1")
                for hf, t1 in pair:
                    pool.wait_ge(S["h1"], t1)
                    pool.tensor_tensor(hb[:, hf, :], h[:, hf, :], b_proj[:, :], ALU.add).then_inc(S["hb"], 1)
                for hf, t1 in pair:
                    power(sr[:, hf, :], ss[:, hf, :], 24, "vss", t1, "srk")
                for hf, t1 in pair:
                    power(rstd[:, hf, :], mv[:, hf, 1:2], 1, "va2", t1, "rs2")
                for hf, t1 in pair:
                    pool.wait_ge(S["rope"], t1)
                    pool.tensor_tensor(qk1[:, hf, :].rearrange("p (n d) -> p n d", d=PAD1)[:, :, 0:HD1],
                                       ropa[:, hf, :].rearrange("p (n d) -> p n d", d=HD1),
                                       ropb[:, hf, :].rearrange("p (n d) -> p n d", d=HD1),
                                       ALU.add).then_inc(S["qk1"], 1)
                kv = [qk1[:, hf, :].rearrange("p (n d) -> p n d", d=PAD1)[:, H1:2 * H1, 0:HD1] for hf in range(2)]
                c3 = [v3(lc[:, hf, :], H1) for hf in range(2)]
                for hf, t1 in pair:
                    pool.wait_ge(S["lmean"], t1)
                    pool.tensor_tensor(c3[hf], kv[hf], lsum[:, hf, :].unsqueeze(2).broadcast_to([P, H1, HD1]),
                                       ALU.add).then_inc(S["lc"], 1)
                for hf, t1 in pair:
                    pool.wait_ge(S["lc"], t1)
                    pool.tensor_tensor(lsq[:, hf, :], lc[:, hf, :], lc[:, hf, :], ALU.mult).then_inc(S["lsq"], 1)
                for hf, t1 in pair:
                    power(lr[:, hf, :], lr[:, hf, :], H1, "lvar", t1, "lr")
                for hf, t1 in pair:
                    pool.wait_ge(S["lr"], t1)
                    pool.tensor_tensor(c3[hf], c3[hf], lr[:, hf, :].unsqueeze(2).broadcast_to([P, H1, HD1]),
                                       ALU.mult).then_inc(S["lv1"], 1)
                for hf, t1 in pair:
                    pool.wait_ge(S["lv1"], t1)
                    pool.tensor_tensor(c3[hf], c3[hf], ln_gb[:, 0:1, :].broadcast_to([P, H1, HD1]),
                                       ALU.mult).then_inc(S["lv2"], 1)
                for hf, t1 in pair:
                    pool.wait_ge(S["lv2"], t1)
                    pool.tensor_tensor(v1_aug[:, hf, :].rearrange("p (n d) -> p n d", d=HD1 + 1)[:, :, 0:HD1],
                                       c3[hf], ln_gb[:, 1:2, :].broadcast_to([P, H1, HD1]),
                                       ALU.add).then_inc(S["v1"], 1)
                for hf, t1 in pair:
                    power(rstd[:, hf, :], mv[:, hf, 1:2], 1, "va3", t1, "rs3")
                for hf, t1 in pair:
                    pool.wait_ge(S["xn3"], t1)
                    pool.tensor_copy(xn_all[:, bass.ds(2 * i + hf, 1), :], xn[:, hf:hf + 1, :]).then_inc(S["xn_kept"], 1)
                    pool.tensor_tensor(base_all[:, bass.ds(2 * i + hf, 1), :], xn[:, hf:hf + 1, :],
                                       h[:, hf:hf + 1, :], ALU.add).then_inc(S["base"], 1)
            moe_gpsimd(pool)

        @block.vector
        def _(dve):
            for rows in (xnT, omT, xeT):
                dve.memset(rows[DH2:DH2 + 1, :, :], 1.0)
            dve.wait_ge(s_w, 16 * len(loads))
            dve.tensor_copy(mask0[:, :], mask0f[:, :])
            dve.tensor_copy(mask1[:, :], mask1f[:, :])
            dve.tensor_scalar(qk_affine[:, 0:2], qk_affine[:, 0:2], HD0 ** -0.5, None, ALU.mult)
            wq = [w_moh[0:DH2 + 1 - c, c, 0:1536].rearrange("p (n d) -> p n d", d=HD0) for c in range(2)]
            for c in range(2):
                dve.tensor_reduce(wmean[0:DH2 + 1 - c, c, :], wq[c], AX.X, ALU.add).then_inc(s_center, 1)
            dve.wait_ge(s_center, 2)
            for c in range(2):
                m = wmean[0:DH2 + 1 - c, c, :]
                dve.tensor_scalar(m, m, -1.0 / HD0, None, ALU.mult).then_inc(s_center, 1)
            dve.wait_ge(s_center, 4)
            for c in range(2):
                n = DH2 + 1 - c
                dve.tensor_tensor(wq[c], wq[c], wmean[0:n, c, :].unsqueeze(2).broadcast_to([n, 24, HD0]), ALU.add)\
                    .then_inc(s_setup_v, 1)
            dve.sem_inc(S["rlg"], 2)

            def norm(pair, k):
                for hf, t1 in pair:
                    dve.wait_ge(S[f"h{k}"], t1)
                    dve.bn_stats(stats[:, hf, :], h[:, hf, :]).then_inc(S[f"st{k}"], 1)
                for hf, t1 in pair:
                    wait_apart(dve, S[f"st{k}"], t1)
                    dve.bn_aggr(mv[:, hf, :], stats[:, hf, :]).then_inc(S[f"ag{k}"], 1)
                for hf, t1 in pair:
                    dve.wait_ge(S[f"ag{k}"], t1)
                    dve.tensor_scalar(mv[:, hf, 1:2], mv[:, hf, 1:2], EPS, None, ALU.add).then_inc(S[f"va{k}"], 1)
                for hf, t1 in pair:
                    dve.wait_ge(S[f"rs{k}"], t1)
                    dve.tensor_scalar(xn[:, hf, :], h[:, hf, :], mv[:, hf, 0:1], rstd[:, hf, 0:1],
                                      ALU.subtract, ALU.mult).then_inc(S[f"xn{k}"], 1)

            def softmax_in(pair, st, g, ready, nm, done):
                for hf, t1 in pair:
                    dve.wait_ge(S[ready], t1)
                    dve.tensor_reduce(v3(nmax[:, hf, 6 * g:6 * g + 6], 2),
                                      banks(slot(st, hf), P, 3 * P).rearrange("p b (h k) -> p b h k", h=3),
                                      AX.X, ALU.max, negate=True).then_inc(S[nm], 1)
                for hf, t1 in pair:
                    dve.wait_ge(S[nm], t1)
                    for b in range(2):
                        c0 = g * HALF6 + b * 3 * P
                        mm = dve.tensor_tensor(v3(sc[0:P, hf, c0:c0 + 3 * P], 3), v3(slot(st, hf)[0:P, b * BANK:b * BANK + 3 * P], 3),
                                          nmax[:, hf, 6 * g + 3 * b:6 * g + 3 * b + 3].unsqueeze(2).broadcast_to([P, 3, P]),
                                          ALU.add)
                    mm.then_inc(S[done], 1)

            with dve.Fori(0, PAIRS) as i:
                pair = [(0, 2 * i + 1), (1, 2 * i + 2)]
                i1 = i + 1
                for hf, t1 in pair:
                    dve.wait_ge(S["psum_tok"], t1)
                    dve.wait_ge(S["base"], t1)
                    dve.tensor_tensor(h[:, hf, :], slot(0, hf)[0:P, 0:D], b_tok[:, :], ALU.add).then_inc(S["h0"], 1)
                norm(pair, 0)
                for hf, t1 in pair:
                    dve.wait_ge(S["psum_qkv0"], t1)
                    dve.tensor_copy(v0[:, hf, :], slot(2, hf)[0:P, BANK:BANK + D]).then_inc(S["v0"], 1)
                for hf, t1 in pair:
                    dve.wait_ge(S["psum_s0"], t1)
                    dve.tensor_tensor(pT0[:, hf, :], slot(3, hf)[0:P, 0:P], retT[:, :], ALU.mult).then_inc(S["pT0"], 1)
                for hf, t1 in pair:
                    dve.wait_ge(S["psum_o0"], t1)
                    dve.tensor_tensor(h[:, hf, :], slot(4, hf)[0:P, 0:D], h[:, hf, :], ALU.add).then_inc(S["h1"], 1)
                norm(pair, 1)

                for hf, t1 in pair:
                    dve.wait_ge(S["v"], t1)
                    dve.tensor_copy(gl[:, hf, :], slot(6, hf)[0:P, BANK + 384:BANK + 384 + RH + 4]).then_inc(S["gl"], 1)
                wait_apart(dve, S["gl"], 2 * i + 2)
                for hf in range(2):
                    dve.max(gmx[:, hf, :], gl[:, hf, 0:RH])
                pairs2 = gl[:, :, RH:RH + 4].rearrange("p a (b c) -> p a b c", b=2)
                dve.tensor_reduce(v3(gm2[:, :], 2), pairs2, AX.X, ALU.max).then_inc(S["gpick"], 1)
                wait_apart(dve, S["gpick"], 2 * i + 1)
                for hf in range(2):
                    m = dve.max_index(gidx[:, hf, :], gmx[:, hf, :], gl[:, hf, 0:RH])
                m.then_inc(S["gpick"], 1)
                dve.wait_ge(S["gpick"], 2 * i + 2)
                dve.tensor_copy(gidf[:, :, :], gidx[:, :, 0:2])
                dve.tensor_tensor(gl[:, :, 0:RH], gl[:, :, 0:RH], gmx[:, :, 0:1].broadcast_to([P, 2, RH]), ALU.subtract)
                dve.tensor_tensor(pairs2, pairs2, v3(gm2[:, :], 2).unsqueeze(3).broadcast_to([P, 2, 2, 2]),
                                  ALU.subtract).then_inc(S["gsub"], 1)

                for st, c0, ready in ((7, 0, "sqq"), (8, 12, "sqk")):
                    for hf, t1 in pair:
                        dve.wait_ge(S[ready], t1)
                        dve.tensor_reduce(ss[:, hf, c0:c0 + 12], v3(sq[:, hf, c0 * 64:c0 * 64 + 768], 12),
                                          AX.X, ALU.add).then_inc(S["ssk"], 1)
                for hf, t1 in pair:
                    dve.wait_ge(S["ssk"], 4 * i + 4)
                    dve.tensor_scalar(ss[:, hf, :], ss[:, hf, :], 1.0 / HD0, EPS, ALU.mult, ALU.add).then_inc(S["vss"], 1)
                for st, c0, done in ((7, 0, "qn"), (8, 12, "kn")):
                    for hf, t1 in pair:
                        dve.wait_ge(S["srk"], t1)
                        for b in range(2):
                            n0 = c0 + 6 * b
                            mm = dve.tensor_tensor(v3(qn[:, hf, n0 * 64:n0 * 64 + 384], 6),
                                                   v3(slot(st, hf)[0:P, b * BANK:b * BANK + 384], 6),
                                                   sr[:, hf, n0:n0 + 6].unsqueeze(2).broadcast_to([P, 6, HD0]), ALU.mult)
                        mm.then_inc(S[done], 1)

                GS = 8

                def gate_step(ins, n):
                    ins.then_inc(S["gstep"], 1)
                    dve.wait_ge(S["gstep"], GS * i + n)

                dve.wait_ge(S["gexp"], i1)
                g2 = ge[:, :, RH:RH + 4].rearrange("p a (b c) -> p a b c", b=2)
                dve.tensor_reduce(gsum[:, :, 0:1], ge[:, :, 0:RH], AX.X, ALU.add)
                dve.tensor_reduce(gsum[:, :, 1:3], g2, AX.X, ALU.add)
                for hf in range(2):
                    m = dve.tensor_scalar(gmask[:, hf, :], small[:, 0:RH], gidf[:, hf, 1:2], None, ALU.is_equal)
                gate_step(m, 1)
                dve.reciprocal(gsum[:, :, 0:3], gsum[:, :, 0:3])
                for hf in range(2):
                    m = dve.scalar_tensor_tensor(gmask[:, hf, :], small[:, 0:RH], gidf[:, hf, 0:1], gmask[:, hf, :],
                                                 ALU.is_equal, ALU.add)
                gate_step(m, 2)
                for hf in range(2):
                    dve.scalar_tensor_tensor(gmask[:, hf, :], ge[:, hf, 0:RH], gsum[:, hf, 0:1], gmask[:, hf, :],
                                             ALU.mult, ALU.mult)
                gate_step(dve.tensor_tensor(g2, g2, gsum[:, :, 1:3].unsqueeze(3).broadcast_to([P, 2, 2, 2]), ALU.mult), 3)
                dve.tensor_reduce(gden[:, :, 0:1], gmask[:, :, :], AX.X, ALU.add)
                gate_step(dve.tensor_tensor(gates[:, :, 0:SH], ge[:, :, RH + 2:RH + 4],
                                            ge[:, :, RH:RH + 1].broadcast_to([P, 2, SH]), ALU.mult), 4)
                gate_step(dve.tensor_scalar(gden[:, :, 0:1], gden[:, :, 0:1], float(np.finfo(np.float32).eps), None,
                                            ALU.max), 5)
                gate_step(dve.reciprocal(gden[:, :, 0:1], gden[:, :, 0:1]), 6)
                gate_step(dve.tensor_tensor(gden[:, :, 1:2], gden[:, :, 0:1], ge[:, :, RH + 1:RH + 2], ALU.mult), 7)
                gate_step(dve.tensor_tensor(gates[:, :, SH:H0], gmask[:, :, :], gden[:, :, 1:2].broadcast_to([P, 2, RH]),
                                            ALU.mult), 8)
                dve.tensor_scalar(gates[:, :, :], gates[:, :, :], 4.0, None, ALU.mult).then_inc(S["gates"], 1)

                for hf, t1 in pair:
                    dve.wait_ge(S["psum_kT"], t1)
                    dve.tensor_scalar(v3(kT[:, hf, :], 2), banks(slot(10, hf), 128, 3 * P),
                                      qk_affine[:, 2:3], qk_affine[:, 3:4], ALU.mult, ALU.add).then_inc(S["kT"], 1)
                softmax_in(pair, 11, 0, "psum_sa", "nma", "suba")
                softmax_in(pair, 12, 1, "psum_sb", "nmb", "subb")

                for hf, t1 in pair:
                    dve.wait_ge(S["psum_pv"], t1)
                    dve.reciprocal(v3(fac[:, hf, :], 2),
                                   banks(slot(15, hf), P, 390).rearrange("p b (h d) -> p b h d", h=6)[:, :, :, HD0])\
                        .then_inc(S["fac0"], 1)
                dve.wait_ge(S["gates"], i1)
                for hf, t1 in pair:
                    dve.wait_ge(S["fac0"], t1)
                    dve.tensor_tensor(fac[:, hf, :], fac[:, hf, :], gates[:, hf, :], ALU.mult).then_inc(S["fac"], 1)
                for hf, t1 in pair:
                    dve.wait_ge(S["fac"], t1)
                    for b in range(2):
                        mm = dve.tensor_tensor(v3(o[:, hf, 384 * b:384 * b + 384], 6),
                                               v3(slot(15, hf)[0:P, BANK * b:BANK * b + 390], 6)[:, :, 0:HD0],
                                               fac[:, hf, 6 * b:6 * b + 6].unsqueeze(2).broadcast_to([P, 6, HD0]), ALU.mult)
                    mm.then_inc(S["o"], 1)
                for hf, t1 in pair:
                    dve.wait_ge(S["psum_proj"], t1)
                    dve.wait_ge(S["hb"], t1)
                    dve.tensor_tensor(h[:, hf, :], slot(17, hf)[0:P, 0:D], hb[:, hf, :], ALU.add).then_inc(S["h2"], 1)
                norm(pair, 2)

                for hf, t1 in pair:
                    dve.wait_ge(S["psum_qkv1"], t1)
                    ps = slot(19, hf)[0:P, 0:2 * D]
                    dve.tensor_tensor(ropa[:, hf, :], ps, rope[:, 0:2 * D], ALU.mult)
                    for b in range(2):
                        def halves(x, k):
                            return x.rearrange("p (n b d) -> p n b d", b=2, d=HD1 // 2)[:, :, k, :]
                        mm = dve.tensor_tensor(halves(ropb[:, hf, :], b), halves(ps, 1 - b),
                                               halves(rope[:, 2 * D:4 * D], b), ALU.mult)
                    mm.then_inc(S["rope"], 1)
                kv = [qk1[:, hf, :].rearrange("p (n d) -> p n d", d=PAD1)[:, H1:2 * H1, 0:HD1] for hf in range(2)]
                for hf, t1 in pair:
                    dve.wait_ge(S["qk1"], t1)
                    dve.tensor_reduce(lsum[:, hf, :], kv[hf], AX.X, ALU.add).then_inc(S["lsum"], 1)
                for hf, t1 in pair:
                    dve.wait_ge(S["lsum"], t1)
                    dve.tensor_scalar(lsum[:, hf, :], lsum[:, hf, :], -1.0 / HD1, None, ALU.mult).then_inc(S["lmean"], 1)
                for hf, t1 in pair:
                    dve.wait_ge(S["lsq"], t1)
                    dve.tensor_reduce(lr[:, hf, :], v3(lsq[:, hf, :], H1), AX.X, ALU.add).then_inc(S["lss"], 1)
                for hf, t1 in pair:
                    dve.wait_ge(S["lss"], t1)
                    dve.tensor_scalar(lr[:, hf, :], lr[:, hf, :], 1.0 / HD1, EPS, ALU.mult, ALU.add).then_inc(S["lvar"], 1)
                softmax_in(pair, 21, 0, "psum_s1a", "nm1a", "sub1a")
                softmax_in(pair, 22, 1, "psum_s1b", "nm1b", "sub1b")
                for hf, t1 in pair:
                    dve.wait_ge(S["psum_pv1"], t1)
                    dve.reciprocal(fac[:, hf, :], v3(slot(25, hf)[0:P, 0:H1 * (HD1 + 1)], H1)[:, :, HD1])\
                        .then_inc(S["rden"], 1)
                for hf, t1 in pair:
                    dve.wait_ge(S["rden"], t1)
                    dve.tensor_tensor(v3(om[:, hf, :], H1), v3(slot(25, hf)[0:P, 0:H1 * (HD1 + 1)], H1)[:, :, 0:HD1],
                                      fac[:, hf, :].unsqueeze(2).broadcast_to([P, H1, HD1]), ALU.mult).then_inc(S["om"], 1)
                for k, done in ((0, "h3a"), (1, "h3")):
                    for hf, t1 in pair:
                        if k == 0:
                            dve.wait_ge(S["psum_out"], t1)
                        else:
                            dve.wait_ge(S["h3a"], t1)
                        dve.scalar_tensor_tensor(h[:, hf, :], slot(27, hf)[0:P, D * k:D * k + D], small[:, 16 + k:17 + k],
                                                 h[:, hf, :], ALU.mult, ALU.add).then_inc(S[done], 1)
                norm(pair, 3)
                for hf, t1 in pair:
                    wait_apart(dve, S["psum_rt"], t1)
                    dve.max(rmx[:, hf, :], slot(29, hf)[0:P, 0:E]).then_inc(S["rtop"], 1)
                for hf, t1 in pair:
                    wait_apart(dve, S["rtop"], t1)
                    dve.max_index(ridx[:, hf, :], rmx[:, hf, :], slot(29, hf)[0:P, 0:E]).then_inc(S["ridx"], 1)
                for hf, t1 in pair:
                    dve.wait_ge(S["ridx"], t1)
                    dve.tensor_copy(id_all[:, bass.ds(2 * i + hf, 1), :], ridx[:, hf:hf + 1, 0:2])
                    dve.tensor_copy(lg_all[:, bass.ds(2 * i + hf, 1), :], slot(29, hf)[0:P, 0:E].unsqueeze(1)).then_inc(S["rlg"], 1)
            moe_vector(dve)


def kernel(**inputs):
    import concourse.bacc as bacc
    from concourse.bass_utils import run_bass_kernel_spmd

    g = {k: np.asarray(v) for k, v in inputs.items()}

    def wide(w):
        return w.reshape(2, DH2, -1).transpose(1, 0, 2)

    x = g["x"].reshape(BATCH, GRID, PATCH, GRID, PATCH * 3).transpose(0, 1, 3, 2, 4).reshape(TILES, P, PC, 128)
    arrays = {
        "x": x.transpose(0, 3, 2, 1).reshape(TILES, 128, PC * P),
        "w_tok": g["L0_tok_W"].reshape(PC, 128, D).transpose(1, 0, 2), "b_tok": g["L0_tok_b"],
        "w_ret": wide(g["L0_attn_W_qkv"]), "b_ret": g["L0_attn_b_qkv"].reshape(1, -1),
        "w_moh": wide(g["L0_ffn_qkv_w"]), "b_moh": g["L0_ffn_qkv_b"].reshape(1, -1),
        "w_gr": wide(g["L0_ffn_wg_w"]), "w_g0": wide(g["L0_ffn_wg0_w"]), "w_g1": wide(g["L0_ffn_wg1_w"]),
        "w_proj": g["L0_ffn_proj_w"].reshape(H0 // 2, 128, D).transpose(1, 0, 2), "b_proj": g["L0_ffn_proj_b"],
        "qw": g["L0_ffn_q_norm_w"].reshape(-1, 1), "qb": g["L0_ffn_q_norm_b"].reshape(-1, 1),
        "kw": g["L0_ffn_k_norm_w"].reshape(-1, 1), "kb": g["L0_ffn_k_norm_b"].reshape(-1, 1),
        "w_q1": wide(g["L1_attn_Wq"]), "w_kv1": wide(g["L1_attn_Wkv"]),
        "w_octx": wide(g["L1_attn_Wo_ctx"]), "w_olat": wide(g["L1_attn_Wo_lat"]),
        "b_octx": g["L1_attn_bo_ctx"].reshape(1, -1), "b_olat": g["L1_attn_bo_lat"].reshape(1, -1),
        "ln_g": g["L1_attn_ln_g"], "ln_b": g["L1_attn_ln_b"], "w_rt": wide(g["L1_ffn_Wr"].T),
        "w1": g["L1_ffn_W1"].reshape(E, 2, DH2, FF).transpose(0, 2, 1, 3).reshape(E, DH2, 2 * FF),
        "b1": g["L1_ffn_b1"].reshape(E, 1, FF),
        "w2": g["L1_ffn_W2"].reshape(E, FC, 128, D).transpose(0, 2, 1, 3).reshape(E, 128, FC * D),
        "b2": g["L1_ffn_b2"].reshape(E, 1, D),
    }
    arrays.update(constants())
    arrays = {f"in_{k}": np.ascontiguousarray(v) for k, v in arrays.items()}
    nc = bacc.Bacc("TRN2", target_bir_lowering=False, num_devices=1)
    aps = {k[3:]: nc.dram_tensor(k, v.shape, mybir.dt.from_np(v.dtype), kind="ExternalInput").ap()
           for k, v in arrays.items()}
    out = nc.dram_tensor("out", (BATCH, N_TOK, D), mybir.dt.float32, kind="ExternalOutput").ap()
    vit_tower(nc, aps, out)
    return run_bass_kernel_spmd(nc, [arrays], core_ids=[0]).results[0]["out"]
```

```python
from contextlib import ExitStack

import numpy as np

import concourse.bass as bass
from concourse import mybir

BATCH, PATCH, GRID = 32, 16, 7
N_TOK = GRID * GRID
D = 192
DH2 = D // 2
PD = PATCH * PATCH * 3
PC = PD // 128
P = 2 * N_TOK
TILES = BATCH // 2
PAIRS = TILES // 2
H0, HD0 = 12, 64
RH, SH = 10, 2
H1, HD1, PAD1 = 12, 16, 32
LATENT = 32
CTX = N_TOK - LATENT
E, FF, FC = 16, 768, 6
EPS = 1e-5
HALF6 = 6 * P
BANK = 512
BIG = -1e30
RSQ = 12

ET = 128
ETILES = (2 * BATCH * N_TOK - E) // ET + E
ETILES += -ETILES % 4
TOKENS = BATCH * N_TOK
ROW = D + 2
MAXT = -(-BATCH * N_TOK // ET)


def constants():
    f = np.float32
    r = np.arange(P)
    n, img = r % N_TOK, r // N_TOK
    diff = (n[:, None] - n[None, :]).astype(f)
    ok = (img[:, None] == img[None, :]) & (diff >= 0)
    decay = np.where(ok, f(0.99) ** np.where(ok, diff, 0).astype(f), f(0)).astype(f)
    retT = np.ascontiguousarray((decay / np.sqrt(f(D))).T.astype(f))
    inv = (1.0 / 10000.0 ** (np.arange(0, HD1, 2, dtype=f) / f(HD1))).astype(f)
    ang = n.astype(f)[:, None] * inv[None, :]
    ang = np.concatenate([ang, ang], -1)
    cos, sin = np.cos(ang).astype(f), np.sin(ang).astype(f)
    sin[:, :HD1 // 2] *= -1
    q = f(HD1 ** -0.5)
    rope = np.stack([np.concatenate([np.tile(cos * q, (1, H1)), np.tile(cos, (1, H1))], 1),
                     np.concatenate([np.tile(sin * q, (1, H1)), np.tile(sin, (1, H1))], 1)], 1)
    imgq = np.stack([img == 0, img == 1]).astype(f)
    imgk = np.stack([img == 1, img == 0]).astype(f) * f(BIG)
    ctx = n < CTX
    grpq = np.stack([(img == i) & (ctx == c) for i in (0, 1) for c in (True, False)]).astype(f)
    grpk = np.stack([(img != i) | (c & ~ctx) for i in (0, 1) for c in (True, False)]).astype(f) * f(BIG)
    m0, m1 = np.zeros((128, 4 * P), f), np.zeros((128, 4 * P), f)
    for r0 in range(0, 128, HD0):
        m0[r0:r0 + 2] = np.concatenate([imgq] + [imgk] * 3, 1)
    for r0 in range(0, 128, PAD1):
        m1[r0:r0 + 4] = np.concatenate([grpq] + [grpk] * 3, 1)
    small = np.zeros((P, 18 + ETILES + MAXT + TILES), f)
    small[:, :16] = np.arange(16)
    small[:, 16] = ctx
    small[:, 17] = ~ctx
    small[:, 18:18 + ETILES] = np.arange(ETILES)
    small[:, 18 + ETILES:18 + ETILES + MAXT] = np.arange(MAXT) * ET
    small[:, 18 + ETILES + MAXT:] = np.arange(TILES) * P + r[:, None]
    return {"ident": np.eye(128, dtype=f), "retT": retT, "rope": rope.reshape(P, -1).astype(f),
            "mask0": m0.astype(f), "mask1": m1.astype(f), "small": small,
            "before": (r[:, None] < r[None, :]).astype(f),
            "pad_row": (TOKENS + np.arange(ET, dtype=f))[:, None]}


def vit_tower(nc, a, out):
    F32, I32, U32, BF16 = mybir.dt.float32, mybir.dt.int32, mybir.dt.uint32, mybir.dt.bfloat16
    ALU, ACT, AX = mybir.AluOpType, mybir.ActivationFunctionType, mybir.AxisListType
    ctx = ExitStack()
    with ctx:
        def sb(name, shape, dt=F32):
            return ctx.enter_context(nc.sbuf_tensor(name, shape, dt))

        def sem(name):
            return ctx.enter_context(nc.semaphore(name))

        rows_dram = nc.dram_tensor("expert_rows", [ETILES * ET, ROW], F32, kind="Internal").ap()

        ident = sb("ident", [128, 128])
        retT = sb("retT", [P, P])
        rope = sb("rope", [P, 4 * D])
        mask0f, mask0 = sb("mask0f", [128, 4 * P]), sb("mask0", [128, 4 * P], BF16)
        mask1f, mask1 = sb("mask1f", [128, 4 * P]), sb("mask1", [128, 4 * P], BF16)
        small = sb("small", [P, 18 + ETILES + MAXT + TILES])
        pad_row = sb("pad_row", [ET, 1])
        before = sb("before", [P, P])
        w_tok = sb("w_tok", [128, PC, D])
        b_tok = sb("b_tok", [P, D])
        w_ret = sb("w_ret", [DH2 + 1, 2, 3 * D])
        w_moh = sb("w_moh", [DH2 + 1, 2, 3 * H0 * HD0])
        w_gate = sb("w_gate", [DH2, 2, RH + 4])
        w_proj = sb("w_proj", [128, H0 // 2, D])
        b_proj = sb("b_proj", [P, D])
        qk_affine = sb("qk_affine", [128, 4])
        w_l1 = sb("w_l1", [DH2, 2, 2 * D])
        w_out = sb("w_out", [DH2 + 1, 2, 2 * D])
        ln_gb = sb("ln_gb", [P, 2, HD1])
        w_rt = sb("w_rt", [DH2, 2, E])
        ones = sb("ones", [P, P])
        neg_half = sb("neg_half", [P, 24])
        wmean = sb("wmean", [DH2 + 1, 2, 24])
        blank = sb("blank", [ET, 4, ROW])

        x_in = sb("x_in", [128, 2, PC * P])
        hb = sb("hb", [P, 2, D])
        xn = [sb(f"xn{k}", [P, 2, D]) for k in range(4)]
        stats = sb("stats", [P, 2, 6])
        mv = [sb(f"mv{k}", [P, 2, 2]) for k in range(4)]
        rstd = [sb(f"rstd{k}", [P, 2, 1]) for k in range(4)]
        xnT = [sb(f"xnT{k}", [DH2 + 1, 2, 2 * P]) for k in range(3)]
        xnT += [xnT[2]]
        qkT0 = sb("qkT0", [DH2, 2, 4 * P])
        v0 = sb("v0", [P, 2, D])
        pT0 = sb("pT0", [P, 2, P])
        ss = sb("ss", [P, 2, 24])
        rs = sb("rs", [P, 3, 24])
        rs_bits = sb("rs_bits", [P, 24], I32)
        qn = sb("qn", [P, 2, 1536])
        qT = sb("qT", [128, 2, 6 * P])
        kT = sb("kT", [128, 2, 6 * P])
        v_aug = sb("v_aug", [P, 2, H0 * (HD0 + 1)])
        nmax = sb("nmax", [P, 2, H0])
        pr = sb("pr", [128, 2, H0 * P])
        pT = sb("pT", [P, 2, H0 * P])
        sqq, sqk = pr[0:P, :, 0:768], pT[:, :, 0:768]
        fac = sb("fac", [P, 2, H0])
        o = sb("o", [P, 2, H0 * HD0])
        oT = qT
        qk1 = sb("qk1", [P, 2, 2 * H1 * PAD1])
        qT1 = sb("qT1", [128, 2, 3 * P])
        kT1 = sb("kT1", [128, 2, 3 * P])
        lsum = sb("lsum", [P, 2, H1])
        lc = sb("lc", [P, 2, D])
        lsq = sb("lsq", [P, 2, D])
        lr = sb("lr", [P, 2, H1])
        v1_aug = sb("v1_aug", [P, 2, H1 * (HD1 + 1)])
        nmax1 = sb("nmax1", [P, 2, H0])
        pr1 = sb("pr1", [128, 2, H1 * P])
        pT1 = sb("pT1", [P, 2, H1 * P])
        ropa, ropb = pr1[0:P, :, 0:2 * D], pr1[0:P, :, 2 * D:4 * D]
        fac1 = sb("fac1", [P, 2, H1])
        om = sb("om", [P, 2, D])
        omT = sb("omT", [DH2 + 1, 2, 2 * P])
        gl = sb("gl", [P, 2, RH + 4])
        gmx = sb("gmx", [P, 2, 8])
        gidx = sb("gidx", [P, 2, 8], U32)
        gidf = sb("gidf", [P, 2, 2])
        gm2 = sb("gm2", [P, 4])
        gsum = sb("gsum", [P, 2, 4])
        ge = sb("ge", [P, 2, RH + 4])
        gmask = sb("gmask", [P, 2, RH])
        gden = sb("gden", [P, 2, 2])
        gates = sb("gates", [P, 2, H0])
        rmx = sb("rmx", [P, 2, 8])
        ridx = sb("ridx", [P, 2, 8], U32)

        TE = TILES * E
        pT_flat, o_flat = pT[:, :, :].rearrange("p a b -> p (a b)"), o[:, :, :].rearrange("p a b -> p (a b)")
        oh = pT_flat[:, 0:2 * TE].rearrange("p (a b) -> p a b", a=2)
        both = pT_flat[:, 2 * TE:3 * TE]
        cnt = pT_flat[:, 3 * TE:4 * TE]
        cum = pT_flat[:, 4 * TE:6 * TE].rearrange("p (a b) -> p a b", a=2)
        prod = pT_flat[:, 6 * TE:8 * TE].rearrange("p (a b) -> p a b", a=2)
        cmp = o_flat[:, 0:E * max(MAXT, ETILES)]
        tmax = sb("tmax", [P, TILES])
        tcum = sb("tcum", [P, 3, E])
        slot_f = sb("slot_f", [P, 2, TILES])
        slot_u = sb("slot_u", [P, 2, TILES], U32)
        gate_k = sb("gate_k", [P, 2, TILES])
        eid_f = sb("eid_f", [1, ETILES])
        eid = sb("eid", [1, ETILES], I32)
        xe = sb("xe", [ET, 4, ROW])
        xeT = sb("xeT", [DH2 + 1, 4, 2 * ET])
        b2 = sb("b2", [ET, 4, D])
        w1 = [w_moh[:, :, :].rearrange("p a b -> p (a b)")[:, 2 * FF * k:2 * FF * (k + 1)] for k in range(3)] + \
             [pT1[:, :, :].rearrange("p a b -> p (a b)")[0:DH2 + 1, 0:2 * FF]]
        pr2, spare = pr1[:, :, :].rearrange("p a b -> p (a b)"), FC * D
        w2 = [pr2[:, 0:spare], pr2[:, spare:2 * spare],
              x_in[:, :, :].rearrange("p a b -> p (a b)")[:, 0:spare], qT[:, :, :].rearrange("p a b -> p (a b)")[:, 0:spare]]
        hT = pr
        ye = sb("ye", [ET, 2, D])
        yb = sb("yb", [ET, 2, D])
        token = sb("token", [ET, 2, 1], U32)

        xn_all = sb("xn_all", [P, TILES, ROW])
        h_all = sb("h_all", [P, TILES, D])
        lg_all = sb("lg_all", [P, TILES, E])
        id_all = sb("id_all", [P, TILES, 2])

        PS = [ctx.enter_context(nc.psum_tensor(f"slot{i}", [128, 2 * BANK], F32)) for i in range(4)]

        s_w, s_center = sem("constants_loaded"), sem("weight_centering")
        s_setup_p, s_setup_v = sem("pool_setup"), sem("vector_setup")
        s_apart = sem("waits_apart")
        s_zero, s_zeros = sem("expert_rows_zeroed"), sem("zeros_ready")
        s_x = [sem(f"patches_loaded{i}") for i in range(2)]
        names = ("psum_tok psum_xnT0 psum_qkv0 psum_s0 psum_o0 psum_xnT1 psum_v psum_q psum_k psum_qT psum_kT "
                 "psum_sa psum_sb psum_pTa psum_pTb psum_pv psum_oT psum_proj psum_xnT2 psum_qkv1 psum_qkT1 "
                 "psum_s1a psum_s1b psum_p1Ta psum_p1Tb psum_pv1 psum_omT psum_out psum_xnT3 psum_rt "
                 "h0 stat0 va0 rs0 xn0 xnT0 qkT0 v0 pT0 "
                 "h1 stat1 va1 rs1 xn1 xnT1 hb v sqq sqk gl gpick gsub gexp gstep gates "
                 "ssq qvar rsq ssk rsk qn kn qT kT nma suba ea nmb subb eb pTa pTb fac0 fac o oT h2 stat2 va2 rs2 xn2 xnT2 "
                 "rope qk1 lsum lsum2 lmean lc lsq lrsq lv1 lv2 v1 q1T nm1a sub1a e1a nm1b sub1b e1b "
                 "p1Ta p1Tb rden om omT h3a h3 stat3 va3 rs3 xn3 base xnT3 rtop rlg ridx").split()
        S = {n: sem(n) for n in names}

        def wait_apart(eng, sm, value):
            eng.wait_ge(sm, value)
            eng.sem_inc(s_apart, 1)

        def v3(ap, k):
            return ap.rearrange("p (a b) -> p a b", a=k)

        def banks(ps, n, used):
            return ps[0:n, :].rearrange("p (b c) -> p b c", b=2)[:, :, 0:used]


        s_route, s_eid = sem("routing_step"), sem("expert_of_tile_ready")
        s_both, s_rank, s_rexp, s_rsub = sem("choices_ready"), sem("psum_ranks"), sem("router_exp"), sem("router_logits_less_max")
        s_slots = sem("slots_ready")
        s_scat = sem("rows_scattered")
        s_rows = [sem(f"expert_rows_loaded{i}") for i in range(4)]
        s_wts = [sem(f"expert_weights_loaded{i}") for i in range(4)]
        s_base, s_tok, s_yb = sem("output_base_stored"), sem("token_numbers_ready"), sem("biased_result_ready")
        s_xeT, s_xe, s_up, s_hT = sem("psum_xeT"), sem("xeT_ready"), sem("psum_hidden"), sem("hidden_ready")
        s_dn, s_y = sem("psum_expert_out"), sem("expert_out_ready")
        s_yfree, s_add, s_gate = sem("result_buffer_free"), sem("results_added"), sem("gates_in_rows")

        def moe_sync(sp):
            out_rows = out[0:TOKENS, :].rearrange("(t p) d -> p t d", p=P)
            sp.wait_ge(S["base"], TILES)
            sp.dma_start(out_rows, h_all[:, :, :]).then_inc(s_base, 16)

            def weights(j, b):
                e = sp.value_load(eid[0:1, bass.ds(j, 1)], min_val=0, max_val=E - 1)
                for dst, src in ((w1[b][0:DH2, :], a["w1"]), (w1[b][DH2:DH2 + 1, 0:FF], a["b1"]), (w2[b], a["w2"])):
                    sp.dma_start(dst, src[bass.ds(e, 1)].rearrange("o p c -> (o p) c")).then_inc(s_wts[b], 16)
                sp.dma_start(b2[:, b, :], a["b2"][bass.ds(e, 1)].rearrange("o p c -> (o p) c").broadcast_to([ET, D]))\
                    .then_inc(s_wts[b], 16)

            def rows(j, b):
                sp.dma_start(xe[:, b, :], rows_dram[bass.ds(j * ET, ET), :]).then_inc(s_rows[b], 16)

            sp.wait_ge(s_eid, 1)
            for b in range(4):
                weights(b, b)
            sp.wait_ge(s_scat, 16 * 2 * TILES)
            for b in range(4):
                rows(b, b)
            with sp.Fori(1, ETILES // 4) as i:
                for b in range(4):
                    sp.wait_ge(s_y, 4 * i + b - 3 + 2)
                    rows(4 * i + b, b)
                    weights(4 * i + b, b)

        def moe_tensor(pe):
            pe.wait_ge(s_both, 1)
            pe.matmul(PS[0][0:P, 0:TILES * E], before[:, :], both[:, :], start=True, stop=True)
            pe.matmul(PS[0][0:P, BANK:BANK + TILES * E], ones[:, :], both[:, :], start=True, stop=True).then_inc(s_rank, 1)
            pe.wait_ge(s_slots, 1)

            def turn(b, loads_done):
                pe.wait_ge(s_rows[b], loads_done)
                for c in range(2):
                    mm = pe.transpose(PS[b % 2][0:DH2, ET * c:ET * c + ET], xe[:, b, DH2 * c:DH2 * c + DH2], ident[:, :])
                mm.then_inc(s_xeT, 1)

            def hidden(b, i, t1):
                pe.wait_ge(s_wts[b], 64 * i + 64)
                pe.wait_ge(s_xe, t1)
                for f in range(FC):
                    for c in range(2):
                        k = DH2 + 1 - c
                        mm = pe.matmul(PS[2 + b % 2][:, ET * f:ET * f + ET],
                                       w1[b][0:k, c * FF + 128 * f:c * FF + 128 * f + 128],
                                       xeT[0:k, b, ET * c:ET * c + ET], start=c == 0, stop=c == 1)
                mm.then_inc(s_up, 1)

            def result(b, t1):
                pe.wait_ge(s_hT, t1)
                pe.wait_ge(s_y, t1)
                for f in range(FC):
                    mm = pe.matmul(PS[b % 2][:, BANK:BANK + D], hT[:, b % 2, ET * f:ET * f + ET],
                                   w2[b][:, f * D:f * D + D], start=f == 0, stop=f == FC - 1)
                mm.then_inc(s_dn, 1)

            def four(i, last):
                for b in (0, 2):
                    hidden(b, i, 4 * i + b + 1)
                    hidden(b + 1, i, 4 * i + b + 2)
                    if not (last and b == 2):
                        for n in ((b + 2) % 4, (b + 3) % 4):
                            turn(n, 16 * i + (16 if b == 0 else 32))
                    result(b, 4 * i + b + 1)
                    result(b + 1, 4 * i + b + 2)

            turn(0, 16)
            turn(1, 16)
            with pe.Fori(0, ETILES // 4 - 1) as i:
                four(i, False)
            four(ETILES // 4 - 1, True)

        def moe_scalar(act):
            act.wait_ge(s_rsub, 1)
            act.activation(lg_all[:, :, :], lg_all[:, :, :], ACT.Exp).then_inc(s_rexp, 1)
            with act.Fori(0, ETILES // 2) as i:
                for hf, t1 in [(0, 2 * i + 1), (1, 2 * i + 2)]:
                    act.wait_ge(s_up, t1)
                    act.activation(hT[:, hf, 0:FF], PS[2 + hf][:, 0:FF], ACT.Gelu).then_inc(s_hT, 1)

        def moe_gpsimd(pool):
            pool.dma_start(out[TOKENS:TOKENS + ET, :], blank[:, 0, 0:D]).then_inc(s_zero, 16)
            pool.wait_ge(s_zero, 16 * (ETILES // 4 + 1))
            pool.wait_ge(s_slots, 2)
            pool.wait_ge(S["base"], TILES)
            for k in range(2):
                pool.wait_ge(s_gate, k + 1)
                for t in range(TILES):
                    pool.indirect_dma_start(out=rows_dram, out_offset=bass.IndirectOffsetOnAxis(ap=slot_u[:, k, t:t + 1], axis=0),
                                            in_=xn_all[:, t, :], in_offset=None).then_inc(s_scat, 16)
            pool.wait_ge(s_base, 16)
            pool.sem_inc(s_yfree, 2)
            with pool.Fori(0, ETILES // 2) as i:
                for hf, t1 in [(0, 2 * i + 1), (1, 2 * i + 2)]:
                    wait_apart(pool, s_y, t1 + 2)
                    pool.indirect_dma_start(out=out, out_offset=bass.IndirectOffsetOnAxis(ap=token[:, hf, 0:1], axis=0),
                                            in_=ye[:, hf, :], in_offset=None, compute_op=ALU.add).then_inc(s_add, 16)
                    pool.wait_ge(s_add, 32 * i + 16 * hf + 16)
                    pool.sem_inc(s_yfree, 1)

        def moe_vector(dve):
            steps = [0]

            def after(ins):
                steps[0] += 1
                ins.then_inc(s_route, 1)
                dve.wait_ge(s_route, steps[0])

            dve.wait_ge(S["rlg"], TILES + 2)
            L = lg_all[:, :, :]
            after(dve.tensor_reduce(tmax[:, :], L, AX.X, ALU.max))
            dve.tensor_tensor(L, L, tmax[:, :].unsqueeze(2).broadcast_to([P, TILES, E]), ALU.subtract).then_inc(s_rsub, 1)
            for k in range(2):
                m = dve.tensor_tensor(v3(oh[:, k, :], TILES), small[:, 0:E].unsqueeze(1).broadcast_to([P, TILES, E]),
                                      id_all[:, :, k:k + 1].broadcast_to([P, TILES, E]), ALU.is_equal)
            after(m)
            dve.tensor_tensor(both[:, :], oh[:, 0, :], oh[:, 1, :], ALU.add).then_inc(s_both, 1)
            dve.wait_ge(s_rank, 1)
            after(dve.tensor_copy(cnt[:, :], PS[0][0:P, BANK:BANK + TE]))
            src, dst = cnt[:, :], 0
            s = 1
            while s < TILES:
                d = cum[:, dst, :]
                dve.tensor_copy(d[:, 0:s * E], src[:, 0:s * E])
                after(dve.tensor_tensor(d[:, s * E:TE], src[:, s * E:TE], src[:, 0:TE - s * E], ALU.add))
                src, dst, s = d, 1 - dst, 2 * s
            total = src[:, TE - E:TE]
            c3 = v3(cmp[:, 0:E * MAXT], E)
            after(dve.tensor_tensor(c3, total.unsqueeze(2).broadcast_to([P, E, MAXT]),
                                    small[:, 18 + ETILES:18 + ETILES + MAXT].unsqueeze(1).broadcast_to([P, E, MAXT]), ALU.is_gt))
            after(dve.tensor_reduce(tcum[:, 0, :], c3, AX.X, ALU.add))
            tsrc, tdst, s = tcum[:, 0, :], 1, 1
            while s < E:
                d = tcum[:, tdst, :]
                dve.tensor_copy(d[:, 0:s], tsrc[:, 0:s])
                after(dve.tensor_tensor(d[:, s:E], tsrc[:, s:E], tsrc[:, 0:E - s], ALU.add))
                tsrc, tdst, s = d, 3 - tdst, 2 * s
            e3 = v3(cmp[0:1, 0:ETILES * E], ETILES)
            after(dve.tensor_tensor(e3, small[0:1, 18:18 + ETILES].unsqueeze(2).broadcast_to([1, ETILES, E]),
                                    tsrc[0:1, :].unsqueeze(1).broadcast_to([1, ETILES, E]), ALU.is_ge))
            after(dve.tensor_reduce(eid_f[:, :], e3, AX.X, ALU.add))
            dve.tensor_scalar(eid[:, :], eid_f[:, :], float(E - 1), None, ALU.min).then_inc(s_eid, 1)
            after(dve.tensor_tensor(tcum[:, 0, :], tsrc, tcum[:, 0, :], ALU.subtract))
            after(dve.tensor_scalar(tcum[:, 0, :], tcum[:, 0, :], float(ET), None, ALU.mult))
            after(dve.tensor_tensor(src, src, cnt[:, :], ALU.subtract))
            after(dve.tensor_tensor(src, PS[0][0:P, 0:TE], src, ALU.add))
            after(dve.tensor_tensor(v3(src, TILES), v3(src, TILES), tcum[:, 0:1, :].broadcast_to([P, TILES, E]), ALU.add))
            for k in range(2):
                m = dve.tensor_tensor(prod[:, k, :], oh[:, k, :], src, ALU.mult)
            m.then_inc(s_slots, 1)
            dve.wait_ge(s_slots, 1)
            dve.tensor_reduce(slot_f[:, 0, :], v3(prod[:, 0, :], TILES), AX.X, ALU.add)
            after(dve.tensor_reduce(slot_f[:, 1, :], v3(prod[:, 1, :], TILES), AX.X, ALU.add))
            dve.tensor_copy(slot_u[:, :, :], slot_f[:, :, :]).then_inc(s_slots, 1)
            dve.wait_ge(s_rexp, 1)
            after(dve.tensor_reduce(tmax[:, :], L, AX.X, ALU.add))
            after(dve.reciprocal(tmax[:, :], tmax[:, :]))
            for k in range(2):
                m = dve.tensor_tensor(prod[:, k, :], oh[:, k, :], L.rearrange("p a b -> p (a b)"), ALU.mult)
            after(m)
            for k in range(2):
                m = dve.tensor_reduce(gate_k[:, k, :], v3(prod[:, k, :], TILES), AX.X, ALU.add)
            after(m)
            for k in range(2):
                if k == 1:
                    dve.wait_ge(s_scat, 16 * TILES)
                dve.tensor_tensor(xn_all[:, :, D + 1], gate_k[:, k, :], tmax[:, :], ALU.mult).then_inc(s_gate, 1)

            dve.sem_inc(s_y, 2)

            def turned(b, t1):
                dve.wait_ge(s_xeT, t1)
                dve.tensor_copy(xeT[0:DH2, b, :], PS[b % 2][0:DH2, 0:2 * ET]).then_inc(s_xe, 1)

            def result(b, t1):
                dve.wait_ge(s_dn, t1)
                dve.wait_ge(s_yfree, t1)
                dve.tensor_tensor(yb[:, b % 2, :], PS[b % 2][:, BANK:BANK + D], b2[:, b, :], ALU.add).then_inc(s_yb, 1)
                dve.tensor_copy(token[:, b % 2, :], xe[:, b, D:D + 1])
                dve.wait_ge(s_yb, t1)
                dve.tensor_scalar(ye[:, b % 2, :], yb[:, b % 2, :], xe[:, b, D + 1:D + 2], None, ALU.mult).then_inc(s_y, 1)

            def four(i, last):
                for b in (0, 2):
                    if not (last and b == 2):
                        for n in (b + 2, b + 3):
                            turned(n % 4, 4 * i + n + 1)
                    result(b, 4 * i + b + 1)
                    result(b + 1, 4 * i + b + 2)

            turned(0, 1)
            turned(1, 2)
            with dve.Fori(0, ETILES // 4 - 1) as i:
                four(i, False)
            four(ETILES // 4 - 1, True)

        block = ctx.enter_context(nc.Block())

        def head0_at(g, b, j):
            return 6 * g + 2 * j + b

        def head1_at(g, b, j):
            return 4 * j + 2 * g + b

        place0 = {head0_at(g, b, j): 6 * g + 3 * b + j for g in range(2) for b in range(2) for j in range(3)}
        place1 = {head1_at(g, b, j): 6 * g + 3 * b + j for g in range(2) for b in range(2) for j in range(3)}

        loads = [(ident[:, :], a["ident"]), (retT[:, :], a["retT"]), (rope[:, :], a["rope"]),
                 (mask0f[:, :], a["mask0"]), (mask1f[:, :], a["mask1"]), (small[:, :], a["small"]),
                 (before[:, :], a["before"]), (pad_row[:, :], a["pad_row"]),
                 (w_tok[:, :, :], a["w_tok"]), (b_tok[:, :], a["b_tok"].partition_broadcast(P)),
                 (w_ret[0:DH2, :, :], a["w_ret"]), (w_ret[DH2:DH2 + 1, 0, :], a["b_ret"]),
                 (w_moh[0:DH2, :, :], a["w_moh"]), (w_moh[DH2:DH2 + 1, 0, :], a["b_moh"]),
                 (w_gate[:, :, 0:RH], a["w_gr"]), (w_gate[:, :, RH:RH + 2], a["w_g0"]),
                 (w_gate[:, :, RH + 2:RH + 4], a["w_g1"]),
                 (w_proj[:, :, :], a["w_proj"]), (b_proj[:, :], a["b_proj"].partition_broadcast(P)),
                 (w_l1[:, :, 0:D], a["w_q1"]), (w_l1[:, :, D:2 * D], a["w_kv1"]),
                 (w_out[0:DH2, :, 0:D], a["w_octx"]), (w_out[0:DH2, :, D:2 * D], a["w_olat"]),
                 (w_out[DH2:DH2 + 1, 0, 0:D], a["b_octx"]), (w_out[DH2:DH2 + 1, 0, D:2 * D], a["b_olat"]),
                 (ln_gb[:, 0, :], a["ln_g"].partition_broadcast(P)),
                 (ln_gb[:, 1, :], a["ln_b"].partition_broadcast(P)),
                 (w_rt[:, :, :], a["w_rt"])]
        for col, name in enumerate(("qw", "qb", "kw", "kb")):
            for k in range(2):
                loads.append((qk_affine[64 * k:64 * k + 64, col:col + 1], a[name]))

        def two(p):
            return [(0, 2 * p + 1), (1, 2 * p + 2)]

        def turned_x(k, hf):
            return PS[2 + hf][:, BANK:2 * BANK] if k in (1, 2) else PS[2 + hf][:, 0:BANK]

        def rounds(eng, ahead, both_of, behind):
            ahead(0)
            both_of(0, True, False)
            with eng.Fori(1, PAIRS - 1) as i:
                both_of(i, True, True)
            both_of(PAIRS - 1, False, True)
            behind(PAIRS - 1)

        @block.sync
        def _(sp):
            for hf in range(2):
                sp.dma_start(x_in[:, hf, :], a["x"][hf]).then_inc(s_x[hf], 16)
            for dst, src in loads:
                sp.dma_start(dst, src).then_inc(s_w, 16)
            with sp.Fori(1, PAIRS) as i:
                for hf in range(2):
                    sp.wait_ge(S["psum_tok"], 2 * i + hf - 1)
                    sp.dma_start(x_in[:, hf, :], a["x"][bass.ds(2 * i + hf, 1)].rearrange("o p c -> (o p) c")).then_inc(s_x[hf], 16)
            moe_sync(sp)

        @block.tensor
        def _(pe):
            pe.wait_ge(s_w, 16 * len(loads))
            pe.wait_ge(s_setup_p, 1)
            pe.wait_ge(s_setup_v, 2)

            def transposes(ps, src, n, w, three=True):
                for c in range(n):
                    c0 = (c // 3) * BANK + (c % 3) * P if three else c * P
                    mm = pe.transpose(ps[0:w, c0:c0 + P], src[:, w * c:w * (c + 1)], ident[0:P, 0:P])
                return mm

            def over_width(dst, lhsT, hf, rhs, rows0=DH2 + 1):
                for c in range(2):
                    k = rows0 if c == 0 else DH2
                    mm = pe.matmul(dst, lhsT[0:k, hf, c * P:(c + 1) * P], rhs(c, k), start=c == 0, stop=c == 1)
                return mm

            def scores(ps, hf, g, rows, head_at, mask, q, k):
                for b in range(2):
                    for j in range(3):
                        hd = head_at(g, b, j)
                        r0, col = rows * (hd % (128 // rows)), hd // (128 // rows) * P
                        pe.matmul(ps[0:P, b * BANK + j * P:b * BANK + j * P + P],
                                  q[r0:r0 + rows, hf, col:col + P], k[r0:r0 + rows, hf, col:col + P],
                                  start=j == 0, stop=False, skip_group_check=True)
                    mm = pe.matmul(ps[0:P, b * BANK:b * BANK + 3 * P], mask[r0:r0 + rows, 0:P],
                                   mask[r0:r0 + rows, P:4 * P], start=False, stop=True, skip_group_check=True)
                return mm

            def tok(p, hf, t1, once):
                pe.wait_ge(s_x[hf], 16 * p + 16)
                if not once:
                    pe.wait_ge(S["rlg"], t1 - 4)
                for c in range(PC):
                    mm = pe.matmul(PS[2 + hf][0:P, 0:D], x_in[:, hf, c * P:(c + 1) * P], w_tok[:, c, :],
                                   start=c == 0, stop=c == PC - 1)
                mm.then_inc(S["psum_tok"], 1)

            def turn_x(k, hf, t1):
                pe.wait_ge(S[f"xn{k}"], t1)
                transposes(turned_x(k, hf), xn[k][:, hf, :], 2, DH2, False).then_inc(S[f"psum_xnT{k}"], 1)

            def qkv0(hf, t1):
                pe.wait_ge(S["xnT0"], t1)
                ps = PS[2 + hf]
                for m in range(4):
                    for c in range(2):
                        k = DH2 + 1 - c
                        pe.matmul(ps[0:DH2, P * m:P * m + P], w_ret[0:k, c, DH2 * m:DH2 * m + DH2],
                                  xnT[0][0:k, hf, c * P:(c + 1) * P], start=c == 0, stop=c == 1)
                over_width(ps[0:P, BANK:BANK + D], xnT[0], hf, lambda c, k: w_ret[0:k, c, 2 * D:3 * D])\
                    .then_inc(S["psum_qkv0"], 1)

            def s0(hf, t1):
                pe.wait_ge(S["qkT0"], t1)
                pe.wait_ge(S["v0"], t1)
                for c in range(2):
                    mm = pe.matmul(PS[2 + hf][0:P, 0:P], qkT0[:, hf, (2 + c) * P:(3 + c) * P],
                                   qkT0[:, hf, c * P:(c + 1) * P], start=c == 0, stop=c == 1)
                mm.then_inc(S["psum_s0"], 1)

            def o0(hf, t1):
                pe.wait_ge(S["pT0"], t1)
                pe.matmul(PS[2 + hf][0:P, 0:D], pT0[:, hf, :], v0[:, hf, :], start=True, stop=True)\
                    .then_inc(S["psum_o0"], 1)

            def wide(hf, part, name):
                for b in range(2):
                    c0 = part * H0 * HD0 + b * 384
                    mm = over_width(PS[hf][0:P, b * BANK:b * BANK + 384], xnT[1], hf,
                                    lambda c, k: w_moh[0:k, c, c0:c0 + 384])
                if part == 2:
                    mm = over_width(PS[hf][0:P, BANK + 384:BANK + 384 + RH + 4], xnT[1], hf,
                                    lambda c, k: w_gate[0:k, c, :], DH2)
                mm.then_inc(S[name], 1)

            def q(hf, t1):
                pe.wait_ge(S["xnT1"], t1)
                pe.wait_ge(S["h2"], t1)
                wide(hf, 0, "psum_q")

            def k(hf, t1):
                pe.wait_ge(S["sqq"], t1)
                wide(hf, 1, "psum_k")

            def v(hf, t1):
                pe.wait_ge(S["sqk"], t1)
                wide(hf, 2, "psum_v")

            def turn_heads(src, n0, ready, free, name, hf, t1):
                pe.wait_ge(S[ready], t1)
                pe.wait_ge(S[free], t1)
                transposes(PS[hf], src[:, hf, n0:n0 + 768], 6, 128).then_inc(S[name], 1)

            def sab(g, hf, t1):
                pe.wait_ge(S["suba" if g else "kT"], t1)
                pe.wait_ge(S["qT"], t1)
                scores(PS[hf], hf, g, HD0, head0_at, mask0, qT, kT).then_inc(S["psum_sb" if g else "psum_sa"], 1)

            def turn_p(g, hf, t1, k1):
                pe.wait_ge(S[("e1b" if g else "e1a") if k1 else ("eb" if g else "ea")], t1)
                pe.wait_ge(S[("p1Ta" if g else "sub1b") if k1 else ("pTa" if g else "subb")], t1)
                src = (pr1 if k1 else pr)[0:P, hf, g * HALF6:(g + 1) * HALF6]
                transposes(PS[2 + hf if k1 else hf], src, 6, P)\
                    .then_inc(S["psum_p" + ("1" if k1 else "") + ("Tb" if g else "Ta")], 1)

            def pv(hf, t1):
                pe.wait_ge(S["pTb"], t1)
                pe.wait_ge(S["v"], t1)
                for hd in range(H0):
                    c0 = (hd // 6) * BANK + (hd % 6) * (HD0 + 1)
                    mm = pe.matmul(PS[hf][0:P, c0:c0 + HD0 + 1], pT[:, hf, place0[hd] * P:(place0[hd] + 1) * P],
                                   v_aug[:, hf, hd * (HD0 + 1):(hd + 1) * (HD0 + 1)], start=True, stop=True)
                mm.then_inc(S["psum_pv"], 1)

            def turn_o(hf, t1):
                pe.wait_ge(S["o"], t1)
                transposes(PS[hf], o[:, hf, :], 6, 128).then_inc(S["psum_oT"], 1)

            def proj(hf, t1):
                pe.wait_ge(S["oT"], t1)
                for c in range(6):
                    mm = pe.matmul(PS[hf][0:P, 0:D], oT[:, hf, c * P:(c + 1) * P], w_proj[:, c, :],
                                   start=c == 0, stop=c == 5)
                mm.then_inc(S["psum_proj"], 1)

            def qkv1(hf, t1):
                pe.wait_ge(S["xnT2"], t1)
                over_width(PS[2 + hf][0:P, 0:2 * D], xnT[2], hf, lambda c, k: w_l1[0:k, c, :], DH2)\
                    .then_inc(S["psum_qkv1"], 1)

            def turn_qk1(hf, t1):
                pe.wait_ge(S["qk1"], t1)
                transposes(PS[2 + hf], qk1[:, hf, :], 6, 128).then_inc(S["psum_qkT1"], 1)

            def sab1(g, hf, t1):
                pe.wait_ge(S["sub1a" if g else "q1T"], t1)
                scores(PS[2 + hf], hf, g, PAD1, head1_at, mask1, qT1, kT1).then_inc(S["psum_s1b" if g else "psum_s1a"], 1)

            def pv1(hf, t1):
                pe.wait_ge(S["v1"], t1)
                pe.wait_ge(S["p1Tb"], t1)
                w = HD1 + 1
                for hd in range(H1):
                    mm = pe.matmul(PS[2 + hf][0:P, hd * w:(hd + 1) * w], pT1[:, hf, place1[hd] * P:(place1[hd] + 1) * P],
                                   v1_aug[:, hf, hd * w:(hd + 1) * w], start=True, stop=True)
                mm.then_inc(S["psum_pv1"], 1)

            def turn_om(hf, t1):
                pe.wait_ge(S["om"], t1)
                transposes(PS[2 + hf], om[:, hf, :], 2, DH2, False).then_inc(S["psum_omT"], 1)

            def out1(hf, t1):
                pe.wait_ge(S["omT"], t1)
                over_width(PS[2 + hf][0:P, 0:2 * D], omT, hf, lambda c, k: w_out[0:k, c, :]).then_inc(S["psum_out"], 1)

            def router(hf, t1):
                pe.wait_ge(S["xnT3"], t1)
                over_width(PS[2 + hf][0:P, 0:E], xnT[3], hf, lambda c, k: w_rt[0:k, c, :], DH2)\
                    .then_inc(S["psum_rt"], 1)

            def each(pair, fn, *args):
                for hf, t1 in pair:
                    fn(*args, hf, t1)

            def free_for_layer1(A, pair, i):
                for hf, t1 in pair:
                    if A:
                        pe.wait_ge(S["h1"], two(i + 1)[hf][1])
                    else:
                        pe.wait_ge(S["rlg"], t1)

            def round_(i, A, C):
                b, an, cp = two(i), two(i + 1), two(i - 1)
                each(b, q)
                if A:
                    for hf, t1 in an:
                        tok(i + 1, hf, t1, not C)
                if C:
                    each(cp, turn_x, 2)
                k(*b[0])
                if A:
                    each(an, turn_x, 0)
                k(*b[1])
                if A:
                    for hf, t1 in an:
                        if C:
                            pe.wait_ge(S["xnT2"], cp[hf][1])
                        qkv0(hf, t1)
                v(*b[0])
                if A:
                    each(an, s0)
                v(*b[1])
                if A:
                    each(an, o0)
                if C:
                    free_for_layer1(A, cp, i)
                    each(cp, qkv1)
                each(b, turn_heads, qn, 0, "qn", "gl", "psum_qT")
                each(b, turn_heads, qn, 768, "kn", "qT", "psum_kT")
                sab(0, *b[0])
                sab(0, *b[1])
                if C:
                    each(cp, turn_qk1)
                    each(cp, sab1, 0)
                each(b, sab, 1)
                if C:
                    each(cp, sab1, 1)
                for hf, t1 in b:
                    turn_p(0, hf, t1, False)
                if C:
                    for hf, t1 in cp:
                        turn_p(0, hf, t1, True)
                for hf, t1 in b:
                    turn_p(1, hf, t1, False)
                if C:
                    for hf, t1 in cp:
                        turn_p(1, hf, t1, True)
                each(b, pv)
                if C:
                    each(cp, pv1)
                if A:
                    each(an, turn_x, 1)
                each(b, turn_o)
                if C:
                    each(cp, turn_om)
                    each(cp, out1)
                each(b, proj)
                if C:
                    each(cp, turn_x, 3)
                    each(cp, router)

            def ahead(p):
                for hf, t1 in two(p):
                    tok(p, hf, t1, True)
                each(two(p), turn_x, 0)
                for fn in (qkv0, s0, o0):
                    each(two(p), fn)
                each(two(p), turn_x, 1)

            def behind(p):
                each(two(p), turn_x, 2)
                free_for_layer1(False, two(p), p + 1)
                for fn, *args in ((qkv1,), (turn_qk1,), (sab1, 0), (sab1, 1)):
                    each(two(p), fn, *args)
                for g in range(2):
                    for hf, t1 in two(p):
                        turn_p(g, hf, t1, True)
                for fn, *args in ((pv1,), (turn_om,), (out1,), (turn_x, 3), (router,)):
                    each(two(p), fn, *args)

            rounds(pe, ahead, round_, behind)
            moe_tensor(pe)

        @block.scalar
        def _(act):
            act.wait_ge(s_w, 16 * len(loads))
            act.wait_ge(s_setup_v, 2)
            act.wait_ge(s_setup_p, 1)

            def copy(dst, src, ready, done, t1):
                act.wait_ge(S[ready], t1)
                act.activation(dst, src, ACT.Copy).then_inc(S[done], 1)

            def x_t(pair, k):
                for hf, t1 in pair:
                    copy(xnT[k][0:DH2, hf, :], turned_x(k, hf)[0:DH2, 0:2 * P], f"psum_xnT{k}", f"xnT{k}", t1)

            def square(hf, t1, c0, sq, ready, done):
                act.wait_ge(S[ready], t1)
                act.activation(v3(qn[:, hf, c0:c0 + 768], 2), banks(PS[hf], P, 384), ACT.Copy)
                act.activation(v3(sq[:, hf, :], 2), banks(PS[hf], P, 384), ACT.Square).then_inc(S[done], 1)

            def expo(pair, buf, g, ready, done):
                for hf, t1 in pair:
                    act.wait_ge(S[ready], t1)
                    x = buf[0:P, hf, g * HALF6:(g + 1) * HALF6]
                    act.activation(x, x, ACT.Exp).then_inc(S[done], 1)

            def p_t(pair, buf, s, g, ready, done):
                for hf, t1 in pair:
                    copy(v3(buf[:, hf, g * HALF6:(g + 1) * HALF6], 2), banks(PS[s + hf], P, 3 * P), ready, done, t1)

            def qk_t0(pair):
                for hf, t1 in pair:
                    copy(qkT0[:, hf, :], PS[2 + hf][0:DH2, 0:4 * P], "psum_qkv0", "qkT0", t1)

            def qk_t1(pair):
                for hf, t1 in pair:
                    act.wait_ge(S["psum_qkT1"], t1)
                    act.activation(qT1[:, hf, :], PS[2 + hf][:, 0:3 * P], ACT.Copy)
                    act.activation(kT1[:, hf, :], PS[2 + hf][:, BANK:BANK + 3 * P], ACT.Copy).then_inc(S["q1T"], 1)

            def om_t(pair):
                for hf, t1 in pair:
                    copy(omT[0:DH2, hf, :], PS[2 + hf][0:DH2, 0:2 * P], "psum_omT", "omT", t1)

            def round_(i, A, C):
                b, an, cp = two(i), two(i + 1), two(i - 1)
                for hf, t1 in b:
                    square(hf, t1, 0, sqq, "psum_q", "sqq")
                if C:
                    x_t(cp, 2)
                square(*b[0], 768, sqk, "psum_k", "sqk")
                if A:
                    x_t(an, 0)
                square(*b[1], 768, sqk, "psum_k", "sqk")
                if A:
                    qk_t0(an)
                for hf, t1 in b:
                    copy(v_aug[:, hf, :].rearrange("p (b h d) -> p b h d", b=2, h=6)[:, :, :, 0:HD0],
                         banks(PS[hf], P, 384).rearrange("p b (h d) -> p b h d", h=6), "psum_v", "v", t1)
                act.wait_ge(S["gsub"], i + 1)
                act.activation(ge[:, :, :], gl[:, :, :], ACT.Exp).then_inc(S["gexp"], 1)
                for hf, t1 in b:
                    act.wait_ge(S["psum_qT"], t1)
                    act.activation(v3(qT[:, hf, :], 2), banks(PS[hf], 128, 3 * P), ACT.Identity,
                                   bias=qk_affine[:, 1:2], scale=qk_affine[:, 0:1]).then_inc(S["qT"], 1)
                if C:
                    qk_t1(cp)
                expo(b, pr, 0, "suba", "ea")
                if C:
                    expo(cp, pr1, 0, "sub1a", "e1a")
                expo(b, pr, 1, "subb", "eb")
                if C:
                    expo(cp, pr1, 1, "sub1b", "e1b")
                p_t(b, pT, 0, 0, "psum_pTa", "pTa")
                if C:
                    p_t(cp, pT1, 2, 0, "psum_p1Ta", "p1Ta")
                p_t(b, pT, 0, 1, "psum_pTb", "pTb")
                if C:
                    p_t(cp, pT1, 2, 1, "psum_p1Tb", "p1Tb")
                if A:
                    x_t(an, 1)
                for hf, t1 in b:
                    copy(v3(oT[:, hf, :], 2), banks(PS[hf], 128, 3 * P), "psum_oT", "oT", t1)
                if C:
                    om_t(cp)
                    x_t(cp, 3)

            def ahead(p):
                x_t(two(p), 0)
                qk_t0(two(p))
                x_t(two(p), 1)

            def behind(p):
                x_t(two(p), 2)
                qk_t1(two(p))
                expo(two(p), pr1, 0, "sub1a", "e1a")
                expo(two(p), pr1, 1, "sub1b", "e1b")
                p_t(two(p), pT1, 2, 0, "psum_p1Ta", "p1Ta")
                p_t(two(p), pT1, 2, 1, "psum_p1Tb", "p1Tb")
                om_t(two(p))
                x_t(two(p), 3)

            rounds(act, ahead, round_, behind)
            moe_scalar(act)

        @block.gpsimd
        def _(pool):
            pool.memset(blank[:, :, :], 0.0).then_inc(s_zeros, 1)
            pool.memset(ones[:, :], 1.0)
            pool.memset(neg_half[:, :], -0.5)
            pool.memset(v_aug[:, :, :], 1.0)
            pool.memset(v1_aug[:, :, :], 1.0)
            pool.memset(qk1[:, :, :], 0.0).then_inc(s_setup_p, 1)
            pool.wait_ge(s_w, 16 * len(loads))
            pool.wait_ge(s_zeros, 1)
            pool.tensor_copy(blank[:, :, D:D + 1], pad_row[:, :].unsqueeze(1).broadcast_to([ET, 4, 1])).then_inc(s_zeros, 1)
            pool.wait_ge(s_zeros, 2)
            rows4 = rows_dram.rearrange("(a j p) c -> a p j c", j=4, p=ET)
            for k in range(ETILES // 4):
                pool.dma_start(rows4[k], blank[:, :, :]).then_inc(s_zero, 16)
            pool.wait_ge(s_setup_p, 1)

            def root(k, p):
                pool.wait_ge(S[f"va{k}"], p + 1)
                pool.tensor_tensor(rstd[k][:, :, 0], mv[k][:, :, 1], neg_half[:, 0:2], ALU.pow).then_inc(S[f"rs{k}"], 1)

            def root_q(p):
                for hf, t1 in two(p):
                    v = ss[:, hf, 0:12]
                    wait_apart(pool, S["ssq"], t1)
                    pool.tensor_scalar(v, v, 1.0 / HD0, EPS, ALU.mult, ALU.add).then_inc(S["qvar"], 1)
                    pool.wait_ge(S["qvar"], t1)
                    pool.tensor_tensor(v, v, neg_half[:, 0:12], ALU.pow).then_inc(S["rsq"], 1)

            def residual(p):
                for hf, t1 in two(p):
                    pool.wait_ge(S["h1"], t1)
                    pool.tensor_tensor(hb[:, hf:hf + 1, :], h_all[:, bass.ds(2 * p + hf, 1), :],
                                       b_proj[:, :].unsqueeze(1), ALU.add).then_inc(S["hb"], 1)

            kv = [qk1[:, hf, :].rearrange("p (n d) -> p n d", d=PAD1)[:, H1:2 * H1, 0:HD1] for hf in range(2)]
            c3 = [v3(lc[:, hf, :], H1) for hf in range(2)]

            def rotate(p):
                for hf, t1 in two(p):
                    pool.wait_ge(S["rope"], t1)
                    pool.tensor_tensor(qk1[:, hf, :].rearrange("p (n d) -> p n d", d=PAD1)[:, :, 0:HD1],
                                       ropa[:, hf, :].rearrange("p (n d) -> p n d", d=HD1),
                                       ropb[:, hf, :].rearrange("p (n d) -> p n d", d=HD1),
                                       ALU.add).then_inc(S["qk1"], 1)

            def centre(p):
                for hf, t1 in two(p):
                    pool.wait_ge(S["lmean"], p + 1)
                    pool.tensor_tensor(c3[hf], kv[hf], lsum[:, hf, :].unsqueeze(2).broadcast_to([P, H1, HD1]),
                                       ALU.add).then_inc(S["lc"], 1)
                for hf, t1 in two(p):
                    pool.wait_ge(S["lc"], t1)
                    pool.tensor_tensor(lsq[:, hf, :], lc[:, hf, :], lc[:, hf, :], ALU.mult).then_inc(S["lsq"], 1)

            def scale(p):
                for hf, t1 in two(p):
                    pool.wait_ge(S["lrsq"], RSQ * p + RSQ)
                    pool.tensor_tensor(c3[hf], c3[hf], lr[:, hf, :].unsqueeze(2).broadcast_to([P, H1, HD1]),
                                       ALU.mult).then_inc(S["lv1"], 1)
                for hf, t1 in two(p):
                    pool.wait_ge(S["lv1"], t1)
                    pool.tensor_tensor(c3[hf], c3[hf], ln_gb[:, 0:1, :].broadcast_to([P, H1, HD1]),
                                       ALU.mult).then_inc(S["lv2"], 1)
                for hf, t1 in two(p):
                    pool.wait_ge(S["lv2"], t1)
                    pool.tensor_tensor(v1_aug[:, hf, :].rearrange("p (n d) -> p n d", d=HD1 + 1)[:, :, 0:HD1],
                                       c3[hf], ln_gb[:, 1:2, :].broadcast_to([P, H1, HD1]),
                                       ALU.add).then_inc(S["v1"], 1)

            def keep(p):
                for hf, t1 in two(p):
                    pool.wait_ge(S["xn3"], t1)
                    pool.tensor_copy(xn_all[:, bass.ds(2 * p + hf, 1), 0:D], xn[3][:, hf:hf + 1, :])
                    pool.tensor_tensor(h_all[:, bass.ds(2 * p + hf, 1), :], h_all[:, bass.ds(2 * p + hf, 1), :],
                                       xn[3][:, hf:hf + 1, :], ALU.add).then_inc(S["base"], 1)

            def round_(i, A, C):
                root_q(i)
                if A:
                    root(0, i + 1)
                residual(i)
                if A:
                    root(1, i + 1)
                if C:
                    rotate(i - 1)
                    centre(i - 1)
                    scale(i - 1)
                    root(3, i - 1)
                    keep(i - 1)
                root(2, i)

            def ahead(p):
                root(0, p)
                root(1, p)

            def behind(p):
                rotate(p)
                centre(p)
                scale(p)
                root(3, p)
                keep(p)

            rounds(pool, ahead, round_, behind)
            moe_gpsimd(pool)

        @block.vector
        def _(dve):
            for rows in (*xnT[:3], omT, xeT):
                dve.memset(rows[DH2:DH2 + 1, :, :], 1.0)
            dve.wait_ge(s_w, 16 * len(loads))
            dve.tensor_copy(xn_all[:, :, D:D + 1], small[:, 18 + ETILES + MAXT:].unsqueeze(2))
            dve.tensor_copy(mask0[:, :], mask0f[:, :])
            dve.tensor_copy(mask1[:, :], mask1f[:, :])
            dve.tensor_scalar(qk_affine[:, 0:2], qk_affine[:, 0:2], HD0 ** -0.5, None, ALU.mult)
            wq = [w_moh[0:DH2 + 1 - c, c, 0:1536].rearrange("p (n d) -> p n d", d=HD0) for c in range(2)]
            for c in range(2):
                dve.tensor_reduce(wmean[0:DH2 + 1 - c, c, :], wq[c], AX.X, ALU.add).then_inc(s_center, 1)
            dve.wait_ge(s_center, 2)
            for c in range(2):
                m = wmean[0:DH2 + 1 - c, c, :]
                dve.tensor_scalar(m, m, -1.0 / HD0, None, ALU.mult).then_inc(s_center, 1)
            dve.wait_ge(s_center, 4)
            for c in range(2):
                n = DH2 + 1 - c
                dve.tensor_tensor(wq[c], wq[c], wmean[0:n, c, :].unsqueeze(2).broadcast_to([n, 24, HD0]), ALU.add)\
                    .then_inc(s_setup_v, 1)
            dve.sem_inc(S["rlg"], 2)
            dve.sem_inc(S["h2"], 2)

            def h_of(p, hf):
                return h_all[:, bass.ds(2 * p + hf, 1), :]

            def stats_of(p, k, credit=0):
                for hf, t1 in two(p):
                    wait_apart(dve, S[f"h{k}"], t1 + credit)
                    m = dve.bn_stats(stats[:, hf, :], h_of(p, hf))
                m.then_inc(S[f"stat{k}"], 1)
                wait_apart(dve, S[f"stat{k}"], 2 * p + 1)
                for hf in range(2):
                    m = dve.bn_aggr(mv[k][:, hf, :], stats[:, hf, :])
                m.then_inc(S[f"stat{k}"], 1)
                dve.wait_ge(S[f"stat{k}"], 2 * p + 2)
                dve.tensor_scalar(mv[k][:, :, 1:2], mv[k][:, :, 1:2], EPS, None, ALU.add).then_inc(S[f"va{k}"], 1)

            def norm(p, k):
                for hf in range(2):
                    dve.wait_ge(S[f"rs{k}"], p + 1)
                    dve.tensor_scalar(xn[k][:, hf:hf + 1, :], h_of(p, hf), mv[k][:, hf, 0:1], rstd[k][:, hf, 0:1],
                                      ALU.subtract, ALU.mult).then_inc(S[f"xn{k}"], 1)

            def rsqrt(dst, src, shape, chain, p, mean):
                n = shape[0] * shape[1]
                nv, y, t = (rs[:, c, 0:n].rearrange("p (a b) -> p a b", a=shape[0]) for c in range(3))
                bits = rs_bits[:, 0:n].rearrange("p (a b) -> p a b", a=shape[0])
                step = [0]

                def then(ins):
                    step[0] += 1
                    ins.then_inc(S[chain], 1)
                    if step[0] < RSQ:
                        dve.wait_ge(S[chain], RSQ * p + step[0])

                then(dve.tensor_scalar(src, src, mean, EPS, ALU.mult, ALU.add))
                dve.tensor_scalar(nv, src, -0.5, None, ALU.mult)
                then(dve.tensor_scalar(bits, src.bitcast(I32), 1, None, ALU.logical_shift_right))
                then(dve.tensor_scalar(y.bitcast(I32), bits, -1.0, float(0x5F3759DF), ALU.mult, ALU.add))
                for last in (False, False, True):
                    then(dve.tensor_tensor(t, y, y, ALU.mult))
                    then(dve.tensor_tensor(t, t, nv, ALU.mult))
                    then(dve.scalar_tensor_tensor(dst if last else y, t, 1.5, y, ALU.add, ALU.mult))
                assert step[0] == RSQ

            def softmax_in(hf, t1, ps, buf, nm_buf, g, ready, nm, done):
                def maxima():
                    dve.wait_ge(S[ready], t1)
                    dve.tensor_reduce(v3(nm_buf[:, hf, 6 * g:6 * g + 6], 2),
                                      banks(ps, P, 3 * P).rearrange("p b (h k) -> p b h k", h=3),
                                      AX.X, ALU.max, negate=True).then_inc(S[nm], 1)

                def subtract():
                    dve.wait_ge(S[nm], t1)
                    for b in range(2):
                        c0 = g * HALF6 + b * 3 * P
                        mm = dve.tensor_tensor(v3(buf[0:P, hf, c0:c0 + 3 * P], 3), v3(ps[0:P, b * BANK:b * BANK + 3 * P], 3),
                                               nm_buf[:, hf, 6 * g + 3 * b:6 * g + 3 * b + 3].unsqueeze(2).broadcast_to([P, 3, P]),
                                               ALU.add)
                    mm.then_inc(S[done], 1)
                return maxima, subtract

            def softmaxes(pair, s, buf, nm_buf, g, *names):
                steps = [softmax_in(hf, t1, PS[s + hf], buf, nm_buf, g, *names) for hf, t1 in pair]
                for maxima, _ in steps:
                    maxima()
                for _, subtract in steps:
                    subtract()

            def embed(p):
                for hf, t1 in two(p):
                    dve.wait_ge(S["psum_tok"], t1)
                    dve.tensor_tensor(h_of(p, hf), PS[2 + hf][0:P, 0:D].unsqueeze(1), b_tok[:, :].unsqueeze(1), ALU.add)\
                        .then_inc(S["h0"], 1)
                stats_of(p, 0)

            def values(p):
                for hf, t1 in two(p):
                    dve.wait_ge(S["psum_qkv0"], t1)
                    dve.tensor_copy(v0[:, hf, :], PS[2 + hf][0:P, BANK:BANK + D]).then_inc(S["v0"], 1)

            def decay(p):
                for hf, t1 in two(p):
                    dve.wait_ge(S["psum_s0"], t1)
                    dve.tensor_tensor(pT0[:, hf, :], PS[2 + hf][0:P, 0:P], retT[:, :], ALU.mult).then_inc(S["pT0"], 1)

            def retained(p):
                for hf, t1 in two(p):
                    dve.wait_ge(S["psum_o0"], t1)
                    dve.tensor_tensor(h_of(p, hf), PS[2 + hf][0:P, 0:D].unsqueeze(1), h_of(p, hf), ALU.add).then_inc(S["h1"], 1)

            def sums(hf, t1, c0, sq, ready):
                dve.wait_ge(S[ready], t1)
                dve.tensor_reduce(ss[:, hf, c0:c0 + 12], v3(sq[:, hf, :], 12),
                                  AX.X, ALU.add).then_inc(S["ssk" if c0 else "ssq"], 1)

            def normed(i, c0, done):
                for hf, t1 in two(i):
                    if c0:
                        dve.wait_ge(S["rsk"], RSQ * i + RSQ)
                    else:
                        dve.wait_ge(S["rsq"], t1)
                    x = v3(qn[:, hf, c0 * 64:c0 * 64 + 768], 12)
                    dve.tensor_tensor(x, x, ss[:, hf, c0:c0 + 12].unsqueeze(2).broadcast_to([P, 12, HD0]), ALU.mult)\
                        .then_inc(S[done], 1)

            def gate_logits(i):
                for hf, t1 in two(i):
                    dve.wait_ge(S["v"], t1)
                    dve.tensor_copy(gl[:, hf, :], PS[hf][0:P, BANK + 384:BANK + 384 + RH + 4]).then_inc(S["gl"], 1)

            def pick(i):
                wait_apart(dve, S["gl"], 2 * i + 2)
                for hf in range(2):
                    dve.max(gmx[:, hf, :], gl[:, hf, 0:RH])
                ways = gl[:, :, RH:RH + 4].rearrange("p a (b c) -> p a b c", b=2)
                dve.tensor_reduce(v3(gm2[:, :], 2), ways, AX.X, ALU.max).then_inc(S["gpick"], 1)
                wait_apart(dve, S["gpick"], 2 * i + 1)
                for hf in range(2):
                    m = dve.max_index(gidx[:, hf, :], gmx[:, hf, :], gl[:, hf, 0:RH])
                m.then_inc(S["gpick"], 1)
                dve.wait_ge(S["gpick"], 2 * i + 2)
                dve.tensor_copy(gidf[:, :, :], gidx[:, :, 0:2])
                dve.tensor_tensor(gl[:, :, 0:RH], gl[:, :, 0:RH], gmx[:, :, 0:1].broadcast_to([P, 2, RH]), ALU.subtract)
                dve.tensor_tensor(ways, ways, v3(gm2[:, :], 2).unsqueeze(3).broadcast_to([P, 2, 2, 2]),
                                  ALU.subtract).then_inc(S["gsub"], 1)

            def gate(i):
                GS = 8

                def gate_step(ins, n):
                    ins.then_inc(S["gstep"], 1)
                    dve.wait_ge(S["gstep"], GS * i + n)

                dve.wait_ge(S["gexp"], i + 1)
                g2 = ge[:, :, RH:RH + 4].rearrange("p a (b c) -> p a b c", b=2)
                dve.tensor_reduce(gsum[:, :, 0:1], ge[:, :, 0:RH], AX.X, ALU.add)
                dve.tensor_reduce(gsum[:, :, 1:3], g2, AX.X, ALU.add)
                for hf in range(2):
                    m = dve.tensor_scalar(gmask[:, hf, :], small[:, 0:RH], gidf[:, hf, 1:2], None, ALU.is_equal)
                gate_step(m, 1)
                dve.reciprocal(gsum[:, :, 0:3], gsum[:, :, 0:3])
                for hf in range(2):
                    m = dve.scalar_tensor_tensor(gmask[:, hf, :], small[:, 0:RH], gidf[:, hf, 0:1], gmask[:, hf, :],
                                                 ALU.is_equal, ALU.add)
                gate_step(m, 2)
                for hf in range(2):
                    dve.scalar_tensor_tensor(gmask[:, hf, :], ge[:, hf, 0:RH], gsum[:, hf, 0:1], gmask[:, hf, :],
                                             ALU.mult, ALU.mult)
                gate_step(dve.tensor_tensor(g2, g2, gsum[:, :, 1:3].unsqueeze(3).broadcast_to([P, 2, 2, 2]), ALU.mult), 3)
                dve.tensor_reduce(gden[:, :, 0:1], gmask[:, :, :], AX.X, ALU.add)
                gate_step(dve.tensor_tensor(gates[:, :, 0:SH], ge[:, :, RH + 2:RH + 4],
                                            ge[:, :, RH:RH + 1].broadcast_to([P, 2, SH]), ALU.mult), 4)
                gate_step(dve.tensor_scalar(gden[:, :, 0:1], gden[:, :, 0:1], float(np.finfo(np.float32).eps), None,
                                            ALU.max), 5)
                gate_step(dve.reciprocal(gden[:, :, 0:1], gden[:, :, 0:1]), 6)
                gate_step(dve.tensor_tensor(gden[:, :, 1:2], gden[:, :, 0:1], ge[:, :, RH + 1:RH + 2], ALU.mult), 7)
                gate_step(dve.tensor_tensor(gates[:, :, SH:H0], gmask[:, :, :], gden[:, :, 1:2].broadcast_to([P, 2, RH]),
                                            ALU.mult), 8)
                dve.tensor_scalar(gates[:, :, :], gates[:, :, :], 4.0, None, ALU.mult).then_inc(S["gates"], 1)

            def keys(i):
                for hf, t1 in two(i):
                    dve.wait_ge(S["psum_kT"], t1)
                    dve.tensor_scalar(v3(kT[:, hf, :], 2), banks(PS[hf], 128, 3 * P),
                                      qk_affine[:, 2:3], qk_affine[:, 3:4], ALU.mult, ALU.add).then_inc(S["kT"], 1)

            def heads(i, hf, t1):
                dve.wait_ge(S["psum_pv"], t1)
                dve.reciprocal(v3(fac[:, hf, :], 2),
                               banks(PS[hf], P, 390).rearrange("p b (h d) -> p b h d", h=6)[:, :, :, HD0])\
                    .then_inc(S["fac0"], 1)
                dve.wait_ge(S["gates"], i + 1)
                dve.wait_ge(S["fac0"], t1)
                dve.tensor_tensor(fac[:, hf, :], fac[:, hf, :], gates[:, hf, :], ALU.mult).then_inc(S["fac"], 1)
                dve.wait_ge(S["fac"], t1)
                for b in range(2):
                    mm = dve.tensor_tensor(v3(o[:, hf, 384 * b:384 * b + 384], 6),
                                           v3(PS[hf][0:P, BANK * b:BANK * b + 390], 6)[:, :, 0:HD0],
                                           fac[:, hf, 6 * b:6 * b + 6].unsqueeze(2).broadcast_to([P, 6, HD0]), ALU.mult)
                mm.then_inc(S["o"], 1)

            def projected(i):
                for hf, t1 in two(i):
                    dve.wait_ge(S["psum_proj"], t1)
                    dve.wait_ge(S["hb"], t1)
                    dve.tensor_tensor(h_of(i, hf), PS[hf][0:P, 0:D].unsqueeze(1), hb[:, hf:hf + 1, :], ALU.add)\
                        .then_inc(S["h2"], 1)
                stats_of(i, 2, 2)

            kv = [qk1[:, hf, :].rearrange("p (n d) -> p n d", d=PAD1)[:, H1:2 * H1, 0:HD1] for hf in range(2)]

            def halves(x, k):
                return x.rearrange("p (n b d) -> p n b d", b=2, d=HD1 // 2)[:, :, k, :]

            def rotary(p):
                for hf, t1 in two(p):
                    dve.wait_ge(S["psum_qkv1"], t1)
                    ps = PS[2 + hf][0:P, 0:2 * D]
                    dve.tensor_tensor(ropa[:, hf, :], ps, rope[:, 0:2 * D], ALU.mult)
                    for b in range(2):
                        mm = dve.tensor_tensor(halves(ropb[:, hf, :], b), halves(ps, 1 - b),
                                               halves(rope[:, 2 * D:4 * D], b), ALU.mult)
                    mm.then_inc(S["rope"], 1)

            def kv_mean(p):
                for hf, t1 in two(p):
                    dve.wait_ge(S["qk1"], t1)
                    m = dve.tensor_reduce(lsum[:, hf, :], kv[hf], AX.X, ALU.add)
                m.then_inc(S["lsum"], 1)
                dve.wait_ge(S["lsum"], p + 1)
                dve.tensor_scalar(lsum[:, :, :], lsum[:, :, :], -1.0 / HD1, None, ALU.mult).then_inc(S["lmean"], 1)

            def kv_rstd(p):
                for hf, t1 in two(p):
                    dve.wait_ge(S["lsq"], t1)
                    m = dve.tensor_reduce(lr[:, hf, :], v3(lsq[:, hf, :], H1), AX.X, ALU.add)
                m.then_inc(S["lsum2"], 1)
                dve.wait_ge(S["lsum2"], p + 1)
                rsqrt(lr[:, :, :], lr[:, :, :], (2, H1), "lrsq", p, 1.0 / HD1)

            def attended(p):
                for hf, t1 in two(p):
                    dve.wait_ge(S["psum_pv1"], t1)
                    dve.reciprocal(fac1[:, hf, :], v3(PS[2 + hf][0:P, 0:H1 * (HD1 + 1)], H1)[:, :, HD1])\
                        .then_inc(S["rden"], 1)
                for hf, t1 in two(p):
                    dve.wait_ge(S["rden"], t1)
                    dve.tensor_tensor(v3(om[:, hf, :], H1), v3(PS[2 + hf][0:P, 0:H1 * (HD1 + 1)], H1)[:, :, 0:HD1],
                                      fac1[:, hf, :].unsqueeze(2).broadcast_to([P, H1, HD1]), ALU.mult).then_inc(S["om"], 1)

            def latents(p):
                for k, done in ((0, "h3a"), (1, "h3")):
                    for hf, t1 in two(p):
                        dve.wait_ge(S["h3a" if k else "psum_out"], t1)
                        dve.scalar_tensor_tensor(h_of(p, hf), PS[2 + hf][0:P, D * k:D * k + D].unsqueeze(1),
                                                 small[:, 16 + k:17 + k], h_of(p, hf), ALU.mult, ALU.add).then_inc(S[done], 1)
                stats_of(p, 3)

            def choose(p):
                for hf, t1 in two(p):
                    wait_apart(dve, S["psum_rt"], t1)
                    dve.max(rmx[:, hf, :], PS[2 + hf][0:P, 0:E]).then_inc(S["rtop"], 1)
                for hf, t1 in two(p):
                    wait_apart(dve, S["rtop"], t1)
                    dve.max_index(ridx[:, hf, :], rmx[:, hf, :], PS[2 + hf][0:P, 0:E]).then_inc(S["ridx"], 1)
                for hf, t1 in two(p):
                    dve.wait_ge(S["ridx"], t1)
                    dve.tensor_copy(id_all[:, bass.ds(2 * p + hf, 1), :], ridx[:, hf:hf + 1, 0:2])
                    dve.tensor_copy(lg_all[:, bass.ds(2 * p + hf, 1), :], PS[2 + hf][0:P, 0:E].unsqueeze(1)).then_inc(S["rlg"], 1)

            def round_(i, A, C):
                b, cp = two(i), two(i - 1)
                for hf, t1 in b:
                    sums(hf, t1, 0, sqq, "sqq")
                if A:
                    embed(i + 1)
                    norm(i + 1, 0)
                sums(*b[0], 12, sqk, "sqk")
                normed(i, 0, "qn")
                sums(*b[1], 12, sqk, "sqk")
                dve.wait_ge(S["ssk"], 2 * i + 2)
                rsqrt(ss[:, :, 12:24], ss[:, :, 12:24], (2, 12), "rsk", i, 1.0 / HD0)
                if A:
                    values(i + 1)
                normed(i, 12, "kn")
                if A:
                    decay(i + 1)
                    retained(i + 1)
                gate_logits(i)
                if A:
                    stats_of(i + 1, 1)
                pick(i)
                if A:
                    norm(i + 1, 1)
                if C:
                    rotary(i - 1)
                keys(i)
                if C:
                    kv_mean(i - 1)
                softmaxes(b, 0, pr, nmax, 0, "psum_sa", "nma", "suba")
                if C:
                    softmaxes(cp, 2, pr1, nmax1, 0, "psum_s1a", "nm1a", "sub1a")
                softmaxes(b, 0, pr, nmax, 1, "psum_sb", "nmb", "subb")
                if C:
                    softmaxes(cp, 2, pr1, nmax1, 1, "psum_s1b", "nm1b", "sub1b")
                    kv_rstd(i - 1)
                gate(i)
                for hf, t1 in b:
                    heads(i, hf, t1)
                if C:
                    attended(i - 1)
                    latents(i - 1)
                    norm(i - 1, 3)
                projected(i)
                norm(i, 2)
                if C:
                    choose(i - 1)

            def ahead(p):
                embed(p)
                norm(p, 0)
                values(p)
                decay(p)
                retained(p)
                stats_of(p, 1)
                norm(p, 1)

            def behind(p):
                rotary(p)
                kv_mean(p)
                kv_rstd(p)
                softmaxes(two(p), 2, pr1, nmax1, 0, "psum_s1a", "nm1a", "sub1a")
                softmaxes(two(p), 2, pr1, nmax1, 1, "psum_s1b", "nm1b", "sub1b")
                attended(p)
                latents(p)
                norm(p, 3)
                choose(p)

            rounds(dve, ahead, round_, behind)
            moe_vector(dve)


def kernel(**inputs):
    import concourse.bacc as bacc
    from concourse.bass_utils import run_bass_kernel_spmd

    g = {k: np.asarray(v) for k, v in inputs.items()}

    def wide(w):
        return w.reshape(2, DH2, -1).transpose(1, 0, 2)

    x = g["x"].reshape(BATCH, GRID, PATCH, GRID, PATCH * 3).transpose(0, 1, 3, 2, 4).reshape(TILES, P, PC, 128)
    arrays = {
        "x": x.transpose(0, 3, 2, 1).reshape(TILES, 128, PC * P),
        "w_tok": g["L0_tok_W"].reshape(PC, 128, D).transpose(1, 0, 2), "b_tok": g["L0_tok_b"],
        "w_ret": wide(g["L0_attn_W_qkv"]), "b_ret": g["L0_attn_b_qkv"].reshape(1, -1),
        "w_moh": wide(g["L0_ffn_qkv_w"]), "b_moh": g["L0_ffn_qkv_b"].reshape(1, -1),
        "w_gr": wide(g["L0_ffn_wg_w"]), "w_g0": wide(g["L0_ffn_wg0_w"]), "w_g1": wide(g["L0_ffn_wg1_w"]),
        "w_proj": g["L0_ffn_proj_w"].reshape(H0 // 2, 128, D).transpose(1, 0, 2), "b_proj": g["L0_ffn_proj_b"],
        "qw": g["L0_ffn_q_norm_w"].reshape(-1, 1), "qb": g["L0_ffn_q_norm_b"].reshape(-1, 1),
        "kw": g["L0_ffn_k_norm_w"].reshape(-1, 1), "kb": g["L0_ffn_k_norm_b"].reshape(-1, 1),
        "w_q1": wide(g["L1_attn_Wq"]), "w_kv1": wide(g["L1_attn_Wkv"]),
        "w_octx": wide(g["L1_attn_Wo_ctx"]), "w_olat": wide(g["L1_attn_Wo_lat"]),
        "b_octx": g["L1_attn_bo_ctx"].reshape(1, -1), "b_olat": g["L1_attn_bo_lat"].reshape(1, -1),
        "ln_g": g["L1_attn_ln_g"], "ln_b": g["L1_attn_ln_b"], "w_rt": wide(g["L1_ffn_Wr"].T),
        "w1": g["L1_ffn_W1"].reshape(E, 2, DH2, FF).transpose(0, 2, 1, 3).reshape(E, DH2, 2 * FF),
        "b1": g["L1_ffn_b1"].reshape(E, 1, FF),
        "w2": g["L1_ffn_W2"].reshape(E, FC, 128, D).transpose(0, 2, 1, 3).reshape(E, 128, FC * D),
        "b2": g["L1_ffn_b2"].reshape(E, 1, D),
    }
    arrays.update(constants())
    arrays = {f"in_{k}": np.ascontiguousarray(v) for k, v in arrays.items()}
    nc = bacc.Bacc("TRN2", target_bir_lowering=False, num_devices=1)
    aps = {k[3:]: nc.dram_tensor(k, v.shape, mybir.dt.from_np(v.dtype), kind="ExternalInput").ap()
           for k, v in arrays.items()}
    out = nc.dram_tensor("out", (TOKENS + ET, D), mybir.dt.float32, kind="ExternalOutput").ap()
    vit_tower(nc, aps, out)
    return run_bass_kernel_spmd(nc, [arrays], core_ids=[0]).results[0]["out"][:TOKENS].reshape(BATCH, N_TOK, D)
```

```python
from contextlib import ExitStack

import numpy as np

import concourse.bass as bass
from concourse import mybir

BATCH, PATCH, GRID = 32, 16, 7
N_TOK = GRID * GRID
D = 192
DH2 = D // 2
PD = PATCH * PATCH * 3
PC = PD // 128
P = 2 * N_TOK
TILES = BATCH // 2
PAIRS = TILES // 2
H0, HD0 = 12, 64
RH, SH = 10, 2
H1, HD1, PAD1 = 12, 16, 32
LATENT = 32
CTX = N_TOK - LATENT
E, FF, FC = 16, 768, 6
EPS = 1e-5
HALF6 = 6 * P
BANK = 512
BIG = -1e30
RS = 6
RSQ = 12

ET = 128
ETILES = (2 * BATCH * N_TOK - E) // ET + E
ETILES += -ETILES % 4
TOKENS = BATCH * N_TOK
ROW = D + 2
MAXT = -(-BATCH * N_TOK // ET)
REGION = TOKENS + ET
PAD_ACT = 10
SPARE = E * REGION
C_CTX, C_TILE, C_MULT, C_TOKEN = 16, 18, 18 + ETILES, 18 + ETILES + MAXT
C_REGION = C_TOKEN + TILES


def constants():
    f = np.float32
    r = np.arange(P)
    n, img = r % N_TOK, r // N_TOK
    diff = (n[:, None] - n[None, :]).astype(f)
    ok = (img[:, None] == img[None, :]) & (diff >= 0)
    decay = np.where(ok, f(0.99) ** np.where(ok, diff, 0).astype(f), f(0)).astype(f)
    retT = np.ascontiguousarray((decay / np.sqrt(f(D))).T.astype(f))
    inv = (1.0 / 10000.0 ** (np.arange(0, HD1, 2, dtype=f) / f(HD1))).astype(f)
    ang = n.astype(f)[:, None] * inv[None, :]
    ang = np.concatenate([ang, ang], -1)
    cos, sin = np.cos(ang).astype(f), np.sin(ang).astype(f)
    sin[:, :HD1 // 2] *= -1
    q = f(HD1 ** -0.5)
    rope = np.stack([np.concatenate([np.tile(cos * q, (1, H1)), np.tile(cos, (1, H1))], 1),
                     np.concatenate([np.tile(sin * q, (1, H1)), np.tile(sin, (1, H1))], 1)], 1)
    imgq = np.stack([img == 0, img == 1]).astype(f)
    imgk = np.stack([img == 1, img == 0]).astype(f) * f(BIG)
    ctx = n < CTX
    grpq = np.stack([(img == i) & (ctx == c) for i in (0, 1) for c in (True, False)]).astype(f)
    grpk = np.stack([(img != i) | (c & ~ctx) for i in (0, 1) for c in (True, False)]).astype(f) * f(BIG)
    m0, m1 = np.zeros((128, 4 * P), f), np.zeros((128, 4 * P), f)
    for r0 in range(0, 128, HD0):
        m0[r0:r0 + 2] = np.concatenate([imgq] + [imgk] * 3, 1)
    for r0 in range(0, 128, PAD1):
        m1[r0:r0 + 4] = np.concatenate([grpq] + [grpk] * 3, 1)
    small = np.zeros((P, C_REGION + E), f)
    small[:, :16] = np.arange(16)
    small[:, C_CTX] = ctx
    small[:, C_CTX + 1] = ~ctx
    small[:, C_TILE:C_MULT] = np.arange(ETILES)
    small[:, C_MULT:C_TOKEN] = np.arange(MAXT) * ET
    small[:, C_TOKEN:C_REGION] = np.arange(TILES) * P + r[:, None]
    small[:, C_REGION:] = np.arange(E) * REGION
    return {"ident": np.eye(128, dtype=f), "retT": retT, "rope": rope.reshape(P, -1).astype(f),
            "mask0": m0.astype(f), "mask1": m1.astype(f), "small": small,
            "before": (r[:, None] < r[None, :]).astype(f),
            "pad_row": (TOKENS + np.arange(ET, dtype=f))[:, None]}


def vit_tower(nc, a, out):
    F32, I32, U32, BF16 = mybir.dt.float32, mybir.dt.int32, mybir.dt.uint32, mybir.dt.bfloat16
    ALU, ACT, AX = mybir.AluOpType, mybir.ActivationFunctionType, mybir.AxisListType
    ctx = ExitStack()
    with ctx:
        def sb(name, shape, dt=F32):
            return ctx.enter_context(nc.sbuf_tensor(name, shape, dt))

        def sem(name):
            return ctx.enter_context(nc.semaphore(name))

        rows_dram = nc.dram_tensor("expert_rows", [SPARE + ET, ROW], F32, kind="Internal").ap()

        ident = sb("ident", [128, 128])
        retT = sb("retT", [P, P])
        rope = sb("rope", [P, 4 * D])
        mask0f, mask0 = sb("mask0f", [128, 4 * P]), sb("mask0", [128, 4 * P], BF16)
        mask1f, mask1 = sb("mask1f", [128, 4 * P]), sb("mask1", [128, 4 * P], BF16)
        small = sb("small", [P, C_REGION + E])
        pad_row = sb("pad_row", [ET, 1])
        before = sb("before", [P, P])
        w_tok = sb("w_tok", [128, PC, D])
        b_tok = sb("b_tok", [P, D])
        w_ret = sb("w_ret", [DH2 + 1, 2, 3 * D])
        w_moh = sb("w_moh", [128, 2, 3 * H0 * HD0])
        w_gate = sb("w_gate", [DH2, 2, RH + 4])
        w_proj = sb("w_proj", [128, H0 // 2, D])
        b_proj = sb("b_proj", [P, D])
        qk_affine = sb("qk_affine", [128, 4])
        w_l1 = sb("w_l1", [DH2, 2, 2 * D])
        w_out = sb("w_out", [DH2 + 1, 2, 2 * D])
        ln_gb = sb("ln_gb", [P, 2, HD1])
        w_rt = sb("w_rt", [DH2, 2, E])
        ones = sb("ones", [P, P])
        neg_half = sb("neg_half", [P, 24])
        wmean = sb("wmean", [DH2 + 1, 2, 24])
        blank = sb("blank", [ET, ROW])

        x_in = sb("x_in", [128, 2, PC * P])
        hb = sb("hb", [P, 2, D])
        xn = [sb(f"xn{k}", [P, 2, D]) for k in range(4)]
        stats = sb("stats", [P, 2, 6])
        mv = [sb(f"mv{k}", [P, 2, 2]) for k in range(4)]
        rstd = [sb(f"rstd{k}", [P, 2, 1]) for k in range(4)]
        xnT = [sb(f"xnT{k}", [128 if k == 1 else DH2 + 1, 2, 2 * P]) for k in range(3)]
        xnT += [xnT[2]]
        qkT0 = sb("qkT0", [DH2, 2, 4 * P])
        v0 = sb("v0", [P, 2, D])
        pT0 = sb("pT0", [P, 2, P])
        ss = sb("ss", [P, 2, 24])
        rs = sb("rs", [P, 3, 24])
        rs_bits = sb("rs_bits", [P, 24], I32)
        qn = sb("qn", [P, 2, 1536])
        qT = sb("qT", [128, 2, 6 * P])
        kT = sb("kT", [128, 2, 6 * P])
        v_aug = sb("v_aug", [P, 2, H0 * (HD0 + 1)])
        nmax = sb("nmax", [P, 2, H0])
        pr = sb("pr", [128, 2, H0 * P])
        pT = sb("pT", [P, 2, H0 * P])
        sqq, sqk = pr[0:P, :, 0:768], pT[:, :, 0:768]
        fac = sb("fac", [P, 2, H0])
        o = sb("o", [P, 2, H0 * HD0])
        oT = qT
        qk1 = sb("qk1", [P, 2, 2 * H1 * PAD1])
        qT1 = sb("qT1", [128, 2, 3 * P])
        kT1 = sb("kT1", [128, 2, 3 * P])
        lsum = sb("lsum", [P, 2, H1])
        lc = sb("lc", [P, 2, D])
        lsq = sb("lsq", [P, 2, D])
        lr = sb("lr", [P, 2, H1])
        v1_aug = sb("v1_aug", [P, 2, H1 * (HD1 + 1)])
        nmax1 = sb("nmax1", [P, 2, H0])
        pr1 = sb("pr1", [128, 2, H1 * P])
        pT1 = sb("pT1", [P, 2, H1 * P])
        ropa, ropb = pr1[0:P, :, 0:2 * D], pr1[0:P, :, 2 * D:4 * D]
        fac1 = sb("fac1", [P, 2, H1])
        om = sb("om", [P, 2, D])
        omT = sb("omT", [DH2 + 1, 2, 2 * P])
        gl = sb("gl", [P, 2, RH + 4])
        gmx = sb("gmx", [P, 2, 8])
        gidx = sb("gidx", [P, 2, 8], U32)
        gidf = sb("gidf", [P, 2, 2])
        gm2 = sb("gm2", [P, 4])
        gsum = sb("gsum", [P, 2, 4])
        ge = sb("ge", [P, 2, RH + 4])
        gmask = sb("gmask", [P, 2, RH])
        gden = sb("gden", [P, 2, 2])
        gates = sb("gates", [P, 2, H0])
        rmx = sb("rmx", [P, 2, 8])
        ridx = sb("ridx", [P, 2, 8], U32)

        idf = sb("idf", [P, 2, 2])
        oh = sb("oh", [P, 2, 2 * E])
        both = sb("both", [P, 2 * E])
        lgm = sb("lgm", [P, 2, E + 1])
        lge = sb("lge", [P, 2, E + 1])
        rsum = sb("rsum", [P, 2])
        base = sb("base", [P, 3, E])
        row_of = sb("row_of", [P, 2, E])
        prod = sb("prod", [P, 2, 2 * E])
        slot_f = sb("slot_f", [P, 2, 2])
        slot_u = sb("slot_u", [P, 2, 2], U32)
        xrow = sb("xrow", [P, 2, 2, ROW])
        o_flat = o[:, :, :].rearrange("p a b -> p (a b)")
        cmp = o_flat[:, 0:E * max(MAXT, ETILES)]
        tcum = sb("tcum", [P, 3, E])
        skip = sb("skip", [1, E])
        tile_f = sb("tile_f", [1, 2, ETILES])
        eid = sb("eid", [1, ETILES], I32)
        row0 = sb("row0", [1, ETILES], I32)
        pad0 = sb("pad0", [1, E], I32)
        xe = sb("xe", [ET, 4, ROW])
        xeT = sb("xeT", [DH2 + 1, 4, 2 * ET])
        b2 = sb("b2", [ET, 4, D])
        w1 = [w_moh[:, :, :].rearrange("p a b -> p (a b)")[:, 2 * FF * k:2 * FF * (k + 1)] for k in range(3)] + \
             [pT1[:, :, :].rearrange("p a b -> p (a b)")[0:DH2 + 1, 0:2 * FF]]
        pr2, spare = pr1[:, :, :].rearrange("p a b -> p (a b)"), FC * D
        w2 = [pr2[:, 0:spare], pr2[:, spare:2 * spare],
              x_in[:, :, :].rearrange("p a b -> p (a b)")[:, 0:spare], qT[:, :, :].rearrange("p a b -> p (a b)")[:, 0:spare]]
        hT = pr
        ye = sb("ye", [ET, 2, D])
        yb = sb("yb", [ET, 2, D])
        token = sb("token", [ET, 2, 1], U32)

        h_all = sb("h_all", [P, TILES, D])

        PS = [ctx.enter_context(nc.psum_tensor(f"slot{i}", [128, 2 * BANK], F32)) for i in range(4)]

        s_w, s_center = sem("constants_loaded"), sem("weight_centering")
        s_wtok, s_wret, s_wmoh = sem("embedding_loaded"), sem("retention_loaded"), sem("head_weights_loaded")
        s_setup_p, s_setup_v = sem("pool_setup"), sem("vector_setup")
        s_apart = sem("waits_apart")
        s_zero, s_zeros = sem("expert_rows_zeroed"), sem("zeros_ready")
        s_x = [sem(f"patches_loaded{i}") for i in range(2)]
        names = ("psum_tok psum_xnT0 psum_qkv0 psum_s0 psum_o0 psum_xnT1 psum_v psum_q psum_k psum_qT psum_kT "
                 "psum_sa psum_sb psum_pTa psum_pTb psum_pv psum_oT psum_proj psum_xnT2 psum_qkv1 psum_qkT1 "
                 "psum_s1a psum_s1b psum_p1Ta psum_p1Tb psum_pv1 psum_omT psum_out psum_xnT3 psum_rt "
                 "h0 stat0 rs0 xn0 xnT0 qkT0 v0 pT0 "
                 "h1 stat1 rs1 xn1 xnT1 hb v sqq sqk gl gpick gsub gexp gstep gates "
                 "ssq qvar rsq ssk rsk qn kn qT kT nma suba ea nmb subb eb pTa pTb fac o oT h2 stat2 rs2 xn2 xnT2 "
                 "rope qk1 lsum lmean lc lsq lss lvar lrsq lv v1 q1T nm1a sub1a e1a nm1b sub1b e1b "
                 "p1Ta p1Tb rden om omT h3a h3 stat3 rs3 xn3 base xnT3 rtop rlg ridx rstep both psum_rank rank lge slots rgate sent xrow").split()
        S = {n: sem(n) for n in names}

        def wait_apart(eng, sm, value):
            eng.wait_ge(sm, value)
            eng.sem_inc(s_apart, 1)

        def v3(ap, k):
            return ap.rearrange("p (a b) -> p a b", a=k)

        def banks(ps, n, used):
            return ps[0:n, :].rearrange("p (b c) -> p b c", b=2)[:, :, 0:used]


        s_route, s_eid, s_row0, s_pad0 = sem("tiling_step"), sem("expert_of_tile"), sem("row_of_tile"), sem("padding_starts")
        s_pad, s_pad2 = sem("padding_stored"), sem("last_padding_stored")
        s_scat = sem("rows_scattered")
        s_rows = [sem(f"expert_rows_loaded{i}") for i in range(4)]
        s_wts = [sem(f"expert_weights_loaded{i}") for i in range(4)]
        s_base, s_yb = sem("output_base_stored"), sem("biased_result_ready")
        s_xeT, s_xe, s_up, s_hT = sem("psum_xeT"), sem("xeT_ready"), sem("psum_hidden"), sem("hidden_ready")
        s_dn, s_y = sem("psum_expert_out"), sem("expert_out_ready")
        s_yfree, s_add = sem("result_buffer_free"), sem("results_added")

        def moe_sync(sp):
            out_rows = out[0:TOKENS, :].rearrange("(t p) d -> p t d", p=P)
            sp.wait_ge(S["base"], TILES)
            sp.dma_start(out_rows, h_all[:, :, :]).then_inc(s_base, 16)

            def weights(j, b):
                e = sp.value_load(eid[0:1, bass.ds(j, 1)], min_val=0, max_val=E - 1)
                for dst, src in ((w1[b][0:DH2, :], a["w1"]), (w1[b][DH2:DH2 + 1, 0:FF], a["b1"]), (w2[b], a["w2"])):
                    sp.dma_start(dst, src[bass.ds(e, 1)].rearrange("o p c -> (o p) c")).then_inc(s_wts[b], 16)
                sp.dma_start(b2[:, b, :], a["b2"][bass.ds(e, 1)].rearrange("o p c -> (o p) c").broadcast_to([ET, D]))\
                    .then_inc(s_wts[b], 16)

            def rows(j, b):
                row = sp.value_load(row0[0:1, bass.ds(j, 1)], min_val=0, max_val=SPARE)
                sp.dma_start(xe[:, b, :], rows_dram[bass.ds(row, ET), :]).then_inc(s_rows[b], 16)

            sp.wait_ge(s_eid, 1)
            for b in range(2):
                weights(b, b)
            sp.wait_ge(s_scat, 16 * 2 * TILES)
            sp.wait_ge(s_pad, 16 * PAD_ACT)
            sp.wait_ge(s_pad2, 16 * (E - PAD_ACT))
            sp.wait_ge(s_zero, 16 * 2)
            sp.wait_ge(s_row0, 1)
            rows(0, 0)
            rows(1, 1)
            weights(2, 2)
            rows(2, 2)
            rows(3, 3)
            weights(3, 3)
            with sp.Fori(1, ETILES // 4) as i:
                for b in (0, 2):
                    for n in (b, b + 1):
                        sp.wait_ge(s_y, 4 * i + n - 3 + 2)
                        rows(4 * i + n, n)
                    for n in (b, b + 1):
                        weights(4 * i + n, n)

        def moe_tensor(pe):
            def turn(b, loads_done):
                pe.wait_ge(s_rows[b], loads_done)
                for c in range(2):
                    mm = pe.transpose(PS[b % 2][0:DH2, ET * c:ET * c + ET], xe[:, b, DH2 * c:DH2 * c + DH2], ident[:, :])
                mm.then_inc(s_xeT, 1)

            def hidden(b, i, t1):
                pe.wait_ge(s_wts[b], 64 * i + 64)
                pe.wait_ge(s_xe, t1)
                for f in range(FC):
                    for c in range(2):
                        k = DH2 + 1 - c
                        mm = pe.matmul(PS[2 + b % 2][:, ET * f:ET * f + ET],
                                       w1[b][0:k, c * FF + 128 * f:c * FF + 128 * f + 128],
                                       xeT[0:k, b, ET * c:ET * c + ET], start=c == 0, stop=c == 1)
                mm.then_inc(s_up, 1)

            def result(b, t1):
                pe.wait_ge(s_hT, t1)
                pe.wait_ge(s_y, t1)
                for f in range(FC):
                    mm = pe.matmul(PS[b % 2][:, BANK:BANK + D], hT[:, b % 2, ET * f:ET * f + ET],
                                   w2[b][:, f * D:f * D + D], start=f == 0, stop=f == FC - 1)
                mm.then_inc(s_dn, 1)

            def four(i, last):
                for b in (0, 2):
                    hidden(b, i, 4 * i + b + 1)
                    hidden(b + 1, i, 4 * i + b + 2)
                    if not (last and b == 2):
                        for n in ((b + 2) % 4, (b + 3) % 4):
                            turn(n, 16 * i + (16 if b == 0 else 32))
                    result(b, 4 * i + b + 1)
                    result(b + 1, 4 * i + b + 2)

            turn(0, 16)
            turn(1, 16)
            with pe.Fori(0, ETILES // 4 - 1) as i:
                four(i, False)
            four(ETILES // 4 - 1, True)

        def moe_scalar(act):
            act.wait_ge(s_pad0, 1)
            act.wait_ge(s_zeros, 2)
            for e in range(PAD_ACT):
                row = act.value_load(pad0[0:1, e:e + 1], min_val=0, max_val=SPARE - ET)
                act.dma_start(rows_dram[bass.ds(row, ET), :], blank[:, :]).then_inc(s_pad, 16)
            with act.Fori(0, ETILES // 2) as i:
                for hf, t1 in [(0, 2 * i + 1), (1, 2 * i + 2)]:
                    act.wait_ge(s_up, t1)
                    act.activation(hT[:, hf, 0:FF], PS[2 + hf][:, 0:FF], ACT.Gelu).then_inc(s_hT, 1)

        def moe_gpsimd(pool):
            pool.wait_ge(s_pad0, 1)
            for e in range(PAD_ACT, E):
                row = pool.value_load(pad0[0:1, e:e + 1], min_val=0, max_val=SPARE - ET)
                pool.dma_start(rows_dram[bass.ds(row, ET), :], blank[:, :]).then_inc(s_pad2, 16)
            pool.wait_ge(s_base, 16)
            pool.sem_inc(s_yfree, 2)
            with pool.Fori(0, ETILES // 2) as i:
                for hf, t1 in [(0, 2 * i + 1), (1, 2 * i + 2)]:
                    wait_apart(pool, s_y, t1 + 2)
                    pool.indirect_dma_start(out=out, out_offset=bass.IndirectOffsetOnAxis(ap=token[:, hf, 0:1], axis=0),
                                            in_=ye[:, hf, :], in_offset=None, compute_op=ALU.add).then_inc(s_add, 16)
                    pool.wait_ge(s_add, 32 * i + 16 * hf + 16)
                    pool.sem_inc(s_yfree, 1)

        def moe_vector(dve):
            steps = [0]

            def after(ins):
                steps[0] += 1
                ins.then_inc(s_route, 1)
                dve.wait_ge(s_route, steps[0])

            dve.wait_ge(S["rstep"], RS * PAIRS)
            dve.tensor_copy(pad0[:, :], base[0:1, 0, :]).then_inc(s_pad0, 1)
            after(dve.tensor_tensor(tcum[:, 2, :], base[:, 0, :], small[:, C_REGION:C_REGION + E], ALU.subtract))
            c3 = v3(cmp[:, 0:E * MAXT], E)
            after(dve.tensor_tensor(c3, tcum[:, 2, :].unsqueeze(2).broadcast_to([P, E, MAXT]),
                                    small[:, C_MULT:C_MULT + MAXT].unsqueeze(1).broadcast_to([P, E, MAXT]), ALU.is_gt))
            after(dve.tensor_reduce(tcum[:, 0, :], c3, AX.X, ALU.add))
            dve.tensor_scalar(skip[:, :], tcum[0:1, 0, :], float(-ET), float(REGION), ALU.mult, ALU.add)
            tsrc, tdst, s = tcum[:, 0, :], 1, 1
            while s < E:
                d = tcum[:, tdst, :]
                dve.tensor_copy(d[:, 0:s], tsrc[:, 0:s])
                after(dve.tensor_tensor(d[:, s:E], tsrc[:, s:E], tsrc[:, 0:E - s], ALU.add))
                tsrc, tdst, s = d, 3 - tdst, 2 * s
            e3 = v3(cmp[0:1, 0:ETILES * E], ETILES)
            after(dve.tensor_tensor(e3, small[0:1, C_TILE:C_TILE + ETILES].unsqueeze(2).broadcast_to([1, ETILES, E]),
                                    tsrc[0:1, :].unsqueeze(1).broadcast_to([1, ETILES, E]), ALU.is_ge))
            after(dve.tensor_reduce(tile_f[:, 0, :], e3, AX.X, ALU.add))
            dve.tensor_scalar(eid[:, :], tile_f[:, 0, :], float(E - 1), None, ALU.min).then_inc(s_eid, 1)
            after(dve.tensor_tensor(e3, e3, skip[:, :].unsqueeze(1).broadcast_to([1, ETILES, E]), ALU.mult))
            after(dve.tensor_reduce(tile_f[:, 1, :], e3, AX.X, ALU.add))
            after(dve.scalar_tensor_tensor(tile_f[:, 1, :], small[0:1, C_TILE:C_TILE + ETILES], float(ET), tile_f[:, 1, :],
                                           ALU.mult, ALU.add))
            dve.tensor_scalar(row0[:, :], tile_f[:, 1, :], float(SPARE), None, ALU.min).then_inc(s_row0, 1)

            dve.sem_inc(s_y, 2)

            def turned(b, t1):
                dve.wait_ge(s_xeT, t1)
                dve.tensor_copy(xeT[0:DH2, b, :], PS[b % 2][0:DH2, 0:2 * ET]).then_inc(s_xe, 1)

            def result(b, t1):
                dve.wait_ge(s_dn, t1)
                dve.wait_ge(s_yfree, t1)
                dve.tensor_tensor(yb[:, b % 2, :], PS[b % 2][:, BANK:BANK + D], b2[:, b, :], ALU.add).then_inc(s_yb, 1)
                dve.tensor_copy(token[:, b % 2, :], xe[:, b, D:D + 1])
                dve.wait_ge(s_yb, t1)
                dve.tensor_scalar(ye[:, b % 2, :], yb[:, b % 2, :], xe[:, b, D + 1:D + 2], None, ALU.mult).then_inc(s_y, 1)

            def four(i, last):
                for b in (0, 2):
                    if not (last and b == 2):
                        for n in (b + 2, b + 3):
                            turned(n % 4, 4 * i + n + 1)
                    result(b, 4 * i + b + 1)
                    result(b + 1, 4 * i + b + 2)

            turned(0, 1)
            turned(1, 2)
            with dve.Fori(0, ETILES // 4 - 1) as i:
                four(i, False)
            four(ETILES // 4 - 1, True)

        block = ctx.enter_context(nc.Block())

        def head0_at(g, b, j):
            return 6 * g + 2 * j + b

        def head1_at(g, b, j):
            return 4 * j + 2 * g + b

        place0 = {head0_at(g, b, j): 6 * g + 3 * b + j for g in range(2) for b in range(2) for j in range(3)}
        place1 = {head1_at(g, b, j): 6 * g + 3 * b + j for g in range(2) for b in range(2) for j in range(3)}

        loads_tok = [(w_tok[:, :, :], a["w_tok"]), (b_tok[:, :], a["b_tok"].partition_broadcast(P))]
        loads_ret = [(ident[:, :], a["ident"]), (w_ret[0:DH2, :, :], a["w_ret"]), (w_ret[DH2:DH2 + 1, 0, :], a["b_ret"]),
                     (retT[:, :], a["retT"])]
        loads_moh = [(w_moh[0:DH2, :, :], a["w_moh"]), (w_moh[DH2:DH2 + 1, 0, :], a["b_moh"])]
        loads = [(small[:, :], a["small"]),
                 (mask0f[:, :], a["mask0"]), (mask1f[:, :], a["mask1"]), (rope[:, :], a["rope"]),
                 (pad_row[:, :], a["pad_row"]),
                 (w_gate[:, :, 0:RH], a["w_gr"]), (w_gate[:, :, RH:RH + 2], a["w_g0"]),
                 (w_gate[:, :, RH + 2:RH + 4], a["w_g1"]),
                 (w_proj[:, :, :], a["w_proj"]), (b_proj[:, :], a["b_proj"].partition_broadcast(P)),
                 (w_l1[:, :, 0:D], a["w_q1"]), (w_l1[:, :, D:2 * D], a["w_kv1"]),
                 (w_out[0:DH2, :, 0:D], a["w_octx"]), (w_out[0:DH2, :, D:2 * D], a["w_olat"]),
                 (w_out[DH2:DH2 + 1, 0, 0:D], a["b_octx"]), (w_out[DH2:DH2 + 1, 0, D:2 * D], a["b_olat"]),
                 (ln_gb[:, 0, :], a["ln_g"].partition_broadcast(P)),
                 (ln_gb[:, 1, :], a["ln_b"].partition_broadcast(P)),
                 (w_rt[:, :, :], a["w_rt"]), (before[:, :], a["before"])]
        for col, name in enumerate(("qw", "qb", "kw", "kb")):
            for k in range(2):
                loads.append((qk_affine[64 * k:64 * k + 64, col:col + 1], a[name]))

        def two(p):
            return [(0, 2 * p + 1), (1, 2 * p + 2)]

        def turned_x(k, hf):
            c0 = BANK if k else 0
            return PS[2 + hf][:, c0:c0 + 2 * P]

        def logits(hf):
            return PS[2 + hf][0:P, BANK:BANK + E]

        def rounds(eng, ahead, constants, round_, behind):
            ahead(0)
            constants()
            round_(0, True, False, False)
            round_(1, True, True, False)
            with eng.Fori(2, PAIRS - 1) as i:
                round_(i, True, True, True)
            round_(PAIRS - 1, False, True, True)
            behind(PAIRS - 1)

        @block.sync
        def _(sp):
            for hf in range(2):
                sp.dma_start(x_in[:, hf, :], a["x"][hf]).then_inc(s_x[hf], 16)
            for batch, done in ((loads_tok, s_wtok), (loads_ret, s_wret), (loads_moh, s_wmoh), (loads, s_w)):
                for n, (dst, src) in enumerate(batch):
                    if done is s_wmoh and n == 1:
                        sp.wait_ge(s_center, 1)
                    sp.dma_start(dst, src).then_inc(done, 16)
            sp.wait_ge(s_zeros, 2)
            sp.dma_start(rows_dram[SPARE:SPARE + ET, :], blank[:, :]).then_inc(s_zero, 16)
            sp.dma_start(out[TOKENS:TOKENS + ET, :], blank[:, 0:D]).then_inc(s_zero, 16)
            with sp.Fori(1, PAIRS) as i:
                for hf in range(2):
                    sp.wait_ge(S["psum_tok"], 2 * i + hf - 1)
                    sp.dma_start(x_in[:, hf, :], a["x"][bass.ds(2 * i + hf, 1)].rearrange("o p c -> (o p) c")).then_inc(s_x[hf], 16)
            moe_sync(sp)

        @block.tensor
        def _(pe):
            def constants():
                pe.wait_ge(s_w, 16 * len(loads))
                pe.wait_ge(s_setup_p, 1)
                pe.wait_ge(s_setup_v, 3)

            def transposes(ps, src, n, w, three=True):
                for c in range(n):
                    c0 = (c // 3) * BANK + (c % 3) * P if three else c * P
                    mm = pe.transpose(ps[0:w, c0:c0 + P], src[:, w * c:w * (c + 1)], ident[0:P, 0:P])
                return mm

            def over_width(dst, lhsT, hf, rhs, rows0=DH2 + 1, rows1=DH2):
                for c in range(2):
                    k = rows0 if c == 0 else rows1
                    mm = pe.matmul(dst, lhsT[0:k, hf, c * P:(c + 1) * P], rhs(c, k), start=c == 0, stop=c == 1)
                return mm

            def scores(ps, hf, g, rows, head_at, mask, q, k):
                for b in range(2):
                    for j in range(3):
                        hd = head_at(g, b, j)
                        r0, col = rows * (hd % (128 // rows)), hd // (128 // rows) * P
                        pe.matmul(ps[0:P, b * BANK + j * P:b * BANK + j * P + P],
                                  q[r0:r0 + rows, hf, col:col + P], k[r0:r0 + rows, hf, col:col + P],
                                  start=j == 0, stop=False, skip_group_check=True)
                    mm = pe.matmul(ps[0:P, b * BANK:b * BANK + 3 * P], mask[r0:r0 + rows, 0:P],
                                   mask[r0:r0 + rows, P:4 * P], start=False, stop=True, skip_group_check=True)
                return mm

            def tok(p, hf, t1):
                pe.wait_ge(s_x[hf], 16 * p + 16)
                for c in range(PC):
                    mm = pe.matmul(PS[2 + hf][0:P, 0:D], x_in[:, hf, c * P:(c + 1) * P], w_tok[:, c, :],
                                   start=c == 0, stop=c == PC - 1)
                mm.then_inc(S["psum_tok"], 1)

            def turn_x(k, hf, t1):
                pe.wait_ge(S[f"xn{k}"], t1)
                transposes(turned_x(k, hf), xn[k][:, hf, :], 2, DH2, False).then_inc(S[f"psum_xnT{k}"], 1)

            def qkv0(hf, t1, x2=None):
                pe.wait_ge(S["xnT0"], t1)
                ps = PS[2 + hf]
                for m in range(4):
                    for c in range(2):
                        k = DH2 + 1 - c
                        pe.matmul(ps[0:DH2, P * m:P * m + P], w_ret[0:k, c, DH2 * m:DH2 * m + DH2],
                                  xnT[0][0:k, hf, c * P:(c + 1) * P], start=c == 0, stop=c == 1)
                if x2 is not None:
                    pe.wait_ge(S["xnT2"], x2)
                over_width(ps[0:P, BANK:BANK + D], xnT[0], hf, lambda c, k: w_ret[0:k, c, 2 * D:3 * D])\
                    .then_inc(S["psum_qkv0"], 1)

            def s0(hf, t1):
                pe.wait_ge(S["qkT0"], t1)
                pe.wait_ge(S["v0"], t1)
                for c in range(2):
                    mm = pe.matmul(PS[2 + hf][0:P, 0:P], qkT0[:, hf, (2 + c) * P:(3 + c) * P],
                                   qkT0[:, hf, c * P:(c + 1) * P], start=c == 0, stop=c == 1)
                mm.then_inc(S["psum_s0"], 1)

            def o0(hf, t1):
                pe.wait_ge(S["pT0"], t1)
                pe.matmul(PS[2 + hf][0:P, 0:D], pT0[:, hf, :], v0[:, hf, :], start=True, stop=True)\
                    .then_inc(S["psum_o0"], 1)

            def wide(hf, part, name):
                for b in range(2):
                    c0 = part * H0 * HD0 + b * 384
                    mm = over_width(PS[hf][0:P, b * BANK:b * BANK + 384], xnT[1], hf,
                                    lambda c, k: w_moh[0:k, c, c0:c0 + 384], 128, 128)
                if part == 2:
                    mm = over_width(PS[hf][0:P, BANK + 384:BANK + 384 + RH + 4], xnT[1], hf,
                                    lambda c, k: w_gate[0:k, c, :], DH2)
                mm.then_inc(S[name], 1)

            def q(hf, t1):
                pe.wait_ge(S["xnT1"], t1)
                pe.wait_ge(S["h2"], t1)
                wide(hf, 0, "psum_q")

            def k(hf, t1):
                pe.wait_ge(S["sqq"], t1)
                wide(hf, 1, "psum_k")

            def v(hf, t1):
                pe.wait_ge(S["sqk"], t1)
                wide(hf, 2, "psum_v")

            def turn_heads(src, n0, ready, free, name, hf, t1):
                pe.wait_ge(S[ready], t1)
                pe.wait_ge(S[free], t1)
                transposes(PS[hf], src[:, hf, n0:n0 + 768], 6, 128).then_inc(S[name], 1)

            def sab(g, hf, t1):
                pe.wait_ge(S["pTa" if g else "kT"], t1)
                pe.wait_ge(S["qT"], t1)
                scores(PS[hf], hf, g, HD0, head0_at, mask0, qT, kT).then_inc(S["psum_sb" if g else "psum_sa"], 1)

            def turn_p(g, hf, t1, k1):
                pe.wait_ge(S[("e1b" if g else "e1a") if k1 else ("eb" if g else "ea")], t1)
                if k1:
                    pe.wait_ge(S["p1Ta" if g else "sub1b"], t1)
                src = (pr1 if k1 else pr)[0:P, hf, g * HALF6:(g + 1) * HALF6]
                transposes(PS[2 + hf if k1 else hf], src, 6, P)\
                    .then_inc(S["psum_p" + ("1" if k1 else "") + ("Tb" if g else "Ta")], 1)

            def pv(hf, t1):
                pe.wait_ge(S["pTb"], t1)
                pe.wait_ge(S["v"], t1)
                for hd in range(H0):
                    c0 = (hd // 6) * BANK + (hd % 6) * (HD0 + 1)
                    mm = pe.matmul(PS[hf][0:P, c0:c0 + HD0 + 1], pT[:, hf, place0[hd] * P:(place0[hd] + 1) * P],
                                   v_aug[:, hf, hd * (HD0 + 1):(hd + 1) * (HD0 + 1)], start=True, stop=True)
                mm.then_inc(S["psum_pv"], 1)

            def turn_o(hf, t1):
                pe.wait_ge(S["o"], t1)
                transposes(PS[hf], o[:, hf, :], 6, 128).then_inc(S["psum_oT"], 1)

            def proj(hf, t1):
                pe.wait_ge(S["oT"], t1)
                for c in range(6):
                    mm = pe.matmul(PS[hf][0:P, 0:D], oT[:, hf, c * P:(c + 1) * P], w_proj[:, c, :],
                                   start=c == 0, stop=c == 5)
                mm.then_inc(S["psum_proj"], 1)

            def qkv1(hf, t1):
                pe.wait_ge(S["xnT2"], t1)
                over_width(PS[2 + hf][0:P, 0:2 * D], xnT[2], hf, lambda c, k: w_l1[0:k, c, :], DH2)\
                    .then_inc(S["psum_qkv1"], 1)

            def turn_qk1(hf, t1):
                pe.wait_ge(S["qk1"], t1)
                transposes(PS[2 + hf], qk1[:, hf, :], 6, 128).then_inc(S["psum_qkT1"], 1)

            def sab1(g, hf, t1):
                pe.wait_ge(S["sub1a" if g else "q1T"], t1)
                scores(PS[2 + hf], hf, g, PAD1, head1_at, mask1, qT1, kT1).then_inc(S["psum_s1b" if g else "psum_s1a"], 1)

            def pv1(hf, t1):
                pe.wait_ge(S["v1"], t1)
                pe.wait_ge(S["p1Tb"], t1)
                w = HD1 + 1
                for hd in range(H1):
                    mm = pe.matmul(PS[2 + hf][0:P, hd * w:(hd + 1) * w], pT1[:, hf, place1[hd] * P:(place1[hd] + 1) * P],
                                   v1_aug[:, hf, hd * w:(hd + 1) * w], start=True, stop=True)
                mm.then_inc(S["psum_pv1"], 1)

            def turn_om(hf, t1):
                pe.wait_ge(S["om"], t1)
                transposes(PS[2 + hf], om[:, hf, :], 2, DH2, False).then_inc(S["psum_omT"], 1)

            def out1(hf, t1):
                pe.wait_ge(S["omT"], t1)
                over_width(PS[2 + hf][0:P, 0:2 * D], omT, hf, lambda c, k: w_out[0:k, c, :]).then_inc(S["psum_out"], 1)

            def router(hf, t1):
                pe.wait_ge(S["xnT3"], t1)
                over_width(logits(hf), xnT[3], hf, lambda c, k: w_rt[0:k, c, :], DH2)\
                    .then_inc(S["psum_rt"], 1)

            def each(pair, fn, *args):
                for hf, t1 in pair:
                    fn(*args, hf, t1)

            def ranks(p):
                pe.wait_ge(S["both"], p + 1)
                pe.wait_ge(S["rlg"], 2 * p + 1)
                for n, lhsT in enumerate((before, ones)):
                    mm = pe.matmul(PS[2][0:P, BANK + 2 * E * n:BANK + 2 * E * (n + 1)], lhsT[:, :], both[:, :],
                                   start=True, stop=True)
                mm.then_inc(S["psum_rank"], 1)

            def turn_x2(pair, routed):
                for hf, t1 in pair:
                    if routed is not None:
                        pe.wait_ge(S["rlg"], 2 * routed + 1 + hf)
                        if hf == 0:
                            pe.wait_ge(S["rank"], routed + 1)
                    turn_x(2, hf, t1)

            def round_(i, A, C, R):
                b, an, cp, rp = two(i), two(i + 1), two(i - 1), two(i - 2)
                each(b, q)
                if R:
                    each(rp, turn_x, 3)
                if A:
                    tok(i + 1, *an[0])
                if R:
                    each(rp, router)
                if A:
                    tok(i + 1, *an[1])
                k(*b[0])
                if A:
                    each(an, turn_x, 0)
                if R:
                    ranks(i - 2)
                k(*b[1])
                if C:
                    turn_x2(cp, i - 2 if R else None)
                if A:
                    for hf, t1 in an:
                        qkv0(hf, t1, cp[hf][1] if C else None)
                v(*b[0])
                if A:
                    each(an, s0)
                v(*b[1])
                if A:
                    each(an, o0)
                turn_heads(qn, 0, "qn", "gl", "psum_qT", *b[0])
                if C:
                    if A:
                        pe.wait_ge(S["h1"], an[0][1])
                    qkv1(*cp[0])
                turn_heads(qn, 0, "qn", "gl", "psum_qT", *b[1])
                turn_heads(qn, 768, "kn", "qT", "psum_kT", *b[0])
                if C:
                    if A:
                        pe.wait_ge(S["h1"], an[1][1])
                    qkv1(*cp[1])
                turn_heads(qn, 768, "kn", "qT", "psum_kT", *b[1])
                sab(0, *b[0])
                if C:
                    turn_qk1(*cp[0])
                sab(0, *b[1])
                if C:
                    sab1(0, *cp[0])
                turn_p(0, *b[0], False)
                if C:
                    turn_qk1(*cp[1])
                sab(1, *b[0])
                turn_p(0, *b[1], False)
                if C:
                    sab1(0, *cp[1])
                sab(1, *b[1])
                turn_p(1, *b[0], False)
                if C:
                    sab1(1, *cp[0])
                pv(*b[0])
                turn_p(1, *b[1], False)
                if C:
                    sab1(1, *cp[1])
                    turn_p(0, *cp[0], True)
                pv(*b[1])
                if C:
                    turn_p(0, *cp[1], True)
                    for hf, t1 in cp:
                        turn_p(1, hf, t1, True)
                if A:
                    if C:
                        pe.wait_ge(S["p1Tb"], cp[0][1])
                    turn_x(1, *an[0])
                each(b, turn_o)
                if A:
                    if C:
                        pe.wait_ge(S["p1Tb"], cp[1][1])
                    turn_x(1, *an[1])
                if C:
                    pv1(*cp[0])
                proj(*b[0])
                if C:
                    pv1(*cp[1])
                    turn_om(*cp[0])
                proj(*b[1])
                if C:
                    turn_om(*cp[1])
                    each(cp, out1)

            def ahead(p):
                pe.wait_ge(s_wtok, 16 * len(loads_tok))
                for hf, t1 in two(p):
                    tok(p, hf, t1)
                pe.wait_ge(s_wret, 16 * len(loads_ret))
                each(two(p), turn_x, 0)
                for fn in (qkv0, s0, o0):
                    each(two(p), fn)
                each(two(p), turn_x, 1)

            def behind(p):
                each(two(p - 1), turn_x, 3)
                each(two(p - 1), router)
                ranks(p - 1)
                turn_x2(two(p), p - 1)
                for fn, *args in ((qkv1,), (turn_qk1,), (sab1, 0), (sab1, 1)):
                    each(two(p), fn, *args)
                for g in range(2):
                    for hf, t1 in two(p):
                        turn_p(g, hf, t1, True)
                for fn, *args in ((pv1,), (turn_om,), (out1,), (turn_x, 3), (router,)):
                    each(two(p), fn, *args)
                ranks(p)

            rounds(pe, ahead, constants, round_, behind)
            moe_tensor(pe)

        @block.scalar
        def _(act):
            def constants():
                act.wait_ge(s_w, 16 * len(loads))
                act.wait_ge(s_setup_v, 3)
                act.wait_ge(s_setup_p, 1)

            def copy(dst, src, ready, done, t1):
                act.wait_ge(S[ready], t1)
                act.activation(dst, src, ACT.Copy).then_inc(S[done], 1)

            def x_t(pair, k):
                for hf, t1 in pair:
                    copy(xnT[k][0:DH2, hf, :], turned_x(k, hf)[0:DH2, :], f"psum_xnT{k}", f"xnT{k}", t1)

            def square(hf, t1, c0, sq, ready, done):
                act.wait_ge(S[ready], t1)
                act.activation(v3(qn[:, hf, c0:c0 + 768], 2), banks(PS[hf], P, 384), ACT.Copy)
                act.activation(v3(sq[:, hf, :], 2), banks(PS[hf], P, 384), ACT.Square).then_inc(S[done], 1)

            def expo(pair, buf, g, ready, done):
                for hf, t1 in pair:
                    act.wait_ge(S[ready], t1)
                    x = buf[0:P, hf, g * HALF6:(g + 1) * HALF6]
                    act.activation(x, x, ACT.Exp).then_inc(S[done], 1)

            def p_t(pair, buf, s, g, ready, done):
                for hf, t1 in pair:
                    copy(v3(buf[:, hf, g * HALF6:(g + 1) * HALF6], 2), banks(PS[s + hf], P, 3 * P), ready, done, t1)

            def affine(pair, dst, c, ready, done):
                for hf, t1 in pair:
                    act.wait_ge(S[ready], t1)
                    act.activation(v3(dst[:, hf, :], 2), banks(PS[hf], 128, 3 * P), ACT.Identity,
                                   bias=qk_affine[:, c + 1:c + 2], scale=qk_affine[:, c:c + 1]).then_inc(S[done], 1)

            def qk_t0(pair):
                for hf, t1 in pair:
                    copy(qkT0[:, hf, :], PS[2 + hf][0:DH2, 0:4 * P], "psum_qkv0", "qkT0", t1)

            def qk_t1(pair):
                for hf, t1 in pair:
                    act.wait_ge(S["psum_qkT1"], t1)
                    act.activation(qT1[:, hf, :], PS[2 + hf][:, 0:3 * P], ACT.Copy)
                    act.activation(kT1[:, hf, :], PS[2 + hf][:, BANK:BANK + 3 * P], ACT.Copy).then_inc(S["q1T"], 1)

            def o_t(hf, t1):
                copy(v3(oT[:, hf, :], 2), banks(PS[hf], 128, 3 * P), "psum_oT", "oT", t1)

            def router_rows(p):
                act.wait_ge(S["sent"], p + 1)
                for hf, t1 in two(p):
                    act.wait_ge(S["xn3"], t1)
                    act.activation(xrow[:, :, hf, 0:D], xn[3][:, hf:hf + 1, :].broadcast_to([P, 2, D]), ACT.Copy)\
                        .then_inc(S["xrow"], 1)

            def router_exp(p):
                act.wait_ge(S["rlg"], 2 * p + 2)
                act.activation(lge[:, :, :], lgm[:, :, :], ACT.Exp).then_inc(S["lge"], 1)

            def om_t(pair):
                for hf, t1 in pair:
                    copy(omT[0:DH2, hf, :], PS[2 + hf][0:DH2, 0:2 * P], "psum_omT", "omT", t1)

            def round_(i, A, C, R):
                b, an, cp = two(i), two(i + 1), two(i - 1)
                for hf, t1 in b:
                    square(hf, t1, 0, sqq, "psum_q", "sqq")
                if R:
                    x_t(two(i - 2), 3)
                square(*b[0], 768, sqk, "psum_k", "sqk")
                if A:
                    x_t(an, 0)
                if R:
                    router_rows(i - 2)
                    router_exp(i - 2)
                if C:
                    x_t(cp, 2)
                square(*b[1], 768, sqk, "psum_k", "sqk")
                if A:
                    qk_t0(an)
                for hf, t1 in b:
                    copy(v_aug[:, hf, :].rearrange("p (b h d) -> p b h d", b=2, h=6)[:, :, :, 0:HD0],
                         banks(PS[hf], P, 384).rearrange("p b (h d) -> p b h d", h=6), "psum_v", "v", t1)
                affine(b, qT, 0, "psum_qT", "qT")
                act.wait_ge(S["gsub"], i + 1)
                act.activation(ge[:, :, :], gl[:, :, :], ACT.Exp).then_inc(S["gexp"], 1)
                affine(b, kT, 2, "psum_kT", "kT")
                (b0, b1), (c0, c1) = (b[:1], b[1:]), (cp[:1], cp[1:])
                if C:
                    qk_t1(c0)
                expo(b0, pr, 0, "suba", "ea")
                p_t(b0, pT, 0, 0, "psum_pTa", "pTa")
                expo(b1, pr, 0, "suba", "ea")
                if C:
                    qk_t1(c1)
                if C:
                    expo(c0, pr1, 0, "sub1a", "e1a")
                p_t(b1, pT, 0, 0, "psum_pTa", "pTa")
                expo(b0, pr, 1, "subb", "eb")
                p_t(b0, pT, 0, 1, "psum_pTb", "pTb")
                if C:
                    expo(c1, pr1, 0, "sub1a", "e1a")
                expo(b1, pr, 1, "subb", "eb")
                if C:
                    expo(c0, pr1, 1, "sub1b", "e1b")
                p_t(b1, pT, 0, 1, "psum_pTb", "pTb")
                if C:
                    p_t(c0, pT1, 2, 0, "psum_p1Ta", "p1Ta")
                    expo(c1, pr1, 1, "sub1b", "e1b")
                    p_t(c1, pT1, 2, 0, "psum_p1Ta", "p1Ta")
                    p_t(cp, pT1, 2, 1, "psum_p1Tb", "p1Tb")
                if A:
                    x_t(an[:1], 1)
                for hf, t1 in b:
                    o_t(hf, t1)
                if A:
                    x_t(an[1:], 1)
                if C:
                    om_t(cp)

            def ahead(p):
                x_t(two(p), 0)
                qk_t0(two(p))
                x_t(two(p), 1)

            def behind(p):
                x_t(two(p - 1), 3)
                router_rows(p - 1)
                router_exp(p - 1)
                x_t(two(p), 2)
                qk_t1(two(p))
                expo(two(p), pr1, 0, "sub1a", "e1a")
                expo(two(p), pr1, 1, "sub1b", "e1b")
                p_t(two(p), pT1, 2, 0, "psum_p1Ta", "p1Ta")
                p_t(two(p), pT1, 2, 1, "psum_p1Tb", "p1Tb")
                om_t(two(p))
                x_t(two(p), 3)
                router_rows(p)
                router_exp(p)

            rounds(act, ahead, constants, round_, behind)
            moe_scalar(act)

        @block.gpsimd
        def _(pool):
            pool.memset(blank[:, :], 0.0).then_inc(s_zeros, 1)
            pool.memset(ones[:, :], 1.0)
            pool.memset(neg_half[:, :], -0.5)
            pool.memset(v_aug[:, :, :], 1.0)
            pool.memset(v1_aug[:, :, :], 1.0)
            pool.memset(qk1[:, :, :], 0.0).then_inc(s_setup_p, 1)
            pool.wait_ge(s_setup_p, 1)

            def constants():
                pool.wait_ge(s_w, 16 * len(loads))
                pool.wait_ge(s_zeros, 1)
                pool.tensor_copy(blank[:, D:D + 1], pad_row[:, :]).then_inc(s_zeros, 1)

            def root(k, p):
                pool.wait_ge(S[f"stat{k}"], 3 * p + 3)
                pool.tensor_tensor(rstd[k][:, :, 0], mv[k][:, :, 1], neg_half[:, 0:2], ALU.pow).then_inc(S[f"rs{k}"], 1)

            def root_of_sum(v, n, ready, var, done, t1):
                wait_apart(pool, S[ready], t1)
                pool.tensor_scalar(v, v, 1.0 / n, EPS, ALU.mult, ALU.add).then_inc(S[var], 1)
                pool.wait_ge(S[var], t1)
                pool.tensor_tensor(v, v, neg_half[:, 0:12], ALU.pow).then_inc(S[done], 1)

            def root_q(p):
                for hf, t1 in two(p):
                    root_of_sum(ss[:, hf, 0:12], HD0, "ssq", "qvar", "rsq", t1)

            def residual(p):
                for hf, t1 in two(p):
                    pool.wait_ge(S["h1"], t1)
                    pool.tensor_tensor(hb[:, hf:hf + 1, :], h_all[:, bass.ds(2 * p + hf, 1), :],
                                       b_proj[:, :].unsqueeze(1), ALU.add).then_inc(S["hb"], 1)

            kv = [qk1[:, hf, :].rearrange("p (n d) -> p n d", d=PAD1)[:, H1:2 * H1, 0:HD1] for hf in range(2)]
            c3 = [v3(lc[:, hf, :], H1) for hf in range(2)]

            def rotate(p):
                for hf, t1 in two(p):
                    pool.wait_ge(S["rope"], t1)
                    pool.tensor_tensor(qk1[:, hf, :].rearrange("p (n d) -> p n d", d=PAD1)[:, :, 0:HD1],
                                       ropa[:, hf, :].rearrange("p (n d) -> p n d", d=HD1),
                                       ropb[:, hf, :].rearrange("p (n d) -> p n d", d=HD1),
                                       ALU.add).then_inc(S["qk1"], 1)

            def centre(p):
                for hf, t1 in two(p):
                    pool.wait_ge(S["lmean"], p + 1)
                    pool.tensor_tensor(c3[hf], kv[hf], lsum[:, hf, :].unsqueeze(2).broadcast_to([P, H1, HD1]),
                                       ALU.add).then_inc(S["lc"], 1)
                for hf, t1 in two(p):
                    pool.wait_ge(S["lc"], t1)
                    pool.tensor_tensor(lsq[:, hf, :], lc[:, hf, :], lc[:, hf, :], ALU.mult).then_inc(S["lsq"], 1)

            def scale(p):
                for hf, t1 in two(p):
                    root_of_sum(lr[:, hf, :], HD1, "lss", "lvar", "lrsq", t1)
                for hf, t1 in two(p):
                    pool.wait_ge(S["lrsq"], t1)
                    pool.tensor_tensor(c3[hf], c3[hf], lr[:, hf, :].unsqueeze(2).broadcast_to([P, H1, HD1]),
                                       ALU.mult).then_inc(S["lv"], 1)
                for hf, t1 in two(p):
                    pool.wait_ge(S["lv"], 4 * p + 1 + hf)
                    pool.tensor_tensor(c3[hf], c3[hf], ln_gb[:, 0:1, :].broadcast_to([P, H1, HD1]),
                                       ALU.mult).then_inc(S["lv"], 1)
                for hf, t1 in two(p):
                    pool.wait_ge(S["lv"], 4 * p + 3 + hf)
                    pool.tensor_tensor(v1_aug[:, hf, :].rearrange("p (n d) -> p n d", d=HD1 + 1)[:, :, 0:HD1],
                                       c3[hf], ln_gb[:, 1:2, :].broadcast_to([P, H1, HD1]),
                                       ALU.add).then_inc(S["v1"], 1)

            def keep(p):
                for hf, t1 in two(p):
                    pool.wait_ge(S["xn3"], t1)
                    pool.tensor_tensor(h_all[:, bass.ds(2 * p + hf, 1), :], h_all[:, bass.ds(2 * p + hf, 1), :],
                                       xn[3][:, hf:hf + 1, :], ALU.add)
                    pool.tensor_copy(xrow[:, :, hf, D:D + 1],
                                     small[:, bass.ds(C_TOKEN + 2 * p + hf, 1)].unsqueeze(1).broadcast_to([P, 2, 1])).then_inc(S["base"], 1)

            def scatter(p):
                wait_apart(pool, S["slots"], p + 1)
                wait_apart(pool, S["rgate"], p + 1)
                wait_apart(pool, S["xrow"], 2 * p + 2)
                wait_apart(pool, S["base"], 2 * p + 2)
                for k in range(2):
                    for hf in range(2):
                        pool.indirect_dma_start(out=rows_dram, out_offset=bass.IndirectOffsetOnAxis(ap=slot_u[:, k, hf:hf + 1], axis=0),
                                                in_=xrow[:, k, hf, :], in_offset=None).then_inc(s_scat, 16)
                pool.wait_ge(s_scat, 64 * p + 64)
                pool.sem_inc(S["sent"], 1)

            def round_(i, A, C, R):
                root_q(i)
                if A:
                    root(0, i + 1)
                if R:
                    keep(i - 2)
                residual(i)
                if A:
                    root(1, i + 1)
                if C:
                    rotate(i - 1)
                    centre(i - 1)
                    scale(i - 1)
                if R:
                    scatter(i - 2)
                root(2, i)
                if C:
                    root(3, i - 1)

            def ahead(p):
                root(0, p)
                root(1, p)

            def behind(p):
                keep(p - 1)
                rotate(p)
                centre(p)
                scale(p)
                scatter(p - 1)
                root(3, p)
                keep(p)
                scatter(p)

            rounds(pool, ahead, constants, round_, behind)
            moe_gpsimd(pool)

        @block.vector
        def _(dve):
            dve.memset(xnT[1][DH2:128, :, :], 0.0)
            dve.memset(w_moh[DH2:128, :, :], 0.0).then_inc(s_center, 1)
            dve.wait_ge(s_center, 1)
            for rows in (*xnT[:3], omT, xeT):
                dve.memset(rows[DH2:DH2 + 1, :, :], 1.0)
            dve.sem_inc(S["sent"], 1)
            dve.sem_inc(S["h2"], 2)

            def centre_weights():
                dve.wait_ge(s_wmoh, 16 * len(loads_moh))
                wq = [w_moh[0:DH2 + 1 - c, c, 0:1536].rearrange("p (n d) -> p n d", d=HD0) for c in range(2)]
                for c in range(2):
                    dve.tensor_reduce(wmean[0:DH2 + 1 - c, c, :], wq[c], AX.X, ALU.add).then_inc(s_center, 1)
                dve.wait_ge(s_center, 3)
                for c in range(2):
                    m = wmean[0:DH2 + 1 - c, c, :]
                    dve.tensor_scalar(m, m, -1.0 / HD0, None, ALU.mult).then_inc(s_center, 1)
                dve.wait_ge(s_center, 5)
                for c in range(2):
                    n = DH2 + 1 - c
                    dve.tensor_tensor(wq[c], wq[c], wmean[0:n, c, :].unsqueeze(2).broadcast_to([n, 24, HD0]), ALU.add)\
                        .then_inc(s_setup_v, 1)

            def constants():
                dve.wait_ge(s_w, 16 * len(loads))
                dve.tensor_copy(base[:, 0, :], small[:, C_REGION:C_REGION + E])
                dve.tensor_copy(mask0[:, :], mask0f[:, :])
                dve.tensor_copy(mask1[:, :], mask1f[:, :])
                dve.tensor_scalar(qk_affine[:, 0:2], qk_affine[:, 0:2], HD0 ** -0.5, None, ALU.mult).then_inc(s_setup_v, 1)

            def h_of(p, hf):
                return h_all[:, bass.ds(2 * p + hf, 1), :]

            def stats_of(p, k, credit=0):
                for hf, t1 in two(p):
                    wait_apart(dve, S[f"h{k}"], t1 + credit)
                    m = dve.bn_stats(stats[:, hf, :], h_of(p, hf))
                m.then_inc(S[f"stat{k}"], 1)
                wait_apart(dve, S[f"stat{k}"], 3 * p + 1)
                for hf in range(2):
                    m = dve.bn_aggr(mv[k][:, hf, :], stats[:, hf, :])
                m.then_inc(S[f"stat{k}"], 1)
                dve.wait_ge(S[f"stat{k}"], 3 * p + 2)
                dve.tensor_scalar(mv[k][:, :, 1:2], mv[k][:, :, 1:2], EPS, None, ALU.add).then_inc(S[f"stat{k}"], 1)

            def norm(p, k):
                for hf in range(2):
                    dve.wait_ge(S[f"rs{k}"], p + 1)
                    dve.tensor_scalar(xn[k][:, hf:hf + 1, :], h_of(p, hf), mv[k][:, hf, 0:1], rstd[k][:, hf, 0:1],
                                      ALU.subtract, ALU.mult).then_inc(S[f"xn{k}"], 1)

            def rsqrt(dst, src, shape, chain, p, mean):
                n = shape[0] * shape[1]
                nv, y, t = (rs[:, c, 0:n].rearrange("p (a b) -> p a b", a=shape[0]) for c in range(3))
                bits = rs_bits[:, 0:n].rearrange("p (a b) -> p a b", a=shape[0])
                step = [0]

                def then(ins):
                    step[0] += 1
                    ins.then_inc(S[chain], 1)
                    if step[0] < RSQ:
                        dve.wait_ge(S[chain], RSQ * p + step[0])

                then(dve.tensor_scalar(src, src, mean, EPS, ALU.mult, ALU.add))
                dve.tensor_scalar(nv, src, -0.5, None, ALU.mult)
                then(dve.tensor_scalar(bits, src.bitcast(I32), 1, None, ALU.logical_shift_right))
                then(dve.tensor_scalar(y.bitcast(I32), bits, -1.0, float(0x5F3759DF), ALU.mult, ALU.add))
                for last in (False, False, True):
                    then(dve.tensor_tensor(t, y, y, ALU.mult))
                    then(dve.tensor_tensor(t, t, nv, ALU.mult))
                    then(dve.scalar_tensor_tensor(dst if last else y, t, 1.5, y, ALU.add, ALU.mult))
                assert step[0] == RSQ

            def softmax_in(hf, t1, ps, buf, nm_buf, g, ready, nm, done):
                dve.wait_ge(S[ready], t1)
                dve.tensor_reduce(v3(nm_buf[:, hf, 6 * g:6 * g + 6], 2),
                                  banks(ps, P, 3 * P).rearrange("p b (h k) -> p b h k", h=3),
                                  AX.X, ALU.max, negate=True).then_inc(S[nm], 1)
                dve.wait_ge(S[nm], t1)
                for b in range(2):
                    c0 = g * HALF6 + b * 3 * P
                    mm = dve.tensor_tensor(v3(buf[0:P, hf, c0:c0 + 3 * P], 3), v3(ps[0:P, b * BANK:b * BANK + 3 * P], 3),
                                           nm_buf[:, hf, 6 * g + 3 * b:6 * g + 3 * b + 3].unsqueeze(2).broadcast_to([P, 3, P]),
                                           ALU.add)
                mm.then_inc(S[done], 1)

            def softmaxes(pair, s, buf, nm_buf, g, *names):
                for hf, t1 in pair:
                    softmax_in(hf, t1, PS[s + hf], buf, nm_buf, g, *names)

            def embed(p, between=None):
                for hf, t1 in two(p):
                    if hf and between is not None:
                        choose(between)
                    dve.wait_ge(S["psum_tok"], t1)
                    dve.tensor_tensor(h_of(p, hf), PS[2 + hf][0:P, 0:D].unsqueeze(1), b_tok[:, :].unsqueeze(1), ALU.add)\
                        .then_inc(S["h0"], 1)
                stats_of(p, 0)

            def values(p):
                for hf, t1 in two(p):
                    dve.wait_ge(S["psum_qkv0"], t1)
                    dve.tensor_copy(v0[:, hf, :], PS[2 + hf][0:P, BANK:BANK + D]).then_inc(S["v0"], 1)

            def decay(p):
                for hf, t1 in two(p):
                    dve.wait_ge(S["psum_s0"], t1)
                    dve.tensor_tensor(pT0[:, hf, :], PS[2 + hf][0:P, 0:P], retT[:, :], ALU.mult).then_inc(S["pT0"], 1)

            def retained(p):
                for hf, t1 in two(p):
                    dve.wait_ge(S["psum_o0"], t1)
                    dve.tensor_tensor(h_of(p, hf), PS[2 + hf][0:P, 0:D].unsqueeze(1), h_of(p, hf), ALU.add).then_inc(S["h1"], 1)

            def sums(hf, t1, c0, sq, ready):
                dve.wait_ge(S[ready], t1)
                dve.tensor_reduce(ss[:, hf, c0:c0 + 12], v3(sq[:, hf, :], 12),
                                  AX.X, ALU.add).then_inc(S["ssk" if c0 else "ssq"], 1)

            def normed(i, c0, done):
                for hf, t1 in two(i):
                    if c0:
                        dve.wait_ge(S["rsk"], RSQ * i + RSQ)
                    else:
                        dve.wait_ge(S["rsq"], t1)
                    x = v3(qn[:, hf, c0 * 64:c0 * 64 + 768], 12)
                    dve.tensor_tensor(x, x, ss[:, hf, c0:c0 + 12].unsqueeze(2).broadcast_to([P, 12, HD0]), ALU.mult)\
                        .then_inc(S[done], 1)

            def gate_logits(hf, t1):
                dve.wait_ge(S["v"], t1)
                dve.tensor_copy(gl[:, hf, :], PS[hf][0:P, BANK + 384:BANK + 384 + RH + 4]).then_inc(S["gl"], 1)

            def pick(i):
                wait_apart(dve, S["gl"], 2 * i + 2)
                for hf in range(2):
                    dve.max(gmx[:, hf, :], gl[:, hf, 0:RH])
                ways = gl[:, :, RH:RH + 4].rearrange("p a (b c) -> p a b c", b=2)
                dve.tensor_reduce(v3(gm2[:, :], 2), ways, AX.X, ALU.max).then_inc(S["gpick"], 1)
                wait_apart(dve, S["gpick"], 2 * i + 1)
                for hf in range(2):
                    m = dve.max_index(gidx[:, hf, :], gmx[:, hf, :], gl[:, hf, 0:RH])
                m.then_inc(S["gpick"], 1)
                dve.wait_ge(S["gpick"], 2 * i + 2)
                dve.tensor_copy(gidf[:, :, :], gidx[:, :, 0:2])
                dve.tensor_tensor(gl[:, :, 0:RH], gl[:, :, 0:RH], gmx[:, :, 0:1].broadcast_to([P, 2, RH]), ALU.subtract)
                dve.tensor_tensor(ways, ways, v3(gm2[:, :], 2).unsqueeze(3).broadcast_to([P, 2, 2, 2]),
                                  ALU.subtract).then_inc(S["gsub"], 1)

            def gate(i):
                GS = 8

                def gate_step(ins, n):
                    ins.then_inc(S["gstep"], 1)
                    dve.wait_ge(S["gstep"], GS * i + n)

                dve.wait_ge(S["gexp"], i + 1)
                g2 = ge[:, :, RH:RH + 4].rearrange("p a (b c) -> p a b c", b=2)
                dve.tensor_reduce(gsum[:, :, 0:1], ge[:, :, 0:RH], AX.X, ALU.add)
                dve.tensor_reduce(gsum[:, :, 1:3], g2, AX.X, ALU.add)
                for hf in range(2):
                    m = dve.tensor_scalar(gmask[:, hf, :], small[:, 0:RH], gidf[:, hf, 1:2], None, ALU.is_equal)
                gate_step(m, 1)
                dve.reciprocal(gsum[:, :, 0:3], gsum[:, :, 0:3])
                for hf in range(2):
                    m = dve.scalar_tensor_tensor(gmask[:, hf, :], small[:, 0:RH], gidf[:, hf, 0:1], gmask[:, hf, :],
                                                 ALU.is_equal, ALU.add)
                gate_step(m, 2)
                for hf in range(2):
                    dve.scalar_tensor_tensor(gmask[:, hf, :], ge[:, hf, 0:RH], gsum[:, hf, 0:1], gmask[:, hf, :],
                                             ALU.mult, ALU.mult)
                gate_step(dve.tensor_tensor(g2, g2, gsum[:, :, 1:3].unsqueeze(3).broadcast_to([P, 2, 2, 2]), ALU.mult), 3)
                dve.tensor_reduce(gden[:, :, 0:1], gmask[:, :, :], AX.X, ALU.add)
                gate_step(dve.tensor_tensor(gates[:, :, 0:SH], ge[:, :, RH + 2:RH + 4],
                                            ge[:, :, RH:RH + 1].broadcast_to([P, 2, SH]), ALU.mult), 4)
                gate_step(dve.tensor_scalar(gden[:, :, 0:1], gden[:, :, 0:1], float(np.finfo(np.float32).eps), None,
                                            ALU.max), 5)
                gate_step(dve.reciprocal(gden[:, :, 0:1], gden[:, :, 0:1]), 6)
                gate_step(dve.tensor_tensor(gden[:, :, 1:2], gden[:, :, 0:1], ge[:, :, RH + 1:RH + 2], ALU.mult), 7)
                gate_step(dve.tensor_tensor(gates[:, :, SH:H0], gmask[:, :, :], gden[:, :, 1:2].broadcast_to([P, 2, RH]),
                                            ALU.mult), 8)
                dve.tensor_scalar(gates[:, :, :], gates[:, :, :], 4.0, None, ALU.mult).then_inc(S["gates"], 1)

            def heads(i, hf, t1):
                dve.wait_ge(S["psum_pv"], t1)
                dve.reciprocal(v3(fac[:, hf, :], 2),
                               banks(PS[hf], P, 390).rearrange("p b (h d) -> p b h d", h=6)[:, :, :, HD0])\
                    .then_inc(S["fac"], 1)
                dve.wait_ge(S["gates"], i + 1)
                dve.wait_ge(S["fac"], 2 * t1 - 1)
                dve.tensor_tensor(fac[:, hf, :], fac[:, hf, :], gates[:, hf, :], ALU.mult).then_inc(S["fac"], 1)
                dve.wait_ge(S["fac"], 2 * t1)
                for b in range(2):
                    mm = dve.tensor_tensor(v3(o[:, hf, 384 * b:384 * b + 384], 6),
                                           v3(PS[hf][0:P, BANK * b:BANK * b + 390], 6)[:, :, 0:HD0],
                                           fac[:, hf, 6 * b:6 * b + 6].unsqueeze(2).broadcast_to([P, 6, HD0]), ALU.mult)
                mm.then_inc(S["o"], 1)

            def projected(i):
                for hf, t1 in two(i):
                    dve.wait_ge(S["psum_proj"], t1)
                    dve.wait_ge(S["hb"], t1)
                    dve.tensor_tensor(h_of(i, hf), PS[hf][0:P, 0:D].unsqueeze(1), hb[:, hf:hf + 1, :], ALU.add)\
                        .then_inc(S["h2"], 1)
                stats_of(i, 2, 2)

            kv = [qk1[:, hf, :].rearrange("p (n d) -> p n d", d=PAD1)[:, H1:2 * H1, 0:HD1] for hf in range(2)]

            def halves(x, k):
                return x.rearrange("p (n b d) -> p n b d", b=2, d=HD1 // 2)[:, :, k, :]

            def rotary(p):
                for hf, t1 in two(p):
                    dve.wait_ge(S["psum_qkv1"], t1)
                    ps = PS[2 + hf][0:P, 0:2 * D]
                    dve.tensor_tensor(ropa[:, hf, :], ps, rope[:, 0:2 * D], ALU.mult)
                    for b in range(2):
                        mm = dve.tensor_tensor(halves(ropb[:, hf, :], b), halves(ps, 1 - b),
                                               halves(rope[:, 2 * D:4 * D], b), ALU.mult)
                    mm.then_inc(S["rope"], 1)

            def kv_mean(p):
                for hf, t1 in two(p):
                    dve.wait_ge(S["qk1"], t1)
                    m = dve.tensor_reduce(lsum[:, hf, :], kv[hf], AX.X, ALU.add)
                m.then_inc(S["lsum"], 1)
                dve.wait_ge(S["lsum"], p + 1)
                dve.tensor_scalar(lsum[:, :, :], lsum[:, :, :], -1.0 / HD1, None, ALU.mult).then_inc(S["lmean"], 1)

            def kv_squares(p):
                for hf, t1 in two(p):
                    dve.wait_ge(S["lsq"], t1)
                    dve.tensor_reduce(lr[:, hf, :], v3(lsq[:, hf, :], H1), AX.X, ALU.add).then_inc(S["lss"], 1)

            def attended(p):
                for hf, t1 in two(p):
                    dve.wait_ge(S["psum_pv1"], t1)
                    dve.reciprocal(fac1[:, hf, :], v3(PS[2 + hf][0:P, 0:H1 * (HD1 + 1)], H1)[:, :, HD1])\
                        .then_inc(S["rden"], 1)
                    dve.wait_ge(S["rden"], t1)
                    dve.tensor_tensor(v3(om[:, hf, :], H1), v3(PS[2 + hf][0:P, 0:H1 * (HD1 + 1)], H1)[:, :, 0:HD1],
                                      fac1[:, hf, :].unsqueeze(2).broadcast_to([P, H1, HD1]), ALU.mult).then_inc(S["om"], 1)

            def latents(p):
                for k, done in ((0, "h3a"), (1, "h3")):
                    for hf, t1 in two(p):
                        dve.wait_ge(S["h3a" if k else "psum_out"], t1)
                        dve.scalar_tensor_tensor(h_of(p, hf), PS[2 + hf][0:P, D * k:D * k + D].unsqueeze(1),
                                                 small[:, C_CTX + k:C_CTX + k + 1], h_of(p, hf), ALU.mult, ALU.add).then_inc(S[done], 1)
                stats_of(p, 3)

            def choose(p):
                for hf, t1 in two(p):
                    wait_apart(dve, S["psum_rt"], t1)
                    dve.max(rmx[:, hf, :], logits(hf)).then_inc(S["rtop"], 1)
                for hf, t1 in two(p):
                    wait_apart(dve, S["rtop"], t1)
                    dve.max_index(ridx[:, hf, :], rmx[:, hf, :], logits(hf)).then_inc(S["ridx"], 1)
                for hf, t1 in two(p):
                    dve.wait_ge(S["ridx"], t1)
                    dve.tensor_tensor(lgm[:, hf, 0:E], logits(hf), rmx[:, hf, 0:1].broadcast_to([P, E]), ALU.subtract)
                    dve.tensor_tensor(lgm[:, hf, E:E + 1], rmx[:, hf, 1:2], rmx[:, hf, 0:1], ALU.subtract).then_inc(S["rlg"], 1)
                route_step(p, 1, dve.tensor_copy(idf[:, :, :], ridx[:, :, 0:2]))
                for k in range(2):
                    m = dve.tensor_tensor(v3(oh[:, k, :], 2), small[:, 0:E].unsqueeze(1).broadcast_to([P, 2, E]),
                                          idf[:, :, k:k + 1].broadcast_to([P, 2, E]), ALU.is_equal)
                route_step(p, 2, m)
                dve.tensor_tensor(both[:, :], oh[:, 0, :], oh[:, 1, :], ALU.add).then_inc(S["both"], 1)

            def route_step(p, n, ins):
                ins.then_inc(S["rstep"], 1)
                dve.wait_ge(S["rstep"], RS * p + n)

            def rows_of(p):
                rank, count = (PS[2][0:P, BANK + 2 * E * n:BANK + 2 * E * (n + 1)] for n in range(2))
                dve.wait_ge(S["psum_rank"], p + 1)
                for t in range(2):
                    route_step(p, 3 + t, dve.tensor_tensor(base[:, t + 1, :], base[:, t, :], count[:, E * t:E * t + E], ALU.add))
                dve.tensor_tensor(row_of[:, :, :], base[:, 0:2, :], v3(rank, 2), ALU.add).then_inc(S["rank"], 1)

            def slots(p):
                dve.wait_ge(S["rank"], p + 1)
                for k in range(2):
                    dve.tensor_tensor(prod[:, k, :], oh[:, k, :], row_of[:, :, :].rearrange("p a b -> p (a b)"), ALU.mult)
                dve.wait_ge(S["lge"], p + 1)
                dve.tensor_reduce(rsum[:, :], lge[:, :, 0:E], AX.X, ALU.add)
                route_step(p, 5, dve.tensor_copy(base[:, 0, :], base[:, 2, :]))
                for k in range(2):
                    dve.tensor_reduce(slot_f[:, k, :], v3(prod[:, k, :], 2), AX.X, ALU.add)
                route_step(p, 6, dve.reciprocal(rsum[:, :], rsum[:, :]))
                dve.wait_ge(S["sent"], p + 1)
                dve.tensor_copy(slot_u[:, :, :], slot_f[:, :, :]).then_inc(S["slots"], 1)
                dve.tensor_copy(xrow[:, 0, :, D + 1], rsum[:, :])
                dve.tensor_tensor(xrow[:, 1, :, D + 1], lge[:, :, E], rsum[:, :], ALU.mult).then_inc(S["rgate"], 1)

            def round_(i, A, C, R):
                b, cp = two(i), two(i - 1)
                for hf, t1 in b:
                    sums(hf, t1, 0, sqq, "sqq")
                if A:
                    embed(i + 1, i - 2 if R else None)
                elif R:
                    choose(i - 2)
                if A:
                    norm(i + 1, 0)
                sums(*b[0], 12, sqk, "sqk")
                if R:
                    rows_of(i - 2)
                normed(i, 0, "qn")
                sums(*b[1], 12, sqk, "sqk")
                dve.wait_ge(S["ssk"], 2 * i + 2)
                rsqrt(ss[:, :, 12:24], ss[:, :, 12:24], (2, 12), "rsk", i, 1.0 / HD0)
                if A:
                    values(i + 1)
                normed(i, 12, "kn")
                if A:
                    decay(i + 1)
                gate_logits(*b[0])
                if A:
                    retained(i + 1)
                gate_logits(*b[1])
                if A:
                    stats_of(i + 1, 1)
                pick(i)
                if A:
                    norm(i + 1, 1)
                if C:
                    rotary(i - 1)
                (b0, b1), (c0, c1) = (b[:1], b[1:]), (cp[:1], cp[1:])
                softmaxes(b0, 0, pr, nmax, 0, "psum_sa", "nma", "suba")
                softmaxes(b1, 0, pr, nmax, 0, "psum_sa", "nma", "suba")
                if C:
                    kv_mean(i - 1)
                    softmaxes(c0, 2, pr1, nmax1, 0, "psum_s1a", "nm1a", "sub1a")
                softmaxes(b0, 0, pr, nmax, 1, "psum_sb", "nmb", "subb")
                if C:
                    kv_squares(i - 1)
                    softmaxes(c1, 2, pr1, nmax1, 0, "psum_s1a", "nm1a", "sub1a")
                softmaxes(b1, 0, pr, nmax, 1, "psum_sb", "nmb", "subb")
                if C:
                    softmaxes(c0, 2, pr1, nmax1, 1, "psum_s1b", "nm1b", "sub1b")
                gate(i)
                if C:
                    softmaxes(c1, 2, pr1, nmax1, 1, "psum_s1b", "nm1b", "sub1b")
                for hf, t1 in b:
                    heads(i, hf, t1)
                if R:
                    slots(i - 2)
                if C:
                    attended(i - 1)
                projected(i)
                if C:
                    latents(i - 1)
                norm(i, 2)
                if C:
                    norm(i - 1, 3)

            def ahead(p):
                dve.wait_ge(s_wtok, 16 * len(loads_tok))
                embed(p)
                norm(p, 0)
                centre_weights()
                values(p)
                dve.wait_ge(s_wret, 16 * len(loads_ret))
                decay(p)
                retained(p)
                stats_of(p, 1)
                norm(p, 1)

            def behind(p):
                choose(p - 1)
                rows_of(p - 1)
                rotary(p)
                kv_mean(p)
                kv_squares(p)
                slots(p - 1)
                softmaxes(two(p), 2, pr1, nmax1, 0, "psum_s1a", "nm1a", "sub1a")
                softmaxes(two(p), 2, pr1, nmax1, 1, "psum_s1b", "nm1b", "sub1b")
                attended(p)
                latents(p)
                norm(p, 3)
                choose(p)
                rows_of(p)
                slots(p)

            rounds(dve, ahead, constants, round_, behind)
            moe_vector(dve)


def kernel(**inputs):
    import concourse.bacc as bacc
    from concourse.bass_utils import run_bass_kernel_spmd

    g = {k: np.asarray(v) for k, v in inputs.items()}

    def wide(w):
        return w.reshape(2, DH2, -1).transpose(1, 0, 2)

    x = g["x"].reshape(BATCH, GRID, PATCH, GRID, PATCH * 3).transpose(0, 1, 3, 2, 4).reshape(TILES, P, PC, 128)
    arrays = {
        "x": x.transpose(0, 3, 2, 1).reshape(TILES, 128, PC * P),
        "w_tok": g["L0_tok_W"].reshape(PC, 128, D).transpose(1, 0, 2), "b_tok": g["L0_tok_b"],
        "w_ret": wide(g["L0_attn_W_qkv"]), "b_ret": g["L0_attn_b_qkv"].reshape(1, -1),
        "w_moh": wide(g["L0_ffn_qkv_w"]), "b_moh": g["L0_ffn_qkv_b"].reshape(1, -1),
        "w_gr": wide(g["L0_ffn_wg_w"]), "w_g0": wide(g["L0_ffn_wg0_w"]), "w_g1": wide(g["L0_ffn_wg1_w"]),
        "w_proj": g["L0_ffn_proj_w"].reshape(H0 // 2, 128, D).transpose(1, 0, 2), "b_proj": g["L0_ffn_proj_b"],
        "qw": g["L0_ffn_q_norm_w"].reshape(-1, 1), "qb": g["L0_ffn_q_norm_b"].reshape(-1, 1),
        "kw": g["L0_ffn_k_norm_w"].reshape(-1, 1), "kb": g["L0_ffn_k_norm_b"].reshape(-1, 1),
        "w_q1": wide(g["L1_attn_Wq"]), "w_kv1": wide(g["L1_attn_Wkv"]),
        "w_octx": wide(g["L1_attn_Wo_ctx"]), "w_olat": wide(g["L1_attn_Wo_lat"]),
        "b_octx": g["L1_attn_bo_ctx"].reshape(1, -1), "b_olat": g["L1_attn_bo_lat"].reshape(1, -1),
        "ln_g": g["L1_attn_ln_g"], "ln_b": g["L1_attn_ln_b"], "w_rt": wide(g["L1_ffn_Wr"].T),
        "w1": g["L1_ffn_W1"].reshape(E, 2, DH2, FF).transpose(0, 2, 1, 3).reshape(E, DH2, 2 * FF),
        "b1": g["L1_ffn_b1"].reshape(E, 1, FF),
        "w2": g["L1_ffn_W2"].reshape(E, FC, 128, D).transpose(0, 2, 1, 3).reshape(E, 128, FC * D),
        "b2": g["L1_ffn_b2"].reshape(E, 1, D),
    }
    arrays.update(constants())
    arrays = {f"in_{k}": np.ascontiguousarray(v) for k, v in arrays.items()}
    nc = bacc.Bacc("TRN2", target_bir_lowering=False, num_devices=1)
    aps = {k[3:]: nc.dram_tensor(k, v.shape, mybir.dt.from_np(v.dtype), kind="ExternalInput").ap()
           for k, v in arrays.items()}
    out = nc.dram_tensor("out", (TOKENS + ET, D), mybir.dt.float32, kind="ExternalOutput").ap()
    vit_tower(nc, aps, out)
    return run_bass_kernel_spmd(nc, [arrays], core_ids=[0]).results[0]["out"][:TOKENS].reshape(BATCH, N_TOK, D)
```
